# Optimizing a Trainium2 kernel written in Bass

```python
import numpy as np
import jax
import jax.numpy as jnp

def _softmax(x, axis=-1):
    return jax.nn.softmax(x, axis=axis)

def _gelu(x):
    return jax.nn.gelu(x, approximate=True)

def _silu(x):
    return jax.nn.silu(x)

def _sigmoid(x):
    return jax.nn.sigmoid(x)

def _layernorm(x, axis=-1, eps=1e-05):
    m = jnp.mean(x, axis=axis, keepdims=True)
    v = jnp.var(x, axis=axis, keepdims=True)
    return (x - m) / jnp.sqrt(v + eps)

def _scatter_add(tgt, idx, src, axis=0):
    return tgt.at[idx].add(src)

def _segment_sum(src, seg, n):
    return jax.ops.segment_sum(src, seg, n)
kernel_name = 'mk_adj_preln_d4_adj_r2_50bd44'

def setup_inputs(seed: int=0):
    np.random.seed(seed)
    _w = jnp.asarray

    def _rec_inputs():
        import jax
        import jax.numpy as jnp
        _gk = jax.random.key(seed)
        x = -0.000929 + 1 * jax.random.normal(jax.random.fold_in(_gk, 1), (2048, 256), jnp.float32)
        _w = (1.0 + jnp.arange(2048, dtype=jnp.float32)) ** (-0.5)
        _w = _w / _w.mean()
        _pij = jnp.clip(0.00390625 * _w[:, None] * _w[None, :], 0.0, 1.0)
        _a = jax.random.uniform(jax.random.fold_in(_gk, 2), (2048, 2048)) < _pij
        adj = _a.astype(jnp.int32)
        return (x, adj)
    x, adj = _rec_inputs()

    def _L0_gnn_setup():
        import jax, jax.numpy as jnp
        import numpy as np
        B, IN_F, OUT_F, H = (1024, 256, 256, 8)
        D = OUT_F // H
        key = jax.random.key(seed)
        ks = jax.random.split(key, 4)
        x = jax.random.normal(ks[0], (B, IN_F), dtype=jnp.float32)
        W_w = jax.random.normal(ks[1], (OUT_F, IN_F), dtype=jnp.float32) * (1.0 / np.sqrt(IN_F))
        W_b = jnp.zeros((OUT_F,), dtype=jnp.float32)
        a = jax.random.normal(ks[2], (2 * D, 1), dtype=jnp.float32) * 0.1
        adj = jax.random.randint(ks[3], (B, B), 0, 2, dtype=jnp.int32)
        return {'x': x, 'adj': adj, 'W_w': W_w, 'W_b': W_b, 'a': a}
    _L0_gnn_all = _L0_gnn_setup()
    _L0_gnn_in = {k: v for k, v in _L0_gnn_all.items() if k in ('W_w', 'W_b', 'a')}
    del _L0_gnn_all

    def _L1_gnn_setup():
        import jax, jax.numpy as jnp
        import numpy as np
        N, D_IN, D_OUT = (4096, 256, 256)
        key = jax.random.key(seed)
        ks = jax.random.split(key, 8)
        scale_in = 1.0 / np.sqrt(D_IN)
        scale_cat = 1.0 / np.sqrt(2 * D_OUT)
        return {'x': jax.random.normal(ks[0], (N, D_IN), dtype=jnp.float32), 'adj': jax.random.randint(ks[1], (N, N), 0, 2, dtype=jnp.int32), 'W_self': jax.random.uniform(ks[2], (D_IN, D_OUT), jnp.float32, -scale_in, scale_in), 'b_self': jax.random.uniform(ks[3], (D_OUT,), jnp.float32, -scale_in, scale_in), 'W_nb': jax.random.uniform(ks[4], (D_IN, D_OUT), jnp.float32, -scale_in, scale_in), 'b_nb': jax.random.uniform(ks[5], (D_OUT,), jnp.float32, -scale_in, scale_in), 'W_comb': jax.random.uniform(ks[6], (2 * D_OUT, D_OUT), jnp.float32, -scale_cat, scale_cat), 'b_comb': jax.random.uniform(ks[7], (D_OUT,), jnp.float32, -scale_cat, scale_cat)}
    _L1_gnn_all = _L1_gnn_setup()
    _L1_gnn_in = {k: v for k, v in _L1_gnn_all.items() if k in ('W_self', 'b_self', 'W_nb', 'b_nb', 'W_comb', 'b_comb')}
    del _L1_gnn_all

    def _L2_gnn_setup():
        import jax, jax.numpy as jnp
        import numpy as np
        N = 2048
        STATE_DIM = 256
        OUTPUT_DIM = 256
        N_STEPS = 5
        W_STD = 0.02

        def _lin_params(key, out_dim, in_dim):
            W = jax.random.normal(key, (out_dim, in_dim), dtype=jnp.float32) * W_STD
            b = jnp.zeros((out_dim,), dtype=jnp.float32)
            return (W, b)
        key = jax.random.key(seed)
        ks = jax.random.split(key, 10)
        prop_state = jax.random.normal(ks[0], (N, STATE_DIM), dtype=jnp.float32)
        A = jax.random.randint(ks[1], (N, N), 0, 2, dtype=jnp.int64)
        in_W, in_b = _lin_params(ks[2], STATE_DIM, STATE_DIM)
        out_W, out_b = _lin_params(ks[3], STATE_DIM, STATE_DIM)
        r_W, r_b = _lin_params(ks[4], STATE_DIM, 3 * STATE_DIM)
        z_W, z_b = _lin_params(ks[5], STATE_DIM, 3 * STATE_DIM)
        h_W, h_b = _lin_params(ks[6], STATE_DIM, 3 * STATE_DIM)
        o1_W, o1_b = _lin_params(ks[7], STATE_DIM, STATE_DIM)
        o2_W, o2_b = _lin_params(ks[8], OUTPUT_DIM, STATE_DIM)
        return {'prop_state': prop_state, 'A': A, 'in_W': in_W, 'in_b': in_b, 'out_W': out_W, 'out_b': out_b, 'r_W': r_W, 'r_b': r_b, 'z_W': z_W, 'z_b': z_b, 'h_W': h_W, 'h_b': h_b, 'o1_W': o1_W, 'o1_b': o1_b, 'o2_W': o2_W, 'o2_b': o2_b}
    _L2_gnn_all = _L2_gnn_setup()
    _L2_gnn_in = {k: v for k, v in _L2_gnn_all.items() if k in ('in_W', 'in_b', 'out_W', 'out_b', 'r_W', 'r_b', 'z_W', 'z_b', 'h_W', 'h_b', 'o1_W', 'o1_b', 'o2_W', 'o2_b')}
    del _L2_gnn_all

    def _L3_gnn_setup():
        import jax, jax.numpy as jnp
        import numpy as np
        N = 2048
        IN_FEAT = 256
        EMBED = 256
        HEADS = 8
        HEAD_DIM = EMBED // HEADS
        SCALING = HEAD_DIM ** (-0.5)
        key = jax.random.key(seed)
        ks = jax.random.split(key, 7)
        x = jax.random.normal(ks[0], (N, IN_FEAT), dtype=jnp.float32)
        adj = jax.random.randint(ks[1], (N, N), 0, 2, dtype=jnp.int32)
        s = 0.04
        WQ = jax.random.normal(ks[2], (EMBED, IN_FEAT), dtype=jnp.float32) * s
        WK = jax.random.normal(ks[3], (EMBED, IN_FEAT), dtype=jnp.float32) * s
        WV = jax.random.normal(ks[4], (EMBED, IN_FEAT), dtype=jnp.float32) * s
        we = jax.random.normal(ks[5], (1, HEAD_DIM), dtype=jnp.float32) * 0.1
        be = jnp.zeros((1,), dtype=jnp.float32)
        return {'x': x, 'adj': adj, 'WQ': WQ, 'WK': WK, 'WV': WV, 'we': we, 'be': be}
    _L3_gnn_all = _L3_gnn_setup()
    _L3_gnn_in = {k: v for k, v in _L3_gnn_all.items() if k in ('WQ', 'WK', 'WV', 'we', 'be')}
    del _L3_gnn_all
    return {'x': x, 'adj': adj, 'L0_gnn_W_w': _L0_gnn_in['W_w'], 'L0_gnn_W_b': _L0_gnn_in['W_b'], 'L0_gnn_a': _L0_gnn_in['a'], 'L1_gnn_W_self': _L1_gnn_in['W_self'], 'L1_gnn_b_self': _L1_gnn_in['b_self'], 'L1_gnn_W_nb': _L1_gnn_in['W_nb'], 'L1_gnn_b_nb': _L1_gnn_in['b_nb'], 'L1_gnn_W_comb': _L1_gnn_in['W_comb'], 'L1_gnn_b_comb': _L1_gnn_in['b_comb'], 'L2_gnn_in_W': _L2_gnn_in['in_W'], 'L2_gnn_in_b': _L2_gnn_in['in_b'], 'L2_gnn_out_W': _L2_gnn_in['out_W'], 'L2_gnn_out_b': _L2_gnn_in['out_b'], 'L2_gnn_r_W': _L2_gnn_in['r_W'], 'L2_gnn_r_b': _L2_gnn_in['r_b'], 'L2_gnn_z_W': _L2_gnn_in['z_W'], 'L2_gnn_z_b': _L2_gnn_in['z_b'], 'L2_gnn_h_W': _L2_gnn_in['h_W'], 'L2_gnn_h_b': _L2_gnn_in['h_b'], 'L2_gnn_o1_W': _L2_gnn_in['o1_W'], 'L2_gnn_o1_b': _L2_gnn_in['o1_b'], 'L2_gnn_o2_W': _L2_gnn_in['o2_W'], 'L2_gnn_o2_b': _L2_gnn_in['o2_b'], 'L3_gnn_WQ': _L3_gnn_in['WQ'], 'L3_gnn_WK': _L3_gnn_in['WK'], 'L3_gnn_WV': _L3_gnn_in['WV'], 'L3_gnn_we': _L3_gnn_in['we'], 'L3_gnn_be': _L3_gnn_in['be']}

def reference(x, adj, L0_gnn_W_w, L0_gnn_W_b, L0_gnn_a, L1_gnn_W_self, L1_gnn_b_self, L1_gnn_W_nb, L1_gnn_b_nb, L1_gnn_W_comb, L1_gnn_b_comb, L2_gnn_in_W, L2_gnn_in_b, L2_gnn_out_W, L2_gnn_out_b, L2_gnn_r_W, L2_gnn_r_b, L2_gnn_z_W, L2_gnn_z_b, L2_gnn_h_W, L2_gnn_h_b, L2_gnn_o1_W, L2_gnn_o1_b, L2_gnn_o2_W, L2_gnn_o2_b, L3_gnn_WQ, L3_gnn_WK, L3_gnn_WV, L3_gnn_we, L3_gnn_be):
    import jax
    import jax.numpy as jnp

    def _L0_gnn_ref(x, adj, W_w, W_b, a):
        import jax, jax.numpy as jnp
        import numpy as np
        B, IN_F, OUT_F, H = (1024, 256, 256, 8)
        D = OUT_F // H
        Bn = x.shape[0]
        h = (x @ W_w.T + W_b).reshape(Bn, H, D)
        a_src, a_dst = (a[:D, 0], a[D:, 0])
        s_src = jnp.einsum('bhd,d->bh', h, a_src)
        s_dst = jnp.einsum('bhd,d->bh', h, a_dst)
        e = jax.nn.leaky_relu(s_src[:, None, :] + s_dst[None, :, :], negative_slope=0.2)
        e = jnp.where(adj[:, :, None] == 0, jnp.float32(-1000000000.0), e)
        attn = jax.nn.softmax(e, axis=1)
        h_prime = jnp.einsum('ijh,jhd->ihd', attn, h).reshape(Bn, H * D)
        return jax.nn.elu(h_prime)

    def _L1_gnn_ref(x, adj, W_self, b_self, W_nb, b_nb, W_comb, b_comb):
        import jax, jax.numpy as jnp
        import numpy as np
        N, D_IN, D_OUT = (4096, 256, 256)
        mask = (adj > 0).astype(x.dtype)
        deg = jnp.sum(mask, axis=1, keepdims=True)
        agg = mask @ x / jnp.maximum(deg, 1.0)
        self_f = x @ W_self + b_self
        nb_f = agg @ W_nb + b_nb
        combined = jnp.concatenate([self_f, nb_f], axis=-1)
        out = combined @ W_comb + b_comb
        return jax.nn.relu(out)

    def _L2_gnn_ref(prop_state, A, in_W, in_b, out_W, out_b, r_W, r_b, z_W, z_b, h_W, h_b, o1_W, o1_b, o2_W, o2_b):
        import jax, jax.numpy as jnp
        import numpy as np
        N = 2048
        STATE_DIM = 256
        OUTPUT_DIM = 256
        N_STEPS = 5
        W_STD = 0.02

        def _lin_params(key, out_dim, in_dim):
            W = jax.random.normal(key, (out_dim, in_dim), dtype=jnp.float32) * W_STD
            b = jnp.zeros((out_dim,), dtype=jnp.float32)
            return (W, b)
        Af = A.astype(prop_state.dtype)
        AfT = Af.T
        state = prop_state
        for _ in range(N_STEPS):
            s_in = state @ in_W.T + in_b
            s_out = state @ out_W.T + out_b
            a_in = Af @ s_in
            a_out = AfT @ s_out
            a = jnp.concatenate([a_in, a_out, state], axis=-1)
            r = jax.nn.sigmoid(a @ r_W.T + r_b)
            z = jax.nn.sigmoid(a @ z_W.T + z_b)
            joined = jnp.concatenate([a_in, a_out, r * state], axis=-1)
            h_hat = jnp.tanh(joined @ h_W.T + h_b)
            state = (1.0 - z) * state + z * h_hat
        out = jnp.tanh(state @ o1_W.T + o1_b) @ o2_W.T + o2_b
        return out

    def _L3_gnn_ref(x, adj, WQ, WK, WV, we, be):
        import jax, jax.numpy as jnp
        import numpy as np
        N = 2048
        IN_FEAT = 256
        EMBED = 256
        HEADS = 8
        HEAD_DIM = EMBED // HEADS
        SCALING = HEAD_DIM ** (-0.5)
        n = x.shape[0]
        Q = (x @ WQ.T).reshape(n, HEADS, HEAD_DIM).transpose(1, 0, 2)
        K = (x @ WK.T).reshape(n, HEADS, HEAD_DIM).transpose(1, 0, 2)
        V = (x @ WV.T).reshape(n, HEADS, HEAD_DIM).transpose(1, 0, 2)
        energy = Q @ we.T + be
        attn = jnp.einsum('hqd,hkd->hqk', Q, K) * SCALING + energy
        attn = attn + jnp.where(adj > 0, 0.0, -jnp.inf)
        attn = jax.nn.softmax(attn, axis=-1)
        hard = (attn == jnp.max(attn, axis=-1, keepdims=True)).astype(jnp.float32) / HEADS
        out = jnp.einsum('hqk,hkd->hqd', hard, V)
        return out.transpose(1, 0, 2).reshape(n, EMBED)
    h = jnp.maximum(_layernorm(x, axis=-1), 0.0)
    x = x + _L0_gnn_ref(h, adj, L0_gnn_W_w, L0_gnn_W_b, L0_gnn_a)
    h = jnp.maximum(_layernorm(x, axis=-1), 0.0)
    x = x + _L1_gnn_ref(h, adj, L1_gnn_W_self, L1_gnn_b_self, L1_gnn_W_nb, L1_gnn_b_nb, L1_gnn_W_comb, L1_gnn_b_comb)
    h = jnp.maximum(_layernorm(x, axis=-1), 0.0)
    x = x + _L2_gnn_ref(h, adj, L2_gnn_in_W, L2_gnn_in_b, L2_gnn_out_W, L2_gnn_out_b, L2_gnn_r_W, L2_gnn_r_b, L2_gnn_z_W, L2_gnn_z_b, L2_gnn_h_W, L2_gnn_h_b, L2_gnn_o1_W, L2_gnn_o1_b, L2_gnn_o2_W, L2_gnn_o2_b)
    h = jnp.maximum(_layernorm(x, axis=-1), 0.0)
    x = x + _L3_gnn_ref(h, adj, L3_gnn_WQ, L3_gnn_WK, L3_gnn_WV, L3_gnn_we, L3_gnn_be)
    return x

_drawn_inputs = setup_inputs


def setup_inputs(seed=0):
    import zlib

    import numpy as np

    out = dict(_drawn_inputs(seed))
    spreads = {'L0_gnn_W_b': (0.0, 0.1),
     'L2_gnn_in_b': (0.0, 0.288),
     'L2_gnn_out_b': (0.0, 0.299),
     'L2_gnn_r_b': (0.0, 0.8),
     'L2_gnn_z_b': (0.0, 0.8),
     'L2_gnn_h_b': (0.0, 0.788),
     'L2_gnn_o1_b': (0.0, 0.1),
     'L2_gnn_o2_b': (0.0, 0.1)}
    factors = {'L1_gnn_b_self': 5.938,
     'L1_gnn_b_nb': 5.225,
     'L1_gnn_b_comb': 3.219,
     'L2_gnn_r_W': 8.0,
     'L2_gnn_z_W': 3.918}
    for name, (base, spread) in spreads.items():
        noise = np.random.default_rng([zlib.crc32(name.encode()), seed]).standard_normal(out[name].shape)
        drawn = base * np.exp(spread * noise) if base else spread * noise
        out[name] = jnp.asarray(drawn.astype(out[name].dtype))
    for name, factor in factors.items():
        out[name] = (out[name] * factor).astype(out[name].dtype)
    return out
```

```python
from contextlib import ExitStack

import concourse.bass as bass
from concourse import mybir
from concourse.alu_op_type import AluOpType as ALU

ACT = mybir.ActivationFunctionType
F32, F16, F8, I32, U32 = (mybir.dt.float32, mybir.dt.float16, mybir.dt.float8e4, mybir.dt.int32,
                          mybir.dt.uint32)
AX_X = mybir.AxisListType.X
RADD, RMAX = bass.bass_isa.ReduceOp.add, bass.bass_isa.ReduceOp.max

P = 128
N = 2048
D = 256
NT = N // P
FT = D // P
H = 8
HD = D // H
CH = 512
NC = N // CH
STEPS = 5
EPS = 1e-5
STATE_SCALE = 2048.0
WEIGHT_SCALE = 4096.0
BIG = 1e38
KB = 1024


class Count:

    def __init__(self, sem, unit=1):
        self.sem, self.unit, self.n = sem, unit, 0

    def on(self, ins):
        ins.then_inc(self.sem, self.unit)
        self.n += self.unit
        return self.n


class Chip:

    def __init__(self, nc, ctx, dram, out):
        self.nc, self.ctx, self.dram, self.out = nc, ctx, dram, out
        self.owned = []
        self.arena = ctx.enter_context(nc.sbuf_tensor("arena", [P, 204 * KB // 4], F32))
        self.psum = ctx.enter_context(nc.psum_tensor("psum", [P, 8, CH], F32))
        self.scales, self.splits = ctx.enter_context(nc.sbuf_tensor("scales", [P, 5, 8], F32)), 0
        self.ident = ctx.enter_context(nc.sbuf_tensor("ident", [P, P], F16))

    def sem(self, name):
        self.owned.append(self.ctx.enter_context(self.nc.semaphore(name)))
        return self.owned[-1]

    def clear_semaphores(self):
        with self.nc.Block() as block:
            @block.gpsimd
            def _(pool):
                for s in self.owned:
                    pool.sem_clear(s)

    def view(self, at, shape, dt):
        size = {F32: 4, F16: 2, F8: 1, I32: 4}[dt]
        n = 1
        for s in shape:
            n *= s
        v = self.arena[:, at // 4:at // 4 + (n * size + 3) // 4]
        if dt != F32:
            v = v.bitcast(dt)
        v = v[:, 0:n]
        names = "abcdeg"[:len(shape)]
        if len(shape) > 1:
            v = v.rearrange(f"p ({' '.join(names)}) -> p {' '.join(names)}",
                            **{k: s for k, s in zip(names, shape)})
        return v

    def bank16(self, b):
        return self.psum[:, b, :].bitcast(F16)


AT_A = 0
AT_AT = 32 * KB
AT_X = 64 * KB
AT_SP = 80 * KB
AT_ST = 96 * KB
AT_W = 112 * KB
AT_FREE = 112 * KB + 28 * KB


def load_phase(c, S):
    nc = c.nc
    stage = c.view(AT_SP, [2, N], I32)
    rows16 = c.view(AT_SP + 16 * KB, [2, N], F16)
    a_rows, a_cols = c.view(AT_A, [NT, N], F8), c.view(AT_AT, [NT, N], F8)
    x = c.view(AT_X, [NT, D], F32)
    adj = c.dram["adj"].rearrange("(t p) j -> t p j", p=P)

    adj_loaded = [c.sem("adj_loaded0"), c.sem("adj_loaded1")]
    x_loaded = c.sem("x_loaded")
    rows_cast = c.sem("rows_cast")
    rows_kept = c.sem("rows_kept")
    turned = c.sem("turned")
    cols_kept = c.sem("cols_kept")
    ident_zero, ident_made = c.sem("ident_zero"), c.sem("ident_made")

    with nc.Block() as block:
        @block.sync
        def _(sp):
            for u in range(2):
                sp.dma_start(stage[:, u, :], adj[u]).then_inc(adj_loaded[u], 16)
            sp.dma_start(x, c.dram["x"].rearrange("(t p) f -> p t f", p=P)).then_inc(x_loaded, 16)
            with sp.Fori(1, NT // 2) as i:
                for u in range(2):
                    sp.wait_ge(rows_kept, 2 * i + u - 1)
                    sp.dma_start(stage[:, u, :], adj[bass.ds(2 * i + u, 1), :, :].rearrange("a p j -> (a p) j")
                                 ).then_inc(adj_loaded[u], 16)
            sp.wait_ge(x_loaded, 16)

        @block.scalar
        def _(act):
            for t in range(NT):
                act.wait_ge(adj_loaded[t % 2], 16 * (t // 2 + 1))
                if t >= 2:
                    act.wait_ge(turned, t - 1)
                nc.scalar.activation(rows16[:, t % 2, :], stage[:, t % 2, :], ACT.Copy,
                                     accum_out=S.degree[:, t:t + 1]).then_inc(rows_cast, 1)
                nc.scalar.activation(a_rows[:, t, :], stage[:, t % 2, :], ACT.Copy,
                                     saturate=False).then_inc(rows_kept, 1)

        @block.gpsimd
        def _(pool):
            nc.gpsimd.memset(c.ident[:, :], 0.0).then_inc(ident_zero, 1)
            pool.wait_ge(ident_zero, 1)
            nc.gpsimd.affine_select(out=c.ident[:, :], in_=c.ident[:, :], compare_op=ALU.not_equal, fill=1.0,
                                    base=0, pattern=[[-1, P]], channel_multiplier=1).then_inc(ident_made, 1)

        @block.tensor
        def _(pe):
            pe.wait_ge(ident_made, 1)

            def turn(i, u):
                pe.wait_ge(rows_cast, 2 * i + u + 1)
                for t in range(NT):
                    last = nc.tensor.transpose(c.bank16(2 * u + t // 8)[:, P * (t % 8):P * (t % 8 + 1)],
                                               rows16[:, u, P * t:P * (t + 1)], c.ident[:, :])
                last.then_inc(turned, 1)

            for u in range(2):
                turn(0, u)
            with pe.Fori(1, NT // 2) as i:
                for u in range(2):
                    pe.wait_ge(cols_kept, 2 * i + u - 1)
                    turn(i, u)

        @block.vector
        def _(dve):
            for t in range(NT):
                u = t % 2
                dve.wait_ge(turned, t + 1)
                src = c.psum[:, 2 * u:2 * u + 2, :].rearrange("p b n -> p (b n)").bitcast(F16)
                nc.vector.tensor_copy(a_cols[:, :, t * P:(t + 1) * P], src.rearrange("p (t i) -> p t i", i=P),
                                      saturate=False).then_inc(cols_kept, 1)


class Chain:

    def __init__(self, eng, sem):
        self.eng, self.sem, self.n = eng, sem, 0

    def __call__(self, ins):
        ins.then_inc(self.sem, 1)
        self.n += 1
        self.eng.wait_ge(self.sem, self.n)


class NodeValues:

    def __init__(self, c, name, tmp):
        self.c, self.nc = c, c.nc
        nc, sem = c.nc, lambda n: c.sem(f"{name}_{n}")
        self.x = c.view(AT_X, [NT, D], F32)
        self.sp = c.view(AT_SP, [NT, 2 * D], F16)
        self.st = c.view(AT_ST, [2 * FT, N], F16)
        self.centred = c.view(tmp, [NT, D], F32)
        small = tmp + 16 * KB
        self.stats = c.view(small, [NT, 6], F32)
        self.moments = c.view(small + 512, [NT, 2], F32)
        self.var = c.view(small + 768, [NT], F32)
        self.dev = c.view(small + 832, [NT], F32)
        self.inv = c.view(small + 896, [NT], F32)
        self.t1 = c.view(small + 960, [NT], F32)
        self.factor = c.view(small + 1024, [NT], F32)
        self.chain_dve = sem("chain")
        self.var_ready, self.dev_ready, self.factor_ready = sem("var"), sem("dev"), sem("factor")
        self.stats_ready = sem("stats")
        self.moments_ready = sem("moments")
        self.centre_ready, self.high, self.low = sem("centre"), sem("high"), sem("low")
        self.turned, self.kept = sem("turned"), sem("kept")

    def vector(self, dve):
        nc = self.nc
        link = Chain(dve, self.chain_dve)
        for t in range(NT):
            nc.vector.bn_stats(self.stats[:, t, :], self.x[:, t, :]).then_inc(self.stats_ready, 1)
        for t in range(NT):
            dve.wait_ge(self.stats_ready, t + 1)
            nc.vector.bn_aggr(self.moments[:, t, :], self.stats[:, t, :]).then_inc(self.moments_ready, 1)
        dve.wait_ge(self.moments_ready, NT)
        nc.vector.tensor_scalar(self.var, self.moments[:, :, 1], EPS, None, ALU.add).then_inc(self.var_ready, 1)
        for t in range(NT):
            nc.vector.tensor_scalar(self.centred[:, t, :], self.x[:, t, :], self.moments[:, t, 0:1], 0.0,
                                    ALU.subtract, ALU.max).then_inc(self.centre_ready, 1)
        dve.wait_ge(self.dev_ready, 1)
        link(nc.vector.reciprocal(self.inv, self.dev))
        dve.wait_ge(self.var_ready, 1)
        link(nc.vector.tensor_tensor(self.t1, self.inv, self.inv, ALU.mult))
        link(nc.vector.tensor_tensor(self.t1, self.t1, self.var, ALU.mult))
        link(nc.vector.tensor_scalar(self.t1, self.t1, -0.5 * STATE_SCALE, 1.5 * STATE_SCALE, ALU.mult, ALU.add))
        nc.vector.tensor_tensor(self.factor, self.t1, self.inv, ALU.mult).then_inc(self.factor_ready, 1)
        dve.wait_ge(self.factor_ready, 1)
        dve.wait_ge(self.centre_ready, NT)
        for t in range(NT):
            dve.wait_ge(self.high, t + 1)
            nc.vector.scalar_tensor_tensor(self.sp[:, t, D:2 * D], self.centred[:, t, :], self.factor[:, t:t + 1],
                                           self.sp[:, t, 0:D], ALU.mult, ALU.subtract).then_inc(self.low, 1)

    def scalar(self, act):
        nc = self.nc
        act.wait_ge(self.var_ready, 1)
        nc.scalar.activation(self.dev, self.var, ACT.Sqrt).then_inc(self.dev_ready, 1)
        act.wait_ge(self.factor_ready, 1)
        act.wait_ge(self.centre_ready, NT)
        for t in range(NT):
            nc.scalar.activation(self.sp[:, t, 0:D], self.centred[:, t, :], ACT.Copy,
                                 scale=self.factor[:, t:t + 1]).then_inc(self.high, 1)
            if t:
                self.keep(act, t - 1)
        self.keep(act, NT - 1)

    def keep(self, act, t):
        act.wait_ge(self.turned, t + 1)
        b = 6 + t % 2
        self.nc.scalar.activation(self.st[:, :, t * P:(t + 1) * P],
                                  self.c.bank16(b)[:, 0:4 * P].rearrange("p (k i) -> p k i", i=P),
                                  ACT.Copy).then_inc(self.kept, 1)

    def tensor(self, pe):
        for t in range(NT):
            pe.wait_ge(self.low, t + 1)
            pe.wait_ge(self.high, t + 1)
            if t >= 2:
                pe.wait_ge(self.kept, t - 1)
            for k in range(4):
                last = self.nc.tensor.transpose(self.c.bank16(6 + t % 2)[:, k * P:(k + 1) * P],
                                                self.sp[:, t, k * P:(k + 1) * P], self.c.ident[:, :])
            last.then_inc(self.turned, 1)


class Split:

    def __init__(self, c, name, w, hi, lo, top=WEIGHT_SCALE):
        self.c, self.nc, self.w, self.hi, self.lo = c, c.nc, w, hi, lo
        t = c.scales[:, c.splits, :]
        c.splits += 1
        self.top = top
        (self.own, self.all_, self.pow2, self.inv, self.scale, self.unscale, self.plain,
         self.half) = (t[:, k:k + 1] for k in range(8))
        sem = lambda n: c.sem(f"{name}_{n}")
        self.own_max, self.all_max, self.chain, self.scaled, self.high, self.low = (
            sem("own_max"), sem("all_max"), sem("chain"), sem("scaled"), sem("high"), sem("low"))

    def vector(self, dve):
        nc = self.nc
        link = Chain(dve, self.chain)
        nc.vector.tensor_reduce(self.own, self.w, AX_X, ALU.max, apply_absolute_value=True).then_inc(self.own_max, 1)
        dve.wait_ge(self.all_max, 1)
        link(nc.vector.tensor_scalar(self.all_, self.all_, 1e-30, None, ALU.max))
        link(nc.vector.tensor_scalar(self.pow2.bitcast(U32), self.all_.bitcast(U32), 0x7F800000, None,
                                     ALU.bitwise_and))
        link(nc.vector.reciprocal(self.inv, self.pow2))
        link(nc.vector.tensor_scalar(self.unscale, self.pow2, 1.0 / (self.top * STATE_SCALE), None, ALU.mult))
        link(nc.vector.tensor_scalar(self.plain, self.pow2, 1.0 / self.top, None, ALU.mult))
        link(nc.vector.tensor_scalar(self.half, self.pow2, 0.5 / self.top, None, ALU.mult))
        nc.vector.tensor_scalar(self.scale, self.inv, self.top, None, ALU.mult).then_inc(self.scaled, 1)
        dve.wait_ge(self.scaled, 1)
        dve.wait_ge(self.high, 1)
        nc.vector.scalar_tensor_tensor(self.lo, self.w, self.scale, self.hi, ALU.mult, ALU.subtract).then_inc(self.low, 1)

    def gpsimd(self, pool):
        pool.wait_ge(self.own_max, 1)
        self.nc.gpsimd.partition_all_reduce(self.all_, self.own, P, RMAX).then_inc(self.all_max, 1)

    def scalar(self, act):
        act.wait_ge(self.scaled, 1)
        self.nc.scalar.activation(self.hi, self.w, ACT.Copy, scale=self.scale).then_inc(self.high, 1)

    def ready(self, eng):
        eng.wait_ge(self.high, 1)
        eng.wait_ge(self.low, 1)


PARTS3 = ((0, 0), (0, 1), (1, 0))


def bc(ap, shape, axis):
    return ap.unsqueeze(axis + 1).broadcast_to([P] + shape)


def attention_layer(c, S):
    nc, dram = c.nc, c.dram
    HX = D + 2 * H
    V = HD + 1
    a_cols = c.view(AT_AT, [NT, N], F8)
    x = c.view(AT_X, [NT, D], F32)
    F = AT_FREE
    hx = c.view(F, [NT, HX], F32)
    s_rep = c.view(F + 18 * KB, [2, N], F32)
    s_rows = c.view(F + 34 * KB, [N], F32)
    edges = c.view(F + 34 * KB, [4, N], F8)
    sums = c.view(F + 42 * KB, [NT, 2, 2, V], F32)
    both = c.view(F + 42 * KB + 8448, [NT, 2, V], F32)
    fbuf = c.view(F + 42 * KB + 8448 + 4224, [2, NT, 2, V], F32)
    fg = c.view(AT_SP, [2, NT, 3, 2, V], F16)
    total = c.view(AT_SP + 13 * KB, [NT, H, V], F32)
    W = AT_W
    w_rows = c.view(W, [FT, D], F32)
    b_rep = c.view(W + 2 * KB, [FT, P], F32)
    bias = c.view(W + 3 * KB, [HX], F32)
    a_blk = c.view(W + 3 * KB + 1088, [FT, 2 * H], F32)
    w32 = c.view(W + 5 * KB, [FT * HX], F32)
    whi = c.view(W + 8 * KB, [FT * HX], F16)
    wlo = c.view(W + 8 * KB + 1088, [FT * HX], F16)
    w32t = w32.rearrange("p (k n) -> p k n", n=HX)
    wp = [v.rearrange("p (k n) -> p k n", n=HX) for v in (whi, wlo)]
    b_col = c.view(W + 11 * KB, [FT], F32)
    mean_h = c.view(W + 11 * KB + 64, [H, V], F32)
    ones = c.view(W + 13 * KB, [P], F32)
    q = W + 14 * KB
    small = {}
    for n in ("ed", "eg", "es", "et", "neg_d", "u", "tmp", "rden"):
        small[n] = c.view(q, [NT, H], F32)
        q += 512
    nd2 = c.view(q, [2, NT], F32)
    empty = c.view(q + 128, [NT], F32)
    s_bias = c.view(q + 192, [1], F32)
    peak = c.view(q + 196, [H + 1], F32)
    peaks = c.view(q + 236, [H + 1], F32)
    hs = c.view(q + 276, [6], F32)
    h_pow, h_inv, h_scale, h_back, h_mean = (hs[:, k:k + 1] for k in range(5))
    et2 = c.view(q + 320, [NT, H, 2], F32)
    v_all = c.view(F, [NT, H, HD], F32)
    e_all = c.view(F + 18 * KB, [NT, H, HD], F32)
    scratch = nc.dram_tensor("s_rows_dram", [H, N], F32, kind="Internal").ap()

    nodes = NodeValues(c, "n0", F + 18 * KB)
    split = Split(c, "w0", w32, whi, wlo)
    sem = lambda n: c.sem("g_" + n)
    w_loaded, a_loaded = sem("w_loaded"), sem("a_loaded")
    blk_zero, rep_made, wa_made, w_made, ba_made = sem("blk_zero"), sem("rep_made"), sem("wa_made"), sem("w_made"), sem("ba_made")
    ones_made = sem("ones_made")
    h_summed, h_kept, s_summed, s_kept = sem("h_summed"), sem("h_kept"), sem("s_summed"), sem("s_kept")
    s_stored, s_spread = sem("s_stored"), [sem("s_spread0"), sem("s_spread1")]
    peak_own, peak_all = sem("peak_own"), sem("peak_all")
    prep, exps, shifts = sem("prep"), sem("exps"), sem("shifts")
    mean_summed = sem("mean_summed")
    f_made, hi_made, lo_made = sem("f_made"), sem("hi_made"), sem("lo_made")
    edge_made, edge_free = sem("edge_made"), sem("edge_free")
    fg_used = sem("fg_used")
    evacuated = sem("evacuated")
    merged = sem("merged")
    nd_copied = sem("nd_copied")
    dchain, pchain, achain = sem("dchain"), sem("pchain"), sem("achain")
    tail = sem("tail")
    pe_steps, dve_steps = sem("pe_steps"), sem("dve_steps")

    with nc.Block() as block:
        @block.sync
        def _(sp):
            sp.dma_start(w_rows, dram["L0_W"].rearrange("(t p) f -> p t f", p=P)).then_inc(w_loaded, 16)
            sp.dma_start(w32t[:, :, 0:D], dram["L0_WT"].rearrange("(t p) f -> p t f", p=P)).then_inc(w_loaded, 16)
            sp.dma_start(bias[:, 0:D], dram["L0_b"].partition_broadcast(P)).then_inc(w_loaded, 16)
            sp.dma_start(b_col, dram["L0_bcol"]).then_inc(w_loaded, 16)
            sp.wait_ge(blk_zero, 1)
            for h in range(H):
                lo = HD * (h % 4)
                sp.dma_start(a_blk[lo:lo + HD, h // 4, h:h + 1], dram["L0_a"][0:HD, :]).then_inc(a_loaded, 16)
                sp.dma_start(a_blk[lo:lo + HD, h // 4, H + h:H + h + 1], dram["L0_a"][HD:2 * HD, :]).then_inc(a_loaded, 16)
            sp.wait_ge(s_kept, NC)
            sp.dma_start(scratch, s_rows[0:H, :]).then_inc(s_stored, 16)
            sp.wait_ge(s_stored, 16)
            for h in range(H):
                if h >= 2:
                    sp.wait_ge(edge_made, NT * (h - 1))
                sp.dma_start(s_rep[:, h % 2, :], scratch[h, :].partition_broadcast(P)).then_inc(s_spread[h % 2], 16)
            sp.wait_ge(s_spread[0], 16 * (H // 2))
            sp.wait_ge(s_spread[1], 16 * (H // 2))

        @block.tensor
        def _(pe):
            pe.wait_ge(w_loaded, 64)
            pe.wait_ge(a_loaded, 16 * 2 * H)
            for k in range(FT):
                for o in range(FT):
                    last = nc.tensor.matmul(c.psum[:, 0, k * 2 * H:(k + 1) * 2 * H], w_rows[:, o, k * P:(k + 1) * P],
                                            a_blk[:, o, :], start=(o == 0), stop=(o == FT - 1))
            last.then_inc(wa_made, 1)
            pe.wait_ge(rep_made, FT)
            for o in range(FT):
                last = nc.tensor.matmul(c.psum[:, 1, 0:2 * H], b_rep[:, o, :], a_blk[:, o, :],
                                        start=(o == 0), stop=(o == FT - 1))
            for o in range(FT):
                last = nc.tensor.matmul(c.psum[0:H, 2, 0:1], a_blk[:, o, 0:H], b_col[:, o:o + 1],
                                        start=(o == 0), stop=(o == FT - 1))
            last.then_inc(ba_made, 1)
            nodes.tensor(pe)
            split.ready(pe)
            pe.wait_ge(nodes.kept, NT)
            pe.wait_ge(w_made, 3)
            for t in range(NT):
                if t >= 4:
                    pe.wait_ge(h_kept, t - 3)
                n = 0
                for k in range(FT):
                    for a, b in PARTS3:
                        last = nc.tensor.matmul(c.psum[:, t % 4, 0:HX], nodes.st[:, 2 * a + k, t * P:(t + 1) * P],
                                                wp[b][:, k, :], start=(n == 0), stop=(n == 5))
                        n += 1
                last.then_inc(h_summed, 1)
            for j in range(NC):
                if j >= 2:
                    pe.wait_ge(s_kept, j - 1)
                n = 0
                for k in range(FT):
                    for a, b in PARTS3:
                        last = nc.tensor.matmul(c.psum[0:H, 4 + j % 2, :], wp[b][:, k, D:D + H],
                                                nodes.st[:, 2 * a + k, j * CH:(j + 1) * CH], start=(n == 0), stop=(n == 5))
                        n += 1
                last.then_inc(s_summed, 1)
            pe.wait_ge(h_kept, NT)
            pe.wait_ge(ones_made, 1)
            for t in range(NT):
                last = nc.tensor.matmul(c.psum[:, 6, 0:D], ones, hx[:, t, 0:D], start=(t == 0), stop=(t == NT - 1))
            last.then_inc(mean_summed, 1)
            pe.wait_ge(evacuated, 1)

            with pe.Fori(0, H // 2) as i:
                for u in range(2):
                    n = 2 * i + u
                    pe.wait_ge(hi_made, n + 1)
                    pe.wait_ge(lo_made, n + 3)
                    pe.wait_ge(evacuated, 6 * n + 1)
                    for j in range(NT):
                        pe.wait_ge(edge_made, NT * n + j + 1)
                        pe.sem_inc(pe_steps)
                        for t in range(NT):
                            o = c.psum[:, t // 3, 4 * V * (t % 3):4 * V * (t % 3 + 1)]
                            mm = nc.tensor.matmul(o, edges[:, j % 4, t * P:(t + 1) * P],
                                                  fg[:, u, j, 0:2, :, :].rearrange("p a b v -> p (a b v)"),
                                                  start=(j == 0 and t % 3 == 0), stop=(j == NT - 1), skip_group_check=True)
                            if t == NT - 1:
                                mm.then_inc(edge_free, 1)
                            last = nc.tensor.matmul(o[:, 2 * V:4 * V], a_cols[:, j, t * P:(t + 1) * P],
                                                    fg[:, u, j, 2, :, :].rearrange("p b v -> p (b v)"),
                                                    start=False, stop=(j == NT - 1), skip_group_check=True)
                    last.then_inc(fg_used, 1)

        @block.vector
        def _(dve):
            link = Chain(dve, dchain)
            nc.vector.memset(ones, 1.0).then_inc(ones_made, 1)
            dve.sem_inc(edge_free, 4)
            dve.sem_inc(lo_made, 2)
            nc.vector.memset(a_blk, 0.0).then_inc(blk_zero, 1)
            dve.wait_ge(w_loaded, 64)
            for o in range(FT):
                nc.vector.tensor_copy(b_rep[:, o, :], b_col[:, o:o + 1].broadcast_to([P, P])).then_inc(rep_made, 1)
            dve.wait_ge(wa_made, 1)
            nc.vector.tensor_copy(w32t[:, :, D:HX], c.psum[:, 0, 0:4 * H].rearrange("p (k n) -> p k n", k=FT)
                                  ).then_inc(w_made, 1)
            dve.wait_ge(w_made, 1)
            split.vector(dve)
            dve.wait_ge(ba_made, 1)
            nc.vector.tensor_copy(bias[:, D:HX], c.psum[:, 1, 0:2 * H]).then_inc(w_made, 1)
            nc.vector.tensor_copy(s_bias[0:H, :], c.psum[0:H, 2, 0:1]).then_inc(w_made, 1)
            dve.wait_ge(w_made, 3)
            nodes.vector(dve)
            nc.vector.tensor_scalar(empty, S.degree[:, :], 0.0, None, ALU.is_equal).then_inc(tail, 1)
            for t in range(NT):
                dve.wait_ge(h_summed, t + 1)
                nc.vector.scalar_tensor_tensor(hx[:, t, :], c.psum[:, t % 4, 0:HX], split.unscale, bias,
                                               ALU.mult, ALU.add).then_inc(h_kept, 1)
            dve.wait_ge(h_kept, NT)
            s_all, d_all = hx[:, :, D:D + H], hx[:, :, D + H:HX]
            link(nc.vector.tensor_reduce(peak[:, H:H + 1], hx[:, :, 0:D], mybir.AxisListType.XY, ALU.max,
                                         apply_absolute_value=True))
            nc.vector.tensor_reduce(peak[:, 0:H], d_all.rearrange("p t h -> p h t"), AX_X, ALU.max).then_inc(peak_own, 1)
            link(nc.vector.tensor_scalar(small["neg_d"], d_all, -1.0, None, ALU.mult))
            dve.wait_ge(peak_all, 1)
            top = peaks[:, 0:H].unsqueeze(1).broadcast_to([P, NT, H])
            link(nc.vector.tensor_tensor(small["u"], s_all, top, ALU.add))
            link(nc.vector.tensor_scalar(small["es"], small["u"], 0.8, 0.0, ALU.mult, ALU.min))
            link(nc.vector.tensor_scalar(small["et"], small["u"], -0.8, 0.0, ALU.mult, ALU.min))
            nc.vector.tensor_tensor(small["tmp"], d_all, top, ALU.subtract).then_inc(shifts, 1)
            link(nc.vector.tensor_scalar(peaks[:, H:H + 1], peaks[:, H:H + 1], 1e-30, None, ALU.max))
            link(nc.vector.tensor_scalar(h_pow.bitcast(U32), peaks[:, H:H + 1].bitcast(U32), 0x7F800000, None, ALU.bitwise_and))
            link(nc.vector.reciprocal(h_inv, h_pow))
            link(nc.vector.tensor_scalar(h_scale, h_inv, WEIGHT_SCALE, None, ALU.mult))
            link(nc.vector.tensor_scalar(h_back, h_pow, 1.0, None, ALU.mult))
            link(nc.vector.tensor_scalar(h_mean, h_scale, 1.0 / N, None, ALU.mult))
            dve.wait_ge(mean_summed, 1)
            nc.vector.tensor_scalar(mean_h[:, :, 0:HD], c.psum[:, 6, 0:D].rearrange("p (h v) -> p h v", v=HD),
                                    h_mean, None, ALU.mult).then_inc(prep, 1)
            nc.vector.memset(mean_h[:, :, HD:V], WEIGHT_SCALE).then_inc(prep, 1)
            dve.wait_ge(exps, 4)

            def make_f(n, u):
                for g, e in enumerate(("ed", "eg")):
                    col = small[e][:, :, bass.ds(n, 1)]
                    nc.vector.scalar_tensor_tensor(fbuf[:, u, :, g, 0:HD], hx[:, :, bass.ds(n * HD, HD)], h_scale,
                                                   col.broadcast_to([P, NT, HD]), ALU.mult, ALU.mult).then_inc(f_made, 1)
                    nc.vector.tensor_scalar(fbuf[:, u, :, g, HD:V], col, WEIGHT_SCALE, None, ALU.mult).then_inc(f_made, 1)
                nc.vector.tensor_copy(nd2[:, u, :], small["neg_d"][:, :, bass.ds(n, 1)].rearrange("p t a -> p (t a)")
                                      ).then_inc(nd_copied, 1)

            with dve.Fori(0, H // 2) as i:
                for u in range(2):
                    n = 2 * i + u
                    dve.wait_ge(lo_made, n + 1)
                    make_f(n, u)
                    dve.wait_ge(nd_copied, n + 1)
                    dve.wait_ge(s_spread[u], 16 * i + 16)
                    for j in range(NT):
                        dve.wait_ge(edge_free, NT * n + j + 1)
                        dve.sem_inc(dve_steps)
                        nc.vector.scalar_tensor_tensor(edges[:, j % 4, :], s_rep[:, u, :], nd2[:, u, j:j + 1],
                                                       a_cols[:, j, :], ALU.is_gt, ALU.mult, saturate=False).then_inc(edge_made, 1)
            dve.wait_ge(merged, 3 * H)
            flat = total.rearrange("p t h v -> p t (h v)")
            for t in range(NT):
                nc.vector.scalar_tensor_tensor(flat[:, t, :], mean_h.rearrange("p h v -> p (h v)"), empty[:, t:t + 1],
                                               flat[:, t, :], ALU.mult, ALU.add).then_inc(tail, 1)
            dve.wait_ge(tail, NT + 1)
            link(nc.vector.reciprocal(small["rden"], total[:, :, :, HD]))
            link(nc.vector.tensor_scalar(small["rden"], small["rden"], h_back, None, ALU.mult))
            for t in range(0, NT, 4):
                nc.vector.tensor_tensor(v_all[:, t:t + 4], total[:, t:t + 4, :, 0:HD],
                                        small["rden"][:, t:t + 4, :].unsqueeze(3).broadcast_to([P, 4, H, HD]),
                                        ALU.mult).then_inc(tail, 1)
            v2, e2 = (v.rearrange("p t h v -> p (t h v)") for v in (v_all, e_all))
            xf = x.rearrange("p t f -> p (t f)")
            dve.wait_ge(tail, NT + 5)
            nc.vector.tensor_scalar(e2, v2, 0.0, None, ALU.min).then_inc(tail, 1)
            dve.wait_ge(exps, 5)
            dve.wait_ge(tail, NT + 6)
            link(nc.vector.scalar_tensor_tensor(v2, v2, 0.0, e2, ALU.max, ALU.add))
            link(nc.vector.scalar_tensor_tensor(xf, v2, -1.0, xf, ALU.add, ALU.add))

        @block.gpsimd
        def _(pool):
            link = Chain(pool, pchain)
            split.gpsimd(pool)
            pool.wait_ge(peak_own, 1)
            nc.gpsimd.partition_all_reduce(peaks, peak, P, RMAX).then_inc(peak_all, 1)
            pool.wait_ge(exps, 4)
            link(nc.gpsimd.tensor_copy(et2[:, :, :, 0], small["es"]))
            link(nc.gpsimd.tensor_copy(et2[:, :, :, 1], small["et"]))
            def parts(n, u):
                pool.wait_ge(f_made, 4 * n + 4)
                pool.wait_ge(hi_made, n + 1)
                f, g = fbuf[:, u, :, 0, :], fbuf[:, u, :, 1, :]
                nc.gpsimd.tensor_tensor(fg[:, u, :, 0, 1, :], f, fg[:, u, :, 0, 0, :], ALU.subtract)
                nc.gpsimd.tensor_tensor(fg[:, u, :, 1, 1, :], fg[:, u, :, 2, 0, :], g, ALU.subtract)
                nc.gpsimd.tensor_tensor(fg[:, u, :, 2, 1, :], g, fg[:, u, :, 2, 0, :], ALU.subtract).then_inc(lo_made, 1)

            def merge(n):
                if n:
                    pool.wait_ge(merged, 3 * n)
                pool.wait_ge(evacuated, 6 * n + 7)
                nc.gpsimd.tensor_tensor(both, sums[:, :, :, 0, :], sums[:, :, :, 1, :], ALU.add).then_inc(merged, 1)
                pool.wait_ge(merged, 3 * n + 1)
                nc.gpsimd.tensor_tensor(both, both, et2[:, :, bass.ds(n, 1), :].rearrange("p t a g -> p t (a g)")
                                        .unsqueeze(3).broadcast_to([P, NT, 2, V]), ALU.mult).then_inc(merged, 1)
                pool.wait_ge(merged, 3 * n + 2)
                nc.gpsimd.tensor_tensor(total[:, :, bass.ds(n, 1), :].rearrange("p t a v -> p t (a v)"), both[:, :, 0, :],
                                        both[:, :, 1, :], ALU.add).then_inc(merged, 1)

            for n in range(H):
                parts(n, n % 2)
                if n:
                    merge(n - 1)
            merge(H - 1)

        @block.scalar
        def _(act):
            split.scalar(act)
            nodes.scalar(act)
            act.wait_ge(w_made, 3)
            for j in range(NC):
                act.wait_ge(s_summed, j + 1)
                nc.scalar.activation(s_rows[0:H, j * CH:(j + 1) * CH], c.psum[0:H, 4 + j % 2, :], ACT.Identity,
                                     bias=s_bias[0:H, :], scale=split.unscale[0:H, :]).then_inc(s_kept, 1)
            act.wait_ge(shifts, 1)
            nc.scalar.activation(small["ed"], small["tmp"], ACT.Exp).then_inc(exps, 1)
            nc.scalar.activation(small["eg"], small["tmp"], ACT.Exp, scale=0.2).then_inc(exps, 1)
            nc.scalar.activation(small["es"], small["es"], ACT.Exp).then_inc(exps, 1)
            nc.scalar.activation(small["et"], small["et"], ACT.Exp).then_inc(exps, 1)
            act.wait_ge(prep, 2)
            act.wait_ge(exps, 4)
            nc.scalar.activation(small["u"], small["u"], ACT.Copy).then_inc(evacuated, 1)

            def high(n, u):
                act.wait_ge(f_made, 4 * n + 4)
                f, g = fbuf[:, u, :, 0, :], fbuf[:, u, :, 1, :]
                nc.scalar.activation(fg[:, u, :, 0, 0, :], f, ACT.Copy)
                nc.scalar.activation(fg[:, u, :, 1, 0, :], g, ACT.Copy, scale=-1.0)
                nc.scalar.activation(fg[:, u, :, 2, 0, :], g, ACT.Copy).then_inc(hi_made, 1)

            def evacuate(n):
                act.wait_ge(fg_used, n + 1)
                if n:
                    act.wait_ge(merged, 3 * n - 2)
                for b in range(6):
                    k = 3 if b < 5 else 1
                    nc.scalar.activation(sums[:, 3 * b:3 * b + k, :, :, :].rearrange("p t g a v -> p (t g a v)"),
                                         c.psum[:, b, 0:4 * V * k], ACT.Copy).then_inc(evacuated, 1)

            for n in range(H):
                if n >= 2:
                    act.wait_ge(fg_used, n - 1)
                high(n, n % 2)
                if n:
                    evacuate(n - 1)
            evacuate(H - 1)
            act.wait_ge(tail, NT + 6)
            e2 = e_all.rearrange("p t h v -> p (t h v)")
            nc.scalar.activation(e2, e2, ACT.Exp).then_inc(exps, 1)


def neighbour_sums(nc, c, pe, values, moving, banks, chunk, tiles, signal):
    for b, bank in enumerate(banks):
        for j in tiles:
            for part in range(2):
                k = part * FT + b % FT
                mm = nc.tensor.matmul(c.psum[:, bank, :], values[:, j, k * P:(k + 1) * P],
                                      moving[b // FT][:, j, chunk * CH:(chunk + 1) * CH],
                                      start=(j == 0 and part == 0), stop=(j == NT - 1 and part == 1))
        if tiles[-1] == NT - 1:
            mm.then_inc(signal, 1)


def mean_layer(c, S):
    nc, dram = c.nc, c.dram
    a_cols = c.view(AT_AT, [NT, N], F8)
    x = c.view(AT_X, [NT, D], F32)
    F, W = AT_FREE, AT_W
    nodes = NodeValues(c, "n1", F)
    mid = c.view(W, [2, FT, D], F32)
    comb = c.view(W + 4 * KB, [2 * FT, D], F32)
    v32 = c.view(W + 8 * KB, [4 * D], F32)
    vhi, vlo = c.view(W + 12 * KB, [4 * D], F16), c.view(W + 14 * KB, [4 * D], F16)
    vp = [v.rearrange("p (k n) -> p k n", n=D) for v in (vhi, vlo)]
    b_rep = c.view(W + 16 * KB, [4, P], F32)
    b_col = c.view(W + 18 * KB, [4], F32)
    bias = c.view(W + 18 * KB + 64, [D], F32)
    r_deg = c.view(W + 20 * KB, [NT], F32)
    sums = c.view(F + 18 * KB, [2, FT, 2, CH], F16)
    y = c.view(F + 26 * KB, [2, D], F32)
    split = Split(c, "w1", v32, vhi, vlo)
    sem = lambda n: c.sem("m_" + n)
    w_loaded, rep_made, v_made, v_kept, bias_made, bias_kept = (
        sem("w_loaded"), sem("rep_made"), sem("v_made"), sem("v_kept"), sem("bias_made"), sem("bias_kept"))
    deg_ready, summed, high, low = sem("deg_ready"), sem("summed"), sem("high"), sem("low")
    out_made, y_made, x_made, chain = sem("out_made"), sem("y_made"), sem("x_made"), sem("chain")

    with nc.Block() as block:
        @block.sync
        def _(sp):
            for m, name in enumerate(("L1_WsT", "L1_WnT")):
                sp.dma_start(mid[:, m], dram[name].rearrange("(t p) f -> p t f", p=P)).then_inc(w_loaded, 16)
            sp.dma_start(comb, dram["L1_Wc"].rearrange("(t p) f -> p t f", p=P)).then_inc(w_loaded, 16)
            for m, name in enumerate(("L1_bs", "L1_bn")):
                sp.dma_start(b_col[:, FT * m:FT * (m + 1)], dram[name]).then_inc(w_loaded, 16)
            sp.dma_start(bias, dram["L1_bc"].partition_broadcast(P)).then_inc(w_loaded, 16)

        @block.tensor
        def _(pe):
            pe.wait_ge(w_loaded, 96)
            for m in range(2):
                for k in range(FT):
                    for o in range(FT):
                        mm = nc.tensor.matmul(c.psum[:, m, k * D:(k + 1) * D], mid[:, m, o, k * P:(k + 1) * P],
                                              comb[:, FT * m + o, :], start=(o == 0), stop=(o == FT - 1))
            mm.then_inc(v_made, 1)
            pe.wait_ge(rep_made, 4)
            for k in range(4):
                mm = nc.tensor.matmul(c.psum[:, 2, 0:D], b_rep[:, k, :], comb[:, k, :], start=(k == 0), stop=(k == 3))
            mm.then_inc(bias_made, 1)
            nodes.tensor(pe)
            pe.wait_ge(v_kept, 1)
            pe.wait_ge(bias_kept, 1)
            split.ready(pe)
            pe.wait_ge(nodes.kept, NT)

            def sums_of(j):
                banks = [2 * (j % 2), 2 * (j % 2) + 1]
                if j >= 2:
                    pe.wait_ge(low, 2 * (j - 1))
                neighbour_sums(nc, c, pe, nodes.sp, [a_cols], banks, j, list(range(NT)), summed)

            def outputs(j):
                pe.wait_ge(high, 2 * (j + 1))
                pe.wait_ge(low, 2 * (j + 1))
                for q in range(CH // P):
                    t = j * (CH // P) + q
                    if t >= 2:
                        pe.wait_ge(x_made, t - 1)
                    for m in range(2):
                        n = 0
                        for k in range(FT):
                            for a, b in PARTS3:
                                st = (nodes.st[:, 2 * a + k, t * P:(t + 1) * P] if m == 0 else
                                      sums[:, j % 2, k, a, q * P:(q + 1) * P])
                                mm = nc.tensor.matmul(c.psum[:, 4 + t % 2, m * D:(m + 1) * D], st, vp[b][:, FT * m + k, :],
                                                      start=(n == 0), stop=(n == 5))
                                n += 1
                    mm.then_inc(out_made, 1)

            sums_of(0)
            for j in range(NC):
                if j + 1 < NC:
                    sums_of(j + 1)
                outputs(j)

        @block.vector
        def _(dve):
            link = Chain(dve, chain)
            dve.wait_ge(w_loaded, 96)
            for k in range(4):
                nc.vector.tensor_copy(b_rep[:, k, :], b_col[:, k:k + 1].broadcast_to([P, P])).then_inc(rep_made, 1)
            dve.wait_ge(v_made, 1)
            nc.vector.tensor_copy(v32, c.psum[:, 0:2, :].rearrange("p b n -> p (b n)")).then_inc(v_kept, 1)
            dve.wait_ge(v_kept, 1)
            split.vector(dve)
            dve.wait_ge(bias_made, 1)
            nc.vector.tensor_tensor(bias, c.psum[:, 2, 0:D], bias, ALU.add).then_inc(bias_kept, 1)
            link(nc.vector.tensor_scalar(r_deg, S.degree[:, :], 1.0, None, ALU.max))
            link(nc.vector.reciprocal(r_deg, r_deg))
            nc.vector.tensor_scalar(r_deg, r_deg, split.plain, None, ALU.mult).then_inc(deg_ready, 1)
            dve.wait_ge(bias_kept, 1)
            dve.wait_ge(deg_ready, 1)
            nodes.vector(dve)

            def low_parts(j):
                for b in range(FT):
                    dve.wait_ge(high, 2 * j + b + 1)
                    nc.vector.scalar_tensor_tensor(sums[:, j % 2, b, 1, :], c.psum[:, 2 * (j % 2) + b, :], 1.0 / STATE_SCALE,
                                                   sums[:, j % 2, b, 0, :], ALU.mult, ALU.subtract).then_inc(low, 1)

            low_parts(0)
            for j in range(NC):
                if j + 1 < NC:
                    low_parts(j + 1)
                for q in range(CH // P):
                    t = j * (CH // P) + q
                    dve.wait_ge(out_made, t + 1)
                    if t >= 2:
                        dve.wait_ge(x_made, t - 1)
                    nc.vector.scalar_tensor_tensor(y[:, t % 2, :], c.psum[:, 4 + t % 2, 0:D], split.unscale, bias,
                                                   ALU.mult, ALU.add).then_inc(y_made, 1)
                    dve.wait_ge(y_made, 2 * t + 1)
                    nc.vector.scalar_tensor_tensor(y[:, t % 2, :], c.psum[:, 4 + t % 2, D:2 * D], r_deg[:, t:t + 1],
                                                   y[:, t % 2, :], ALU.mult, ALU.add).then_inc(y_made, 1)
                    dve.wait_ge(y_made, 2 * t + 2)
                    nc.vector.scalar_tensor_tensor(x[:, t, :], y[:, t % 2, :], 0.0, x[:, t, :], ALU.max,
                                                   ALU.add).then_inc(x_made, 1)

        @block.gpsimd
        def _(pool):
            split.gpsimd(pool)

        @block.scalar
        def _(act):
            split.scalar(act)
            nodes.scalar(act)
            for j in range(NC):
                for b in range(FT):
                    act.wait_ge(summed, 2 * j + b + 1)
                    if j >= 2:
                        act.wait_ge(out_made, (CH // P) * (j - 1))
                    nc.scalar.activation(sums[:, j % 2, b, 0, :], c.psum[:, 2 * (j % 2) + b, :], ACT.Copy,
                                         scale=1.0 / STATE_SCALE).then_inc(high, 1)


def gated_layer(c, S):
    nc, dram = c.nc, c.dram
    G3 = 3 * D
    GT = G3 // P
    KT = 3 * FT
    TOP = 16384.0
    a_rows, a_cols = c.view(AT_A, [NT, N], F8), c.view(AT_AT, [NT, N], F8)
    x = c.view(AT_X, [NT, D], F32)
    F, W = AT_FREE, AT_W
    NM = (KT + 1) * G3
    m_hi, m_lo = c.view(W, [NM], F16), c.view(W + 10752, [NM], F16)
    mp = [v.rearrange("p (k n) -> p k n", n=G3) for v in (m_hi, m_lo)]
    o_hi, o_lo = c.view(W + 21504, [2 * FT * D], F16), c.view(W + 23552, [2 * FT * D], F16)
    op = [v.rearrange("p (k n) -> p k n", n=D) for v in (o_hi, o_lo)]
    uv = c.view(W + 25600, [G3], F16)
    g_bias = c.view(W + 27136, [GT], F32)
    h_bias = c.view(W + 27168, [GT], F32)
    o1_bias = c.view(W + 27200, [FT], F32)
    io_col = c.view(W + 27216, [2 * FT], F32)
    m32 = c.view(F, [NM], F32)
    m32t = m32.rearrange("p (k n) -> p k n", n=G3)
    wg = c.view(F + 21 * KB, [KT, G3], F32)
    io = c.view(F + 39 * KB, [2, FT, D], F32)
    o32 = c.view(F + 43 * KB, [2 * FT * D], F32)
    io_b = c.view(F + 47 * KB, [2 * FT, 34], F32)
    pattern = c.view(F + 48 * KB, [2, 34], F16)
    deg_rows = c.view(F + 60 * KB, [N], F16)
    nodes = NodeValues(c, "n2", F + 21 * KB)
    st, sp_ = nodes.st, nodes.sp
    X = c.view(F, [2, 2, FT, 2, CH], F16)
    rs = c.view(F + 16 * KB, [FT, 2, CH], F16)
    s32 = c.view(F + 20 * KB, [FT, CH], F32)
    tr, tz, th, p32 = (c.view(F + (24 + 4 * k) * KB, [FT, CH], F32) for k in range(4))
    t32, tp = c.view(F + 24 * KB, [FT, CH], F32), c.view(F + 28 * KB, [FT, 2, CH], F16)
    o2_bias = c.view(F + 48 * KB + 256, [D], F32)
    y = c.view(F + 50 * KB, [2, D], F32)

    split = Split(c, "w2", m32, m_hi, m_lo, TOP)
    osplit = Split(c, "w3", o32, o_hi, o_lo)
    sem = lambda n: c.sem("r_" + n)
    w_loaded, io_zero, io_made, pattern_made = sem("w_loaded"), sem("io_zero"), sem("io_made"), sem("pattern")
    m_made, m_kept, uv_made, uv_kept, uv_zero, uv_set = (sem("m_made"), sem("m_kept"), sem("uv_made"), sem("uv_kept"),
                                                         sem("uv_zero"), sem("uv_set"))
    deg_made, deg_kept = sem("deg_made"), sem("deg_kept")
    biases, steps_pe = sem("biases"), sem("steps_pe")
    summed, x_high, x_low = sem("summed"), sem("x_high"), sem("x_low")
    gate_done, gate_read = sem("gate_done"), sem("gate_read")
    s_made, p_made, rs_high, rs_low, d_made, e_made, new_made, st_high, st_low = (
        sem(n) for n in ("s_made", "p_made", "rs_high", "rs_low", "d_made", "e_made", "new_made", "st_high", "st_low"))
    turned, sp_kept = sem("turned"), sem("sp_kept")
    o_made, t_made, t_high, t_low, y_summed, y_made, x_made = (
        sem(n) for n in ("o_made", "t_made", "t_high", "t_low", "y_summed", "y_made", "x_made"))
    CB, GB, TB = 2 * FT, 4, 7

    with nc.Block() as block:
        @block.sync
        def _(sp):
            for m, name in enumerate(("L2_in_W", "L2_out_W")):
                sp.dma_start(io[:, m], dram[name].rearrange("(t p) f -> p t f", p=P)).then_inc(w_loaded, 16)
            sp.dma_start(wg, dram["L2_WgT"].rearrange("(t p) n -> p t n", p=P)).then_inc(w_loaded, 16)
            for m, name in enumerate(("L2_o1T", "L2_o2T")):
                sp.dma_start(o32.rearrange("p (m t f) -> p m t f", m=2, f=D)[:, m],
                             dram[name].rearrange("(t p) f -> p t f", p=P)).then_inc(w_loaded, 16)
            sp.dma_start(g_bias, dram["L2_gbcol"]).then_inc(w_loaded, 16)
            sp.dma_start(o1_bias, dram["L2_o1bcol"]).then_inc(w_loaded, 16)
            sp.dma_start(io_col, dram["L2_iobcol"]).then_inc(w_loaded, 16)
            sp.dma_start(o2_bias, dram["L2_o2b"].partition_broadcast(P)).then_inc(w_loaded, 16)

        @block.tensor
        def _(pe):
            pe.wait_ge(w_loaded, 144)
            n = 0
            for m in range(2):
                for k in range(FT):
                    for g in range(3):
                        if n >= 6:
                            pe.wait_ge(m_kept, n - 5)
                        for o in range(FT):
                            mm = nc.tensor.matmul(c.psum[:, n % 6, 0:D], io[:, m, o, k * P:(k + 1) * P],
                                                  wg[:, FT * m + o, g * D:(g + 1) * D], start=(o == 0), stop=(o == FT - 1))
                        mm.then_inc(m_made, 1)
                        n += 1
            pe.wait_ge(io_made, 8)
            pe.wait_ge(m_kept, 12)
            for g in range(3):
                for k in range(2 * FT):
                    mm = nc.tensor.matmul(c.psum[0:34, g, 0:D], io_b[:, k, :], wg[:, k, g * D:(g + 1) * D],
                                          start=(k == 0), stop=(k == 2 * FT - 1))
            mm.then_inc(uv_made, 1)
            nodes.tensor(pe)
            pe.wait_ge(pattern_made, 3)
            pe.wait_ge(uv_kept, 1)
            for j in range(NC):
                if j >= 4:
                    pe.wait_ge(deg_kept, j - 3)
                for m, adj in enumerate((a_cols, a_rows)):
                    for t in range(NT):
                        mm = nc.tensor.matmul(c.psum[0:34, j, :], pattern[:, m, :], adj[:, t, j * CH:(j + 1) * CH],
                                              start=(m == 0 and t == 0), stop=(m == 1 and t == NT - 1))
                mm.then_inc(deg_made, 1)
            split.ready(pe)
            osplit.ready(pe)
            pe.wait_ge(uv_set, 2)
            pe.wait_ge(nodes.kept, NT)
            pe.wait_ge(deg_kept, NC)

            def passes(sem, value):
                pe.wait_ge(sem, value)
                pe.sem_inc(steps_pe)

            def sums_of(j, tiles):
                neighbour_sums(nc, c, pe, sp_, [a_cols, a_rows], range(CB), j, tiles, summed)

            def gates(s, j):
                passes(x_low, CB * (NC * s + j + 1))
                passes(x_high, CB * (NC * s + j + 1))

                def factor(g, kinds, first, last):
                    bank, n = c.psum[:, GB + g % 3, :], 0
                    total = 3 * len(kinds) + (1 if 0 in kinds else 0)
                    if 0 in kinds:
                        nc.tensor.matmul(bank, uv[0:34, g * P:(g + 1) * P], deg_rows[0:34, j * CH:(j + 1) * CH],
                                         start=first, stop=False)
                        n = 1
                    for k in kinds:
                        for a, b in PARTS3:
                            if k < 2 * FT:
                                mov = X[:, j % 2, k // FT, k % FT, a, :]
                            elif g < 4:
                                mov = st[:, 2 * a + k % FT, j * CH:(j + 1) * CH]
                            else:
                                mov = rs[:, k % FT, a, :]
                            n += 1
                            mm = nc.tensor.matmul(bank, mp[b][:, k, g * P:(g + 1) * P], mov, start=False,
                                                  stop=(last and n == total))
                    return mm

                for g in range(GT):
                    passes(gate_read, GT * (NC * s + j) + g + 1)
                    if g < 4:
                        factor(g, list(range(KT)), True, True).then_inc(gate_done, 1)
                    else:
                        factor(g, list(range(2 * FT)), True, False)
                passes(rs_low, FT * (NC * s + j + 1))
                passes(rs_high, FT * (NC * s + j + 1))
                for g in range(4, GT):
                    factor(g, [2 * FT, 2 * FT + 1], False, True).then_inc(gate_done, 1)

            def turn(s, j):
                passes(st_low, FT * (NC * s + j + 1) + 1)
                passes(st_high, FT * (NC * s + j + 1))
                for half in range(2):
                    passes(sp_kept, 2 * (NC * s + j) + half + 1)
                    for q in range(2):
                        t = j * (CH // P) + 2 * half + q
                        for k in range(4):
                            mm = nc.tensor.transpose(c.bank16(TB)[:, (4 * q + k) * P:(4 * q + k + 1) * P],
                                                     st[:, k, t * P:(t + 1) * P], c.ident[:, :])
                    mm.then_inc(turned, 1)

            def next_sums(s, j):
                for b in range(1):
                    passes(x_low, CB * (NC * s + j))
                sums_of(j, list(range(NT)))

            def step(s, more):
                for j in range(NC):
                    if j + 1 < NC:
                        next_sums(s, j + 1)
                    if j == NC - 1:
                        turn(s, 0)
                        turn(s, 1)
                    gates(s, j)
                if more:
                    turn(s, 2)
                    passes(x_low, CB * NC * (s + 1))
                    passes(sp_kept, 2 * (NC * s + 3) + 1)
                    sums_of(0, list(range(0, 12)))
                    turn(s, 3)
                    passes(sp_kept, 2 * NC * (s + 1) + 1)
                    sums_of(0, list(range(12, NT)))

            sums_of(0, list(range(NT)))
            with pe.Fori(0, STEPS - 1) as s:
                step(s, True)
            step(STEPS - 1, False)

            for j in range(NC):
                pe.wait_ge(st_low, FT * (NC * (STEPS - 1) + j + 1) + 1)
                pe.wait_ge(st_high, FT * (NC * (STEPS - 1) + j + 1))
                for g in range(FT):
                    if j:
                        pe.wait_ge(t_made, FT * (j - 1) + g + 1)
                    n = 0
                    for k in range(FT):
                        for a, b in PARTS3:
                            mm = nc.tensor.matmul(c.psum[:, g, :], op[b][:, k, g * P:(g + 1) * P],
                                                  st[:, 2 * a + k, j * CH:(j + 1) * CH], start=(n == 0), stop=(n == 5))
                            n += 1
                    mm.then_inc(o_made, 1)
                pe.wait_ge(t_low, FT * (j + 1))
                pe.wait_ge(t_high, FT * (j + 1))
                for q in range(CH // P):
                    t = j * (CH // P) + q
                    if t >= 2:
                        pe.wait_ge(y_made, t - 1)
                    n = 0
                    for k in range(FT):
                        for a, b in PARTS3:
                            mm = nc.tensor.matmul(c.psum[:, 2 + t % 2, 0:D], tp[:, k, a, q * P:(q + 1) * P],
                                                  op[b][:, FT + k, :], start=(n == 0), stop=(n == 5))
                            n += 1
                    mm.then_inc(y_summed, 1)

        @block.vector
        def _(dve):
            nc.vector.memset(io_b, 0.0).then_inc(io_zero, 1)
            nc.vector.memset(pattern, 0.0).then_inc(pattern_made, 1)
            nc.vector.memset(m32t[:, KT, :], 0.0).then_inc(uv_zero, 1)
            dve.wait_ge(io_zero, 1)
            dve.wait_ge(w_loaded, 144)
            for m in range(2):
                for k in range(FT):
                    for at in (0, 32):
                        nc.vector.tensor_copy(io_b[:, FT * m + k, at + m:at + m + 1],
                                              io_col[:, FT * m + k:FT * m + k + 1]).then_inc(io_made, 1)
            dve.wait_ge(pattern_made, 1)
            for m in range(2):
                nc.vector.memset(pattern[:, m, m:m + 33:32], 1.0).then_inc(pattern_made, 1)
            nc.vector.tensor_scalar(h_bias, g_bias, 0.5, None, ALU.mult).then_inc(biases, 1)
            nc.vector.tensor_scalar(m32t[:, 2 * FT:KT, :], wg[:, 2 * FT:KT, :], 1.0 / STATE_SCALE, None,
                                    ALU.mult).then_inc(uv_zero, 1)
            n = 0
            for m in range(2):
                for k in range(FT):
                    for g in range(3):
                        dve.wait_ge(m_made, n + 1)
                        nc.vector.tensor_copy(m32t[:, FT * m + k, g * D:(g + 1) * D], c.psum[:, n % 6, 0:D]
                                              ).then_inc(m_kept, 1)
                        n += 1
            dve.wait_ge(uv_made, 1)
            dve.wait_ge(uv_zero, 2)
            nc.vector.tensor_copy(m32t[0:34, KT, :].rearrange("p (g n) -> p g n", n=D), c.psum[0:34, 0:3, 0:D]
                                  ).then_inc(uv_kept, 1)
            dve.wait_ge(uv_kept, 1)
            dve.wait_ge(m_kept, 12)
            split.vector(dve)
            dve.wait_ge(split.low, 1)
            nc.vector.tensor_copy(uv[0:32, :], mp[0][0:32, KT, :]).then_inc(uv_set, 1)
            nc.vector.tensor_copy(uv[32:64, :], mp[1][32:64, KT, :]).then_inc(uv_set, 1)
            osplit.vector(dve)
            nodes.vector(dve)
            for j in range(NC):
                dve.wait_ge(deg_made, j + 1)
                nc.vector.tensor_copy(deg_rows[0:34, j * CH:(j + 1) * CH], c.psum[0:34, j, :]).then_inc(deg_kept, 1)

            def low_parts(s, j):
                for b in range(CB):
                    dve.wait_ge(x_high, CB * (NC * s + j) + b + 1)
                    nc.vector.scalar_tensor_tensor(X[:, j % 2, b // FT, b % FT, 1, :], c.psum[:, b, :], 1.0 / STATE_SCALE,
                                                   X[:, j % 2, b // FT, b % FT, 0, :], ALU.mult, ALU.subtract
                                                   ).then_inc(x_low, 1)

            def update(s, j):
                at = FT * (NC * s + j)
                dve.wait_ge(st_low, at + 1)
                for k in range(FT):
                    nc.vector.tensor_tensor(s32[:, k, :], st[:, k, j * CH:(j + 1) * CH],
                                            st[:, FT + k, j * CH:(j + 1) * CH], ALU.add).then_inc(s_made, 1)
                for k in range(FT):
                    dve.wait_ge(gate_read, GT * (NC * s + j) + k + 4)
                    dve.wait_ge(s_made, at + k + 1)
                    nc.vector.scalar_tensor_tensor(p32[:, k, :], tr[:, k, :], 1.0, s32[:, k, :], ALU.add, ALU.mult
                                                   ).then_inc(p_made, 1)
                for k in range(FT):
                    dve.wait_ge(rs_high, at + k + 1)
                    nc.vector.scalar_tensor_tensor(rs[:, k, 1, :], p32[:, k, :], 0.5, rs[:, k, 0, :], ALU.mult,
                                                   ALU.subtract).then_inc(rs_low, 1)
                for k in range(FT):
                    dve.wait_ge(gate_read, GT * (NC * s + j) + k + 8)
                    nc.vector.scalar_tensor_tensor(th[:, k, :], th[:, k, :], STATE_SCALE, s32[:, k, :], ALU.mult,
                                                   ALU.subtract).then_inc(d_made, 1)
                    dve.wait_ge(d_made, at + k + 1)
                    nc.vector.scalar_tensor_tensor(tz[:, k, :], tz[:, k, :], 1.0, th[:, k, :], ALU.add, ALU.mult
                                                   ).then_inc(e_made, 1)
                    dve.wait_ge(e_made, at + k + 1)
                    nc.vector.scalar_tensor_tensor(s32[:, k, :], tz[:, k, :], 0.5, s32[:, k, :], ALU.mult, ALU.add
                                                   ).then_inc(new_made, 1)
                for k in range(FT):
                    dve.wait_ge(st_high, at + k + 1)
                    nc.vector.tensor_tensor(st[:, FT + k, j * CH:(j + 1) * CH], s32[:, k, :],
                                            st[:, k, j * CH:(j + 1) * CH], ALU.subtract).then_inc(st_low, 1)

            def step(s, more):
                for j in range(NC):
                    if j + 1 < NC:
                        low_parts(s, j + 1)
                    update(s, j)
                if more:
                    low_parts(s + 1, 0)

            dve.sem_inc(st_low, 1)
            low_parts(0, 0)
            with dve.Fori(0, STEPS - 1) as s:
                step(s, True)
            step(STEPS - 1, False)

            for j in range(NC):
                for g in range(FT):
                    dve.wait_ge(t_high, FT * j + g + 1)
                    nc.vector.scalar_tensor_tensor(tp[:, g, 1, :], t32[:, g, :], STATE_SCALE, tp[:, g, 0, :], ALU.mult,
                                                   ALU.subtract).then_inc(t_low, 1)
                for q in range(CH // P):
                    t = j * (CH // P) + q
                    dve.wait_ge(y_summed, t + 1)
                    if t >= 2:
                        dve.wait_ge(x_made, t - 1)
                    nc.vector.scalar_tensor_tensor(y[:, t % 2, :], c.psum[:, 2 + t % 2, 0:D], osplit.unscale, o2_bias,
                                                   ALU.mult, ALU.add).then_inc(y_made, 1)
                    dve.wait_ge(y_made, t + 1)
                    nc.vector.tensor_tensor(x[:, t, :], y[:, t % 2, :], x[:, t, :], ALU.add).then_inc(x_made, 1)

        @block.gpsimd
        def _(pool):
            split.gpsimd(pool)
            osplit.gpsimd(pool)

        @block.scalar
        def _(act):
            split.scalar(act)
            osplit.scalar(act)
            nodes.scalar(act)
            act.wait_ge(biases, 1)
            act.wait_ge(split.scaled, 1)
            act.sem_inc(gate_read, 3)
            act.sem_inc(sp_kept, 1)

            def high_parts(s, j):
                for b in range(CB):
                    act.wait_ge(summed, CB * (NC * s + j) + b + 1)
                    nc.scalar.activation(X[:, j % 2, b // FT, b % FT, 0, :], c.psum[:, b, :], ACT.Copy,
                                         scale=1.0 / STATE_SCALE).then_inc(x_high, 1)

            def update(s, j):
                at = FT * (NC * s + j)

                def gate(g, out, bias, scale):
                    act.wait_ge(gate_done, GT * (NC * s + j) + g + 1)
                    nc.scalar.activation(out[:, g % FT, :], c.psum[:, GB + g % 3, :], ACT.Tanh, bias=bias[:, g:g + 1],
                                         scale=scale).then_inc(gate_read, 1)

                for g in range(FT):
                    gate(g, tr, h_bias, split.half)
                for k in range(FT):
                    act.wait_ge(p_made, at + k + 1)
                    nc.scalar.activation(rs[:, k, 0, :], p32[:, k, :], ACT.Copy, scale=0.5).then_inc(rs_high, 1)
                for g in range(FT, 2 * FT):
                    gate(g, tz, h_bias, split.half)
                for g in range(2 * FT, 3 * FT):
                    gate(g, th, g_bias, split.plain)
                for k in range(FT):
                    act.wait_ge(new_made, at + k + 1)
                    nc.scalar.activation(st[:, k, j * CH:(j + 1) * CH], s32[:, k, :], ACT.Copy).then_inc(st_high, 1)

            def keep(s, j):
                for half in range(2):
                    act.wait_ge(turned, 2 * (NC * s + j) + half + 1)
                    t = j * (CH // P) + 2 * half
                    nc.scalar.activation(sp_[:, t:t + 2, :].rearrange("p t n -> p (t n)"), c.bank16(TB),
                                         ACT.Copy).then_inc(sp_kept, 1)

            def step(s, more):
                for j in range(NC):
                    if j + 1 < NC:
                        high_parts(s, j + 1)
                    if j == NC - 1:
                        keep(s, 0)
                        keep(s, 1)
                    update(s, j)
                if more:
                    keep(s, 2)
                    keep(s, 3)
                    high_parts(s + 1, 0)

            high_parts(0, 0)
            with act.Fori(0, STEPS - 1) as s:
                step(s, True)
            step(STEPS - 1, False)

            for j in range(NC):
                if j:
                    act.wait_ge(y_summed, (CH // P) * j)
                for g in range(FT):
                    act.wait_ge(o_made, FT * j + g + 1)
                    nc.scalar.activation(t32[:, g, :], c.psum[:, g, :], ACT.Tanh, bias=o1_bias[:, g:g + 1],
                                         scale=osplit.unscale).then_inc(t_made, 1)
                for g in range(FT):
                    act.wait_ge(t_made, FT * j + g + 1)
                    nc.scalar.activation(tp[:, g, 0, :], t32[:, g, :], ACT.Copy, scale=STATE_SCALE).then_inc(t_high, 1)


def hard_attention_layer(c, S):
    nc, dram = c.nc, c.dram
    SCALING = HD ** -0.5
    DOWN = 2.0 ** -17
    x = c.view(AT_X, [NT, D], F32)
    a_rows = c.view(AT_A, [NT, N], F8)
    F, W = AT_FREE, AT_W
    ks = c.view(AT_AT, [H, N], F16)
    qs = c.view(F, [H, N], F16)
    values = c.view(AT_SP, [NT, H, 2, HD], F16)
    w32 = c.view(W, [3 * FT * D + 1], F32)
    w_hi, w_lo = c.view(W + 7 * KB, [3 * FT * D + 1], F16), c.view(W + 11 * KB, [3 * FT * D + 1], F16)
    wp = [v[:, 0:3 * FT * D].rearrange("p (m k n) -> p m k n", m=3, k=FT) for v in (w_hi, w_lo)]
    wide = c.view(W + 15 * KB, [2, 2, FT, P], F16)
    temp = c.view(W + 17 * KB, [2, CH], F32)
    scal = c.view(W + 27 * KB, [16], F32)
    k_bias, back, bias, be, sq = (scal[:, k:k + 1] for k in range(5))
    best = c.view(W + 27 * KB + 64, [2, 4], F32)
    hard = c.view(AT_ST, [2, N], F16)
    hard_t = c.view(AT_ST + 8 * KB, [2, NT, P], F16)
    scores = c.view(F + 32 * KB, [2, N], F32)
    mask = c.view(F + 48 * KB, [2, N], F32)
    y = c.view(W + 22 * KB, [2, D], F32)

    nodes = NodeValues(c, "n3", F + 32 * KB)
    split = Split(c, "w4", w32, w_hi, w_lo)
    sem = lambda n: c.sem("h_" + n)
    w_loaded, wide_made, wide_used = sem("w_loaded"), sem("wide_made"), sem("wide_used")
    proj, proj_read = sem("proj"), sem("proj_read")
    q_high, q_low, k_full, k_high, k_low = sem("q_high"), sem("q_low"), sem("k_full"), sem("k_high"), sem("k_low")
    v_sum, v_high, v_low = sem("v_sum"), sem("v_high"), sem("v_low")
    consts, masked, mask_ready = sem("consts"), sem("masked"), sem("mask_ready")
    scored, maxed, combined, marked, turned, turned_kept, taken = (
        sem(n) for n in ("scored", "maxed", "combined", "marked", "turned", "turned_kept", "taken"))
    y_half, y_made, stored = sem("y_half"), sem("y_made"), [sem("stored0"), sem("stored1")]
    chain, waited = sem("chain"), sem("waited")
    HALF = N // 2

    with nc.Block() as block:
        @block.sync
        def _(sp):
            for m, name in enumerate(("L3_WQT", "L3_WKT", "L3_WVT")):
                sp.dma_start(w32[:, m * FT * D:(m + 1) * FT * D].rearrange("p (t f) -> p t f", f=D),
                             dram[name].rearrange("(t p) f -> p t f", p=P)).then_inc(w_loaded, 16)
            for g in range(4):
                sp.dma_start(w32[HD * g:HD * (g + 1), 3 * FT * D:3 * FT * D + 1], dram["L3_we"]).then_inc(w_loaded, 16)
            sp.dma_start(be, dram["L3_be"].partition_broadcast(P)).then_inc(w_loaded, 16)
            with sp.Fori(0, NT // 2) as i:
                for u in range(2):
                    sp.wait_ge(y_made, 2 * i + u + 1)
                    sp.dma_start(c.out.rearrange("(t p) f -> t p f", p=P)[bass.ds(2 * i + u, 1), :, :]
                                 .rearrange("a p f -> (a p) f"), y[:, u, :]).then_inc(stored[u], 16)
            for u in range(2):
                sp.wait_ge(stored[u], 16 * NT // 2)

        @block.tensor
        def _(pe):
            nodes.tensor(pe)
            split.ready(pe)
            pe.wait_ge(nodes.kept, NT)
            for t in range(NT):
                if t >= 2:
                    pe.wait_ge(v_low, t - 1)
                n = 0
                for k in range(FT):
                    for a, b in PARTS3:
                        mm = nc.tensor.matmul(c.psum[:, 4 + t % 2, 0:D], nodes.st[:, 2 * a + k, t * P:(t + 1) * P],
                                              wp[b][:, 2, k, :], start=(n == 0), stop=(n == 5))
                        n += 1
                mm.then_inc(v_sum, 1)
            for r in range(2 * H):
                pe.wait_ge(wide_made, 2 * r + 2)
                for j in range(NC):
                    n = NC * r + j
                    if n >= 4:
                        g, rest = divmod(n - 4, 2 * NC)
                        if rest < NC:
                            pe.wait_ge(q_low, NC * g + rest + 1)
                        else:
                            pe.wait_ge(k_full, NC * g + rest - NC + 1)
                    m = 0
                    for k in range(FT):
                        for a, b in PARTS3:
                            mm = nc.tensor.matmul(c.psum[:, n % 4, :], wide[:, r % 2, b, k, :],
                                                  nodes.st[:, 2 * a + k, j * CH:(j + 1) * CH], start=(m == 0), stop=(m == 5))
                            m += 1
                    mm.then_inc(proj, 1)
            pe.wait_ge(q_low, NC * H)
            pe.wait_ge(k_low, 2 * NC * H)
            pe.wait_ge(k_high, NC * H)
            pe.wait_ge(v_low, NT)
            pe.wait_ge(v_high, NT)

            def score(i, k):
                n = 16 * i + k
                for half in range(2):
                    if not (isinstance(i, int) and n == 0):
                        pe.wait_ge(maxed, 2 * (n - 1) + half + 1)
                    for q in range(2):
                        col = HALF * half + CH * q
                        mm = nc.tensor.matmul(c.psum[:, 2 * half + q, :],
                                              qs[:, k % H, bass.ds((2 * i + k // H) * P, P)],
                                              ks[:, k % H, col:col + CH], start=True, stop=True)
                    mm.then_inc(scored, 1)

            def take(i, k):
                n = 16 * i + k
                h, u = k % H, (k // H) % 2
                pe.wait_ge(turned_kept, 2 * n + 2)
                if h == 0 and not (isinstance(i, int) and n < 16):
                    pe.wait_ge(y_made, 2 * i + k // H - 1)
                for t in range(NT):
                    mm = nc.tensor.matmul(c.psum[:, 6 + u, 2 * HD * h:2 * HD * (h + 1)], hard_t[:, k % 2, t, :],
                                          values[:, t, h, :, :].rearrange("p a d -> p (a d)"),
                                          start=(t == 0), stop=(t == NT - 1))
                mm.then_inc(taken, 1)

            def turn(i, k):
                n = 16 * i + k
                pe.wait_ge(marked, n + 1)
                for half in range(2):
                    if not (isinstance(i, int) and n == 0):
                        pe.wait_ge(turned_kept, 2 * (n - 1) + half + 1)
                    for t in range(8):
                        mm = nc.tensor.transpose(c.bank16(4 + half)[:, t * P:(t + 1) * P],
                                                 hard[:, k % 2, (8 * half + t) * P:(8 * half + t + 1) * P], c.ident[:, :])
                    mm.then_inc(turned, 1)

            def units(i):
                for k in range(16):
                    first = isinstance(i, int)
                    score(i, k)
                    if not (first and k < 2):
                        take(i, k - 2)
                    if not (first and k < 1):
                        turn(i, k - 1)

            units(0)
            with pe.Fori(1, NT // 2) as i:
                units(i)
            last = NT // 2 - 1
            take(last, 14)
            turn(last, 15)
            take(last, 15)

        @block.vector
        def _(dve):
            link = Chain(dve, chain)
            dve.wait_ge(w_loaded, 16 * 8)
            split.vector(dve)
            link(nc.vector.tensor_scalar(k_bias, w32[:, 3 * FT * D:3 * FT * D + 1], split.scale, STATE_SCALE * DOWN,
                                         ALU.mult, ALU.mult))
            link(nc.vector.tensor_scalar(back, split.plain, 1.0 / (H * STATE_SCALE * DOWN), None, ALU.mult))
            link(nc.vector.tensor_scalar(sq, split.scale, STATE_SCALE * DOWN, None, ALU.mult))
            link(nc.vector.tensor_scalar(bias, be, sq, sq, ALU.mult, ALU.mult))
            dve.sem_inc(consts, 1)
            nodes.vector(dve)
            dve.wait_ge(split.low, 1)

            def widen(r):
                if r >= 2:
                    dve.wait_ge(proj, NC * (r - 1))
                for b in range(2):
                    nc.vector.tensor_copy(wide[:, r % 2, b].rearrange("p k (g d) -> p k g d", g=4),
                                          wp[b][:, r % 2, :, HD * (r // 2):HD * (r // 2 + 1)].unsqueeze(2)
                                          .broadcast_to([P, FT, 4, HD])).then_inc(wide_made, 1)

            widen(0)
            widen(1)
            for t in range(NT):
                dve.wait_ge(v_high, t + 1)
                nc.vector.scalar_tensor_tensor(values[:, t, :, 1, :], c.psum[:, 4 + t % 2, 0:D].rearrange("p (h d) -> p h d", d=HD),
                                               DOWN, values[:, t, :, 0, :], ALU.mult, ALU.subtract).then_inc(v_low, 1)
            for r in range(2 * H):
                h = r // 2
                for j in range(NC):
                    if r % 2 == 0:
                        dve.wait_ge(q_high, NC * h + j + 1)
                        v = qs[2 * HD:P, h, j * CH:(j + 1) * CH]
                        nc.vector.scalar_tensor_tensor(v, c.psum[2 * HD:P, (NC * r + j) % 4, :], DOWN, v,
                                                       ALU.mult, ALU.subtract).then_inc(q_low, 1)
                    else:
                        dve.wait_ge(k_high, NC * h + j + 1)
                        for g in (1, 3):
                            v = ks[HD * g:HD * (g + 1), h, j * CH:(j + 1) * CH]
                            nc.vector.tensor_tensor(v, temp[HD * g:HD * (g + 1), j % 2, :], v, ALU.subtract).then_inc(k_low, 1)
                if r + 2 < 2 * H:
                    widen(r + 2)

            def unit(i, k):
                n = 16 * i + k
                first = isinstance(i, int) and i == 0
                if k % H == 0:
                    dve.wait_ge(mask_ready, 2 * i + k // H + 1)
                for half in range(2):
                    dve.wait_ge(scored, 2 * n + half + 1)
                    if not (first and k < 2):
                        dve.wait_ge(marked, n - 1)
                    dve.sem_inc(waited)
                    at = slice(HALF * half, HALF * (half + 1))
                    nc.vector.tensor_tensor_reduce(scores[:, k % 2, at],
                                                   c.psum[:, 2 * half:2 * half + 2, :].rearrange("p b n -> p (b n)"),
                                                   mask[:, (k // H) % 2, at], 1.0, -3e38, ALU.add, ALU.max,
                                                   best[:, k % 2, half:half + 1]).then_inc(maxed, 1)
                dve.wait_ge(maxed, 2 * n + 2)
                nc.vector.tensor_scalar(best[:, k % 2, 2:3], best[:, k % 2, 0:1], best[:, k % 2, 1:2], -BIG / 4,
                                        ALU.max, ALU.max).then_inc(combined, 1)
                dve.wait_ge(combined, n + 1)
                if not (first and k < 2):
                    dve.wait_ge(turned, 2 * (n - 1))
                nc.vector.tensor_scalar(hard[:, k % 2, :], scores[:, k % 2, :], best[:, k % 2, 2:3], None, ALU.is_equal
                                        ).then_inc(marked, 1)

            def finish(i, u, after_first):
                qt = 2 * i + u
                dve.wait_ge(taken, H * (qt + 1))
                if after_first:
                    dve.wait_ge(stored[u], 16 * i)
                o = c.psum[:, 6 + u, :].rearrange("p (h a d) -> p h a d", a=2, d=HD)
                yv = y[:, u, :].rearrange("p (h d) -> p h d", d=HD)
                xv = x[:, bass.ds(qt, 1), :].rearrange("p a (h d) -> p (a h) d", d=HD)
                nc.vector.scalar_tensor_tensor(yv, o[:, :, 0, :], back, xv, ALU.mult, ALU.add).then_inc(y_half, 1)
                dve.wait_ge(y_half, qt + 1)
                nc.vector.scalar_tensor_tensor(yv, o[:, :, 1, :], back, yv, ALU.mult, ALU.add).then_inc(y_made, 1)

            def units(i):
                for k in range(16):
                    unit(i, k)
                    if k == 11:
                        finish(i, 0, not isinstance(i, int))

            units(0)
            with dve.Fori(1, NT // 2) as i:
                for k in range(16):
                    unit(i, k)
                    if k == 3:
                        dve.wait_ge(stored[0], 16 * i)
                        finish(i - 1, 1, False)
                    if k == 11:
                        finish(i, 0, True)
            dve.wait_ge(stored[0], 16 * (NT // 2))
            finish(NT // 2 - 1, 1, True)

        @block.gpsimd
        def _(pool):
            split.gpsimd(pool)
            for h in range(H):
                for j in range(NC):
                    pool.wait_ge(k_full, NC * h + j + 1)
                    nc.gpsimd.tensor_copy(ks[:, h, j * CH:(j + 1) * CH], temp[:, j % 2, :]).then_inc(k_high, 1)
            pool.wait_ge(consts, 1)
            for t in range(NT):
                pool.wait_ge(masked, t + 1)
                nc.gpsimd.tensor_scalar(mask[:, t % 2, :], mask[:, t % 2, :], bias, None, ALU.min).then_inc(mask_ready, 1)

        @block.scalar
        def _(act):
            split.scalar(act)
            nodes.scalar(act)
            act.wait_ge(nodes.low, NT)
            for t in range(NT):
                act.wait_ge(v_sum, t + 1)
                nc.scalar.activation(values[:, t, :, 0, :], c.psum[:, 4 + t % 2, 0:D].rearrange("p (h d) -> p h d", d=HD),
                                     ACT.Copy, scale=DOWN).then_inc(v_high, 1)
            act.wait_ge(consts, 1)
            for r in range(2 * H):
                h = r // 2
                for j in range(NC):
                    act.wait_ge(proj, NC * r + j + 1)
                    src = c.psum[:, (NC * r + j) % 4, :]
                    if r % 2 == 0:
                        nc.scalar.activation(qs[:, h, j * CH:(j + 1) * CH], src, ACT.Copy, scale=DOWN).then_inc(q_high, 1)
                    else:
                        n = NC * h + j
                        if n >= 2:
                            act.wait_ge(k_low, 2 * (n - 1))
                            act.wait_ge(k_high, n - 1)
                        nc.scalar.activation(temp[:, j % 2, :], src, ACT.Identity, bias=k_bias,
                                             scale=SCALING * DOWN).then_inc(k_full, 1)

            def mask_rows(t):
                if t >= 2:
                    act.wait_ge(maxed, 2 * H * (t - 1))
                    act.wait_ge(mask_ready, t - 1)
                nc.scalar.activation(mask[:, t % 2, :], a_rows[:, t, :], ACT.Copy, scale=BIG, bias=-BIG / 2
                                     ).then_inc(masked, 1)

            mask_rows(0)
            mask_rows(1)
            for n in range(NT * H):
                for half in range(2):
                    act.wait_ge(turned, 2 * n + half + 1)
                    if n >= 2:
                        act.wait_ge(taken, n - 1)
                    nc.scalar.activation(hard_t[:, n % 2, 8 * half:8 * half + 8, :].rearrange("p t q -> p (t q)"),
                                         c.bank16(4 + half), ACT.Copy).then_inc(turned_kept, 1)
                if n % H == H - 1 and n // H + 2 < NT:
                    mask_rows(n // H + 2)


class Shared:
    pass
''

def graph_layers(nc, dram, out):
    with ExitStack() as ctx:
        c = Chip(nc, ctx, dram, out)
        S = Shared()
        S.degree = ctx.enter_context(nc.sbuf_tensor("degree", [P, NT], F32))
        layers = [load_phase, attention_layer, mean_layer, gated_layer, hard_attention_layer]
        for layer in layers:
            with ExitStack() as own:
                c.ctx, c.owned = own, []
                layer(c, S)
                if layer is not layers[-1]:
                    c.clear_semaphores()


def kernel(**inputs):
    import numpy as _np
    import concourse.bacc as _bacc
    from concourse import mybir as _mybir
    from concourse.bass_utils import run_bass_kernel_spmd as _run

    nc = _bacc.Bacc("TRN2", target_bir_lowering=False, num_devices=1)
    arrays, dram = {}, {}

    def give(name, a):
        a = _np.ascontiguousarray(a)
        arrays[f"in_{name}_dram"] = a
        dram[name] = nc.dram_tensor(f"in_{name}_dram", a.shape, _mybir.dt.from_np(a.dtype),
                                    kind="ExternalInput").ap()

    give("x", inputs["x"])
    give("adj", inputs["adj"])
    give("L0_W", inputs["L0_gnn_W_w"])
    give("L0_WT", _np.asarray(inputs["L0_gnn_W_w"]).T)
    give("L0_b", inputs["L0_gnn_W_b"])
    give("L0_bcol", _np.asarray(inputs["L0_gnn_W_b"]).reshape(FT, P).T)
    give("L0_a", inputs["L0_gnn_a"])
    I = {k: _np.asarray(v) for k, v in inputs.items()}
    cols = lambda a: a.reshape(-1, P).T
    give("L1_WsT", I["L1_gnn_W_self"].T)
    give("L1_WnT", I["L1_gnn_W_nb"].T)
    give("L1_Wc", I["L1_gnn_W_comb"])
    give("L1_bs", cols(I["L1_gnn_b_self"]))
    give("L1_bn", cols(I["L1_gnn_b_nb"]))
    give("L1_bc", I["L1_gnn_b_comb"])
    give("L2_in_W", I["L2_gnn_in_W"])
    give("L2_out_W", I["L2_gnn_out_W"])
    give("L2_WgT", _np.concatenate([I[f"L2_gnn_{g}_W"].T for g in "rzh"], axis=1))
    give("L2_o1T", I["L2_gnn_o1_W"].T)
    give("L2_o2T", I["L2_gnn_o2_W"].T)
    give("L2_gbcol", _np.concatenate([cols(I[f"L2_gnn_{g}_b"]) for g in "rzh"], axis=1))
    give("L2_o1bcol", cols(I["L2_gnn_o1_b"]))
    give("L2_iobcol", _np.concatenate([cols(I["L2_gnn_in_b"]), cols(I["L2_gnn_out_b"])], axis=1))
    give("L3_WQT", I["L3_gnn_WQ"].T)
    give("L3_WKT", I["L3_gnn_WK"].T)
    give("L3_WVT", I["L3_gnn_WV"].T)
    give("L3_we", I["L3_gnn_we"].reshape(HD, 1))
    give("L3_be", I["L3_gnn_be"])
    give("L2_o2b", I["L2_gnn_o2_b"])
    out = nc.dram_tensor("out_0_dram", (2048, 256), _mybir.dt.float32, kind="ExternalOutput").ap()
    graph_layers(nc, dram, out)
    r = _run(nc, [arrays], core_ids=[0])
    return r.results[0]["out_0_dram"]
```

```python
from contextlib import ExitStack

import concourse.bass as bass
from concourse import mybir
from concourse.alu_op_type import AluOpType as ALU

ACT = mybir.ActivationFunctionType
F32, F16, F8, I32, U32 = (mybir.dt.float32, mybir.dt.float16, mybir.dt.float8e4, mybir.dt.int32,
                          mybir.dt.uint32)
AX_X = mybir.AxisListType.X
RADD, RMAX = bass.bass_isa.ReduceOp.add, bass.bass_isa.ReduceOp.max

P = 128
N = 2048
D = 256
NT = N // P
FT = D // P
H = 8
HD = D // H
CH = 512
NC = N // CH
STEPS = 5
EPS = 1e-5
STATE_SCALE = 2048.0
WEIGHT_SCALE = 4096.0
BIG = 1e38
KB = 1024


class Count:

    def __init__(self, sem, unit=1):
        self.sem, self.unit, self.n = sem, unit, 0

    def on(self, ins):
        ins.then_inc(self.sem, self.unit)
        self.n += self.unit
        return self.n


class Chip:

    def __init__(self, nc, ctx, dram, out):
        self.nc, self.ctx, self.dram, self.out = nc, ctx, dram, out
        self.owned = []
        self.arena = ctx.enter_context(nc.sbuf_tensor("arena", [P, 829 * KB // 16], F32))
        self.psum = ctx.enter_context(nc.psum_tensor("psum", [P, 8, CH], F32))
        self.scales, self.splits = ctx.enter_context(nc.sbuf_tensor("scales", [P, 5, 8], F32)), 0
        self.ident = ctx.enter_context(nc.sbuf_tensor("ident", [P, P], F16))

    def sem(self, name):
        self.owned.append(self.ctx.enter_context(self.nc.semaphore(name)))
        return self.owned[-1]

    def clear_semaphores(self):
        with self.nc.Block() as block:
            @block.gpsimd
            def _(pool):
                for s in self.owned:
                    pool.sem_clear(s)

    def view(self, at, shape, dt):
        size = {F32: 4, F16: 2, F8: 1, I32: 4}[dt]
        n = 1
        for s in shape:
            n *= s
        v = self.arena[:, at // 4:at // 4 + (n * size + 3) // 4]
        if dt != F32:
            v = v.bitcast(dt)
        v = v[:, 0:n]
        names = "abcdeg"[:len(shape)]
        if len(shape) > 1:
            v = v.rearrange(f"p ({' '.join(names)}) -> p {' '.join(names)}",
                            **{k: s for k, s in zip(names, shape)})
        return v

    def bank16(self, b):
        return self.psum[:, b, :].bitcast(F16)


AT_A = 0
AT_AT = 32 * KB
AT_X = 64 * KB
AT_SP = 80 * KB
AT_ST = 96 * KB
AT_W = 112 * KB
AT_FREE = 112 * KB + 28 * KB
AT_DEG = AT_FREE + 252 * KB // 4 + KB // 4
PARTS_BYTES = 27136


def load_phase(c, S):
    nc = c.nc
    stage = c.view(AT_SP, [2, N], I32)
    rows16 = c.view(AT_SP + 16 * KB, [2, N], F16)
    a_rows, a_cols = c.view(AT_A, [NT, N], F8), c.view(AT_AT, [NT, N], F8)
    x = c.view(AT_X, [NT, D], F32)
    adj = c.dram["adj"].rearrange("(t p) j -> t p j", p=P)

    adj_loaded = [c.sem("adj_loaded0"), c.sem("adj_loaded1")]
    x_loaded = c.sem("x_loaded")
    rows_cast = c.sem("rows_cast")
    rows_kept = c.sem("rows_kept")
    turned = c.sem("turned")
    cols_kept = c.sem("cols_kept")
    ident_zero, ident_made = c.sem("ident_zero"), c.sem("ident_made")
    weights = S.weights = GatedWeights(c, S)

    def one(steps):
        next(steps, None)

    with nc.Block() as block:
        @block.sync
        def _(sp):
            for u in range(2):
                sp.dma_start(stage[:, u, :], adj[u]).then_inc(adj_loaded[u], 16)
            sp.dma_start(x, c.dram["x"].rearrange("(t p) f -> p t f", p=P)).then_inc(x_loaded, 16)
            weights.sync(sp)
            with sp.Fori(1, NT // 2) as i:
                for u in range(2):
                    sp.wait_ge(rows_kept, 2 * i + u - 1)
                    sp.dma_start(stage[:, u, :], adj[bass.ds(2 * i + u, 1), :, :].rearrange("a p j -> (a p) j")
                                 ).then_inc(adj_loaded[u], 16)
            sp.wait_ge(x_loaded, 16)

        @block.scalar
        def _(act):
            steps = weights.scalar(act)
            for t in range(NT):
                one(steps)
                act.wait_ge(adj_loaded[t % 2], 16 * (t // 2 + 1))
                if t >= 2:
                    act.wait_ge(turned, t - 1)
                nc.scalar.activation(rows16[:, t % 2, :], stage[:, t % 2, :], ACT.Copy,
                                     accum_out=S.degree[:, t:t + 1]).then_inc(rows_cast, 1)
                nc.scalar.activation(a_rows[:, t, :], stage[:, t % 2, :], ACT.Copy,
                                     saturate=False).then_inc(rows_kept, 1)
            for _ in steps:
                pass

        @block.gpsimd
        def _(pool):
            nc.gpsimd.memset(c.ident[:, :], 0.0).then_inc(ident_zero, 1)
            pool.wait_ge(ident_zero, 1)
            nc.gpsimd.affine_select(out=c.ident[:, :], in_=c.ident[:, :], compare_op=ALU.not_equal, fill=1.0,
                                    base=0, pattern=[[-1, P]], channel_multiplier=1).then_inc(ident_made, 1)
            weights.gpsimd(pool)

        @block.tensor
        def _(pe):
            pe.wait_ge(ident_made, 1)

            def turn(t):
                u = t % 2
                pe.wait_ge(rows_cast, t + 1)
                for k in range(NT):
                    last = nc.tensor.transpose(c.bank16(2 * u + k // 8)[:, P * (k % 8):P * (k % 8 + 1)],
                                               rows16[:, u, P * k:P * (k + 1)], c.ident[:, :])
                last.then_inc(turned, 1)

            steps = weights.tensor(pe)
            for t in range(NT):
                if t >= 2:
                    pe.wait_ge(cols_kept, t - 1)
                turn(t)
                if t >= 1:
                    one(steps)
            for _ in steps:
                pass

        @block.vector
        def _(dve):
            steps = weights.vector(dve)
            for t in range(NT):
                u = t % 2
                if t >= 1:
                    one(steps)
                dve.wait_ge(turned, t + 1)
                src = c.psum[:, 2 * u:2 * u + 2, :].rearrange("p b n -> p (b n)").bitcast(F16)
                nc.vector.tensor_copy(a_cols[:, :, t * P:(t + 1) * P], src.rearrange("p (t i) -> p t i", i=P),
                                      saturate=False).then_inc(cols_kept, 1)
            for _ in steps:
                pass


class Chain:

    def __init__(self, eng, sem):
        self.eng, self.sem, self.n = eng, sem, 0

    def __call__(self, ins):
        ins.then_inc(self.sem, 1)
        self.n += 1
        self.eng.wait_ge(self.sem, self.n)


class NodeValues:

    def __init__(self, c, name, tmp):
        self.c, self.nc = c, c.nc
        nc, sem = c.nc, lambda n: c.sem(f"{name}_{n}")
        self.x = c.view(AT_X, [NT, D], F32)
        self.sp = c.view(AT_SP, [NT, 2 * D], F16)
        self.st = c.view(AT_ST, [2 * FT, N], F16)
        self.centred = c.view(tmp, [NT, D], F32)
        small = tmp + 16 * KB
        self.stats = c.view(small, [NT, 6], F32)
        self.moments = c.view(small + 512, [NT, 2], F32)
        self.var = c.view(small + 768, [NT], F32)
        self.dev = c.view(small + 832, [NT], F32)
        self.inv = c.view(small + 896, [NT], F32)
        self.t1 = c.view(small + 960, [NT], F32)
        self.factor = c.view(small + 1024, [NT], F32)
        self.chain_dve = sem("chain")
        self.var_ready, self.dev_ready, self.factor_ready = sem("var"), sem("dev"), sem("factor")
        self.stats_ready = sem("stats")
        self.moments_ready = sem("moments")
        self.centre_ready, self.high, self.low = sem("centre"), sem("high"), sem("low")
        self.turned, self.kept = sem("turned"), sem("kept")

    def vector(self, dve):
        nc = self.nc
        link = Chain(dve, self.chain_dve)
        for t in range(NT):
            nc.vector.bn_stats(self.stats[:, t, :], self.x[:, t, :]).then_inc(self.stats_ready, 1)
        for t in range(NT):
            dve.wait_ge(self.stats_ready, t + 1)
            nc.vector.bn_aggr(self.moments[:, t, :], self.stats[:, t, :]).then_inc(self.moments_ready, 1)
        dve.wait_ge(self.moments_ready, NT)
        nc.vector.tensor_scalar(self.var, self.moments[:, :, 1], EPS, None, ALU.add).then_inc(self.var_ready, 1)
        for t in range(NT):
            nc.vector.tensor_scalar(self.centred[:, t, :], self.x[:, t, :], self.moments[:, t, 0:1], 0.0,
                                    ALU.subtract, ALU.max).then_inc(self.centre_ready, 1)
        dve.wait_ge(self.dev_ready, 1)
        link(nc.vector.reciprocal(self.inv, self.dev))
        dve.wait_ge(self.var_ready, 1)
        link(nc.vector.tensor_tensor(self.t1, self.inv, self.inv, ALU.mult))
        link(nc.vector.tensor_tensor(self.t1, self.t1, self.var, ALU.mult))
        link(nc.vector.tensor_scalar(self.t1, self.t1, -0.5 * STATE_SCALE, 1.5 * STATE_SCALE, ALU.mult, ALU.add))
        nc.vector.tensor_tensor(self.factor, self.t1, self.inv, ALU.mult).then_inc(self.factor_ready, 1)
        dve.wait_ge(self.factor_ready, 1)
        dve.wait_ge(self.centre_ready, NT)
        for t in range(NT):
            dve.wait_ge(self.high, t + 1)
            nc.vector.scalar_tensor_tensor(self.sp[:, t, D:2 * D], self.centred[:, t, :], self.factor[:, t:t + 1],
                                           self.sp[:, t, 0:D], ALU.mult, ALU.subtract).then_inc(self.low, 1)

    def scalar(self, act):
        nc = self.nc
        act.wait_ge(self.var_ready, 1)
        nc.scalar.activation(self.dev, self.var, ACT.Sqrt).then_inc(self.dev_ready, 1)
        act.wait_ge(self.factor_ready, 1)
        act.wait_ge(self.centre_ready, NT)
        for t in range(NT):
            nc.scalar.activation(self.sp[:, t, 0:D], self.centred[:, t, :], ACT.Copy,
                                 scale=self.factor[:, t:t + 1]).then_inc(self.high, 1)
            if t:
                self.keep(act, t - 1)
        self.keep(act, NT - 1)

    def keep(self, act, t):
        act.wait_ge(self.turned, t + 1)
        b = 6 + t % 2
        self.nc.scalar.activation(self.st[:, :, t * P:(t + 1) * P],
                                  self.c.bank16(b)[:, 0:4 * P].rearrange("p (k i) -> p k i", i=P),
                                  ACT.Copy).then_inc(self.kept, 1)

    def tensor(self, pe):
        for t in range(NT):
            pe.wait_ge(self.low, t + 1)
            pe.wait_ge(self.high, t + 1)
            if t >= 2:
                pe.wait_ge(self.kept, t - 1)
            for k in range(4):
                last = self.nc.tensor.transpose(self.c.bank16(6 + t % 2)[:, k * P:(k + 1) * P],
                                                self.sp[:, t, k * P:(k + 1) * P], self.c.ident[:, :])
            last.then_inc(self.turned, 1)


class Split:

    def __init__(self, c, name, w, hi, lo, top=WEIGHT_SCALE):
        self.c, self.nc, self.w, self.hi, self.lo = c, c.nc, w, hi, lo
        t = c.scales[:, c.splits, :]
        c.splits += 1
        self.top = top
        (self.own, self.all_, self.pow2, self.inv, self.scale, self.unscale, self.plain,
         self.half) = (t[:, k:k + 1] for k in range(8))
        sem = lambda n: c.sem(f"{name}_{n}")
        self.own_max, self.all_max, self.chain, self.scaled, self.high, self.low = (
            sem("own_max"), sem("all_max"), sem("chain"), sem("scaled"), sem("high"), sem("low"))

    def vector(self, dve):
        for _ in self.vector_steps(dve):
            pass

    def vector_steps(self, dve):
        nc = self.nc
        link = Chain(dve, self.chain)
        nc.vector.tensor_reduce(self.own, self.w, AX_X, ALU.max, apply_absolute_value=True).then_inc(self.own_max, 1)
        yield
        dve.wait_ge(self.all_max, 1)
        link(nc.vector.tensor_scalar(self.all_, self.all_, 1e-30, None, ALU.max))
        link(nc.vector.tensor_scalar(self.pow2.bitcast(U32), self.all_.bitcast(U32), 0x7F800000, None,
                                     ALU.bitwise_and))
        link(nc.vector.reciprocal(self.inv, self.pow2))
        link(nc.vector.tensor_scalar(self.unscale, self.pow2, 1.0 / (self.top * STATE_SCALE), None, ALU.mult))
        link(nc.vector.tensor_scalar(self.plain, self.pow2, 1.0 / self.top, None, ALU.mult))
        link(nc.vector.tensor_scalar(self.half, self.pow2, 0.5 / self.top, None, ALU.mult))
        nc.vector.tensor_scalar(self.scale, self.inv, self.top, None, ALU.mult).then_inc(self.scaled, 1)
        yield
        dve.wait_ge(self.scaled, 1)
        dve.wait_ge(self.high, 1)
        nc.vector.scalar_tensor_tensor(self.lo, self.w, self.scale, self.hi, ALU.mult, ALU.subtract).then_inc(self.low, 1)

    def gpsimd(self, pool):
        pool.wait_ge(self.own_max, 1)
        self.nc.gpsimd.partition_all_reduce(self.all_, self.own, P, RMAX).then_inc(self.all_max, 1)

    def scalar(self, act):
        act.wait_ge(self.scaled, 1)
        self.nc.scalar.activation(self.hi, self.w, ACT.Copy, scale=self.scale).then_inc(self.high, 1)

    def ready(self, eng):
        eng.wait_ge(self.high, 1)
        eng.wait_ge(self.low, 1)


PARTS3 = ((0, 0), (0, 1), (1, 0))


def bc(ap, shape, axis):
    return ap.unsqueeze(axis + 1).broadcast_to([P] + shape)


def attention_layer(c, S):
    nc, dram = c.nc, c.dram
    HX = D + 2 * H
    V = HD + 1
    a_cols = c.view(AT_AT, [NT, N], F8)
    x = c.view(AT_X, [NT, D], F32)
    F = AT_FREE
    hx = c.view(F, [NT, HX], F32)
    s_rep = c.view(F + 18 * KB, [2, N], F32)
    s_rows = c.view(F + 34 * KB, [N], F32)
    edges = c.view(F + 34 * KB, [4, N], F8)
    sums = c.view(F + 42 * KB, [NT, 2, 2, V], F32)
    both = c.view(F + 42 * KB + 8448, [NT, 2, V], F32)
    fbuf = c.view(F + 42 * KB + 8448 + 4224, [2, NT, 2, V], F32)
    fg = c.view(AT_SP, [2, NT, 3, 2, V], F16)
    total = c.view(AT_SP + 13 * KB, [NT, H, V], F32)
    W = AT_W
    w_rows = c.view(W, [FT, D], F32)
    b_rep = c.view(W + 2 * KB, [FT, P], F32)
    bias = c.view(W + 3 * KB, [HX], F32)
    a_blk = c.view(W + 3 * KB + 1088, [FT, 2 * H], F32)
    w32 = c.view(W + 5 * KB, [FT * HX], F32)
    whi = c.view(W + 8 * KB, [FT * HX], F16)
    wlo = c.view(W + 8 * KB + 1088, [FT * HX], F16)
    w32t = w32.rearrange("p (k n) -> p k n", n=HX)
    wp = [v.rearrange("p (k n) -> p k n", n=HX) for v in (whi, wlo)]
    b_col = c.view(W + 11 * KB, [FT], F32)
    mean_h = c.view(W + 11 * KB + 64, [H, V], F32)
    ones = c.view(W + 13 * KB, [P], F32)
    q = W + 14 * KB
    small = {}
    for n in ("ed", "eg", "es", "et", "neg_d", "u", "tmp", "rden"):
        small[n] = c.view(q, [NT, H], F32)
        q += 512
    nd2 = c.view(q, [2, NT], F32)
    empty = c.view(q + 128, [NT], F32)
    s_bias = c.view(q + 192, [1], F32)
    peak = c.view(q + 196, [H + 1], F32)
    peaks = c.view(q + 236, [H + 1], F32)
    hs = c.view(q + 276, [6], F32)
    h_pow, h_inv, h_scale, h_back, h_mean = (hs[:, k:k + 1] for k in range(5))
    et2 = c.view(q + 320, [NT, H, 2], F32)
    v_all = c.view(F, [NT, H, HD], F32)
    e_all = c.view(F + 18 * KB, [NT, H, HD], F32)
    scratch = nc.dram_tensor("s_rows_dram", [H, N], F32, kind="Internal").ap()

    nodes = NodeValues(c, "n0", F + 18 * KB)
    split = Split(c, "w0", w32, whi, wlo)
    sem = lambda n: c.sem("g_" + n)
    w_loaded, a_loaded = sem("w_loaded"), sem("a_loaded")
    blk_zero, rep_made, wa_made, w_made, ba_made = sem("blk_zero"), sem("rep_made"), sem("wa_made"), sem("w_made"), sem("ba_made")
    ones_made = sem("ones_made")
    h_summed, h_kept, s_summed, s_kept = sem("h_summed"), sem("h_kept"), sem("s_summed"), sem("s_kept")
    s_stored, s_spread = sem("s_stored"), [sem("s_spread0"), sem("s_spread1")]
    peak_own, peak_all = sem("peak_own"), sem("peak_all")
    prep, exps, shifts = sem("prep"), sem("exps"), sem("shifts")
    mean_summed = sem("mean_summed")
    f_made, hi_made, lo_made = sem("f_made"), sem("hi_made"), sem("lo_made")
    edge_made, edge_free = sem("edge_made"), sem("edge_free")
    fg_used = sem("fg_used")
    evacuated = sem("evacuated")
    merged = sem("merged")
    nd_copied = sem("nd_copied")
    dchain, pchain, achain = sem("dchain"), sem("pchain"), sem("achain")
    tail = sem("tail")
    spilled, pattern_made, deg_made, deg_kept = sem("spilled"), sem("pattern_made"), sem("deg_made"), sem("deg_kept")
    a_rows = c.view(AT_A, [NT, N], F8)
    pattern = c.view(W + 20 * KB, [2, 34], F16)
    deg_rows = c.view(AT_DEG, [N], F16)
    S.parts_dram = nc.dram_tensor("parts_dram", [P, PARTS_BYTES // 4], F32, kind="Internal").ap()
    pe_steps, dve_steps = sem("pe_steps"), sem("dve_steps")
    POOLED = (2, 5, 10, 14)
    OWN = NT - len(POOLED)
    BANKS = -(-NT // 3)
    signs = c.view(W, [2, N], F16)
    pooled = c.view(W + 21 * KB, [2, N], F8)
    signed, rectified, pooled_made, pooled_free, nd_free = (
        sem(n) for n in ("signed", "rectified", "pooled_made", "pooled_free", "nd_free"))

    with nc.Block() as block:
        @block.sync
        def _(sp):
            sp.dma_start(w_rows, dram["L0_W"].rearrange("(t p) f -> p t f", p=P)).then_inc(w_loaded, 16)
            sp.dma_start(w32t[:, :, 0:D], dram["L0_WT"].rearrange("(t p) f -> p t f", p=P)).then_inc(w_loaded, 16)
            sp.dma_start(bias[:, 0:D], dram["L0_b"].partition_broadcast(P)).then_inc(w_loaded, 16)
            sp.dma_start(b_col, dram["L0_bcol"]).then_inc(w_loaded, 16)
            sp.wait_ge(blk_zero, 1)
            for h in range(H):
                lo = HD * (h % 4)
                sp.dma_start(a_blk[lo:lo + HD, h // 4, h:h + 1], dram["L0_a"][0:HD, :]).then_inc(a_loaded, 16)
                sp.dma_start(a_blk[lo:lo + HD, h // 4, H + h:H + h + 1], dram["L0_a"][HD:2 * HD, :]).then_inc(a_loaded, 16)
            sp.dma_start(S.parts_dram, S.weights.all).then_inc(spilled, 16)
            sp.wait_ge(s_kept, NC)
            sp.dma_start(scratch, s_rows[0:H, :]).then_inc(s_stored, 16)
            sp.wait_ge(s_stored, 16)
            for h in range(H):
                if h >= 2:
                    sp.wait_ge(edge_made, OWN * (h - 1))
                    sp.wait_ge(rectified, len(POOLED) * (h - 1))
                sp.dma_start(s_rep[:, h % 2, :], scratch[h, :].partition_broadcast(P)).then_inc(s_spread[h % 2], 16)
            sp.wait_ge(s_spread[0], 16 * (H // 2))
            sp.wait_ge(s_spread[1], 16 * (H // 2))

        @block.tensor
        def _(pe):
            pe.wait_ge(w_loaded, 64)
            pe.wait_ge(a_loaded, 16 * 2 * H)
            for k in range(FT):
                for o in range(FT):
                    last = nc.tensor.matmul(c.psum[:, 0, k * 2 * H:(k + 1) * 2 * H], w_rows[:, o, k * P:(k + 1) * P],
                                            a_blk[:, o, :], start=(o == 0), stop=(o == FT - 1))
            last.then_inc(wa_made, 1)
            pe.wait_ge(rep_made, FT)
            for o in range(FT):
                last = nc.tensor.matmul(c.psum[:, 1, 0:2 * H], b_rep[:, o, :], a_blk[:, o, :],
                                        start=(o == 0), stop=(o == FT - 1))
            for o in range(FT):
                last = nc.tensor.matmul(c.psum[0:H, 2, 0:1], a_blk[:, o, 0:H], b_col[:, o:o + 1],
                                        start=(o == 0), stop=(o == FT - 1))
            last.then_inc(ba_made, 1)
            nodes.tensor(pe)
            split.ready(pe)
            pe.wait_ge(nodes.kept, NT)
            pe.wait_ge(w_made, 3)
            for t in range(NT):
                if t >= 4:
                    pe.wait_ge(h_kept, t - 3)
                n = 0
                for k in range(FT):
                    for a, b in PARTS3:
                        last = nc.tensor.matmul(c.psum[:, t % 4, 0:HX], nodes.st[:, 2 * a + k, t * P:(t + 1) * P],
                                                wp[b][:, k, :], start=(n == 0), stop=(n == 5))
                        n += 1
                last.then_inc(h_summed, 1)
            for j in range(NC):
                if j >= 2:
                    pe.wait_ge(s_kept, j - 1)
                n = 0
                for k in range(FT):
                    for a, b in PARTS3:
                        last = nc.tensor.matmul(c.psum[0:H, 4 + j % 2, :], wp[b][:, k, D:D + H],
                                                nodes.st[:, 2 * a + k, j * CH:(j + 1) * CH], start=(n == 0), stop=(n == 5))
                        n += 1
                last.then_inc(s_summed, 1)
            pe.wait_ge(h_kept, NT)
            pe.wait_ge(ones_made, 1)
            for t in range(NT):
                last = nc.tensor.matmul(c.psum[:, 6, 0:D], ones, hx[:, t, 0:D], start=(t == 0), stop=(t == NT - 1))
            last.then_inc(mean_summed, 1)
            pe.wait_ge(evacuated, BANKS)

            with pe.Fori(0, H // 2) as i:
                for u in range(2):
                    n = 2 * i + u
                    pe.wait_ge(hi_made, n + 1)
                    pe.wait_ge(lo_made, n + 3)
                    for j in range(NT):
                        if j in POOLED:
                            m = POOLED.index(j)
                            buffer, used = pooled[:, m % 2, :], pooled_free
                            pe.wait_ge(pooled_made, len(POOLED) * n + m + 1)
                        else:
                            m = j - sum(q < j for q in POOLED)
                            buffer, used = edges[:, m % 4, :], edge_free
                            pe.wait_ge(edge_made, OWN * n + m + 1)
                        pe.sem_inc(pe_steps)
                        for t in range(NT):
                            if j == 0 and t % 3 == 0:
                                pe.wait_ge(evacuated, BANKS * n + t // 3 + 1)
                                pe.sem_inc(pe_steps)
                            o = c.psum[:, t // 3, 4 * V * (t % 3):4 * V * (t % 3 + 1)]
                            mm = nc.tensor.matmul(o, buffer[:, t * P:(t + 1) * P],
                                                  fg[:, u, j, 0:2, :, :].rearrange("p a b v -> p (a b v)"),
                                                  start=(j == 0 and t % 3 == 0), stop=(j == NT - 1), skip_group_check=True)
                            if t == NT - 1:
                                mm.then_inc(used, 1)
                            last = nc.tensor.matmul(o[:, 2 * V:4 * V], a_cols[:, j, t * P:(t + 1) * P],
                                                    fg[:, u, j, 2, :, :].rearrange("p b v -> p (b v)"),
                                                    start=False, stop=(j == NT - 1), skip_group_check=True)
                    last.then_inc(fg_used, 1)
            pe.wait_ge(pattern_made, 3)
            for j in range(NC):
                if j >= 2:
                    pe.wait_ge(deg_kept, j - 1)
                for m, adj in enumerate((a_cols, a_rows)):
                    for t in range(NT):
                        mm = nc.tensor.matmul(c.psum[0:34, 6 + j % 2, :], pattern[:, m, :], adj[:, t, j * CH:(j + 1) * CH],
                                              start=(m == 0 and t == 0), stop=(m == 1 and t == NT - 1))
                mm.then_inc(deg_made, 1)

        @block.vector
        def _(dve):
            link = Chain(dve, dchain)
            nc.vector.memset(ones, 1.0).then_inc(ones_made, 1)
            dve.sem_inc(edge_free, 4)
            dve.sem_inc(lo_made, 2)
            dve.sem_inc(nd_free, 1)
            nc.vector.memset(a_blk, 0.0).then_inc(blk_zero, 1)
            nc.vector.memset(pattern, 0.0).then_inc(pattern_made, 1)
            dve.wait_ge(pattern_made, 1)
            for m in range(2):
                nc.vector.memset(pattern[:, m, m:m + 33:32], 1.0).then_inc(pattern_made, 1)
            dve.wait_ge(w_loaded, 64)
            for o in range(FT):
                nc.vector.tensor_copy(b_rep[:, o, :], b_col[:, o:o + 1].broadcast_to([P, P])).then_inc(rep_made, 1)
            dve.wait_ge(wa_made, 1)
            nc.vector.tensor_copy(w32t[:, :, D:HX], c.psum[:, 0, 0:4 * H].rearrange("p (k n) -> p k n", k=FT)
                                  ).then_inc(w_made, 1)
            dve.wait_ge(w_made, 1)
            split.vector(dve)
            dve.wait_ge(ba_made, 1)
            nc.vector.tensor_copy(bias[:, D:HX], c.psum[:, 1, 0:2 * H]).then_inc(w_made, 1)
            nc.vector.tensor_copy(s_bias[0:H, :], c.psum[0:H, 2, 0:1]).then_inc(w_made, 1)
            dve.wait_ge(w_made, 3)
            nodes.vector(dve)
            nc.vector.tensor_scalar(empty, S.degree[:, :], 0.0, None, ALU.is_equal).then_inc(tail, 1)
            for t in range(NT):
                dve.wait_ge(h_summed, t + 1)
                nc.vector.scalar_tensor_tensor(hx[:, t, :], c.psum[:, t % 4, 0:HX], split.unscale, bias,
                                               ALU.mult, ALU.add).then_inc(h_kept, 1)
            dve.wait_ge(h_kept, NT)
            s_all, d_all = hx[:, :, D:D + H], hx[:, :, D + H:HX]
            link(nc.vector.tensor_reduce(peak[:, H:H + 1], hx[:, :, 0:D], mybir.AxisListType.XY, ALU.max,
                                         apply_absolute_value=True))
            nc.vector.tensor_reduce(peak[:, 0:H], d_all.rearrange("p t h -> p h t"), AX_X, ALU.max).then_inc(peak_own, 1)
            link(nc.vector.tensor_scalar(small["neg_d"], d_all, -1.0, None, ALU.mult))
            dve.wait_ge(peak_all, 1)
            top = peaks[:, 0:H].unsqueeze(1).broadcast_to([P, NT, H])
            link(nc.vector.tensor_tensor(small["u"], s_all, top, ALU.add))
            link(nc.vector.tensor_scalar(small["es"], small["u"], 0.8, 0.0, ALU.mult, ALU.min))
            link(nc.vector.tensor_scalar(small["et"], small["u"], -0.8, 0.0, ALU.mult, ALU.min))
            nc.vector.tensor_tensor(small["tmp"], d_all, top, ALU.subtract).then_inc(shifts, 1)
            link(nc.vector.tensor_scalar(peaks[:, H:H + 1], peaks[:, H:H + 1], 1e-30, None, ALU.max))
            link(nc.vector.tensor_scalar(h_pow.bitcast(U32), peaks[:, H:H + 1].bitcast(U32), 0x7F800000, None, ALU.bitwise_and))
            link(nc.vector.reciprocal(h_inv, h_pow))
            link(nc.vector.tensor_scalar(h_scale, h_inv, WEIGHT_SCALE, None, ALU.mult))
            link(nc.vector.tensor_scalar(h_back, h_pow, 1.0, None, ALU.mult))
            link(nc.vector.tensor_scalar(h_mean, h_scale, 1.0 / N, None, ALU.mult))
            dve.wait_ge(mean_summed, 1)
            nc.vector.tensor_scalar(mean_h[:, :, 0:HD], c.psum[:, 6, 0:D].rearrange("p (h v) -> p h v", v=HD),
                                    h_mean, None, ALU.mult).then_inc(prep, 1)
            nc.vector.memset(mean_h[:, :, HD:V], WEIGHT_SCALE).then_inc(prep, 1)
            dve.wait_ge(exps, 4)

            def make_f(n, u):
                for g, e in enumerate(("ed", "eg")):
                    col = small[e][:, :, bass.ds(n, 1)]
                    nc.vector.scalar_tensor_tensor(fbuf[:, u, :, g, 0:HD], hx[:, :, bass.ds(n * HD, HD)], h_scale,
                                                   col.broadcast_to([P, NT, HD]), ALU.mult, ALU.mult).then_inc(f_made, 1)
                    nc.vector.tensor_scalar(fbuf[:, u, :, g, HD:V], col, WEIGHT_SCALE, None, ALU.mult).then_inc(f_made, 1)
                nc.vector.tensor_copy(nd2[:, u, :], small["neg_d"][:, :, bass.ds(n, 1)].rearrange("p t a -> p (t a)")
                                      ).then_inc(nd_copied, 1)

            def head(i, u, more):
                n = 2 * i + u
                dve.wait_ge(nd_copied, n + 1)
                dve.wait_ge(s_spread[u], 16 * i + 16)
                for m, j in enumerate(j for j in range(NT) if j not in POOLED):
                    if more and m == 6:
                        dve.wait_ge(lo_made, n + 2)
                        dve.wait_ge(nd_free, n + 1)
                        make_f(n + 1, 1 - u)
                    dve.wait_ge(edge_free, OWN * n + m + 1)
                    dve.sem_inc(dve_steps)
                    nc.vector.scalar_tensor_tensor(edges[:, m % 4, :], s_rep[:, u, :], nd2[:, u, j:j + 1],
                                                   a_cols[:, j, :], ALU.is_gt, ALU.mult, saturate=False).then_inc(edge_made, 1)

            make_f(0, 0)
            with dve.Fori(0, H // 2 - 1) as i:
                head(i, 0, True)
                head(i, 1, True)
            head(H // 2 - 1, 0, True)
            head(H // 2 - 1, 1, False)
            dve.wait_ge(merged, 3 * H)
            flat = total.rearrange("p t h v -> p t (h v)")
            for t in range(NT):
                nc.vector.scalar_tensor_tensor(flat[:, t, :], mean_h.rearrange("p h v -> p (h v)"), empty[:, t:t + 1],
                                               flat[:, t, :], ALU.mult, ALU.add).then_inc(tail, 1)
            dve.wait_ge(tail, NT + 1)
            link(nc.vector.reciprocal(small["rden"], total[:, :, :, HD]))
            link(nc.vector.tensor_scalar(small["rden"], small["rden"], h_back, None, ALU.mult))
            for t in range(0, NT, 4):
                nc.vector.tensor_tensor(v_all[:, t:t + 4], total[:, t:t + 4, :, 0:HD],
                                        small["rden"][:, t:t + 4, :].unsqueeze(3).broadcast_to([P, 4, H, HD]),
                                        ALU.mult).then_inc(tail, 1)
            v2, e2 = (v.rearrange("p t h v -> p (t h v)") for v in (v_all, e_all))
            xf = x.rearrange("p t f -> p (t f)")
            dve.wait_ge(tail, NT + 5)
            nc.vector.tensor_scalar(e2, v2, 0.0, None, ALU.min).then_inc(tail, 1)
            dve.wait_ge(exps, 5)
            dve.wait_ge(tail, NT + 6)
            link(nc.vector.scalar_tensor_tensor(v2, v2, 0.0, e2, ALU.max, ALU.add))
            link(nc.vector.scalar_tensor_tensor(xf, v2, -1.0, xf, ALU.add, ALU.add))

        @block.gpsimd
        def _(pool):
            link = Chain(pool, pchain)
            split.gpsimd(pool)
            pool.wait_ge(peak_own, 1)
            nc.gpsimd.partition_all_reduce(peaks, peak, P, RMAX).then_inc(peak_all, 1)
            pool.wait_ge(exps, 4)
            link(nc.gpsimd.tensor_copy(et2[:, :, :, 0], small["es"]))
            link(nc.gpsimd.tensor_copy(et2[:, :, :, 1], small["et"]))
            def parts(n, u):
                pool.wait_ge(f_made, 4 * n + 4)
                pool.wait_ge(hi_made, n + 1)
                f, g = fbuf[:, u, :, 0, :], fbuf[:, u, :, 1, :]
                nc.gpsimd.tensor_tensor(fg[:, u, :, 0, 1, :], f, fg[:, u, :, 0, 0, :], ALU.subtract)
                nc.gpsimd.tensor_tensor(fg[:, u, :, 1, 1, :], fg[:, u, :, 2, 0, :], g, ALU.subtract)
                nc.gpsimd.tensor_tensor(fg[:, u, :, 2, 1, :], g, fg[:, u, :, 2, 0, :], ALU.subtract).then_inc(lo_made, 1)

            def merge(n):
                if n:
                    pool.wait_ge(merged, 3 * n)
                pool.wait_ge(evacuated, BANKS * (n + 2))
                nc.gpsimd.tensor_tensor(both, sums[:, :, :, 0, :], sums[:, :, :, 1, :], ALU.add).then_inc(merged, 1)
                pool.wait_ge(merged, 3 * n + 1)
                nc.gpsimd.tensor_tensor(both, both, et2[:, :, bass.ds(n, 1), :].rearrange("p t a g -> p t (a g)")
                                        .unsqueeze(3).broadcast_to([P, NT, 2, V]), ALU.mult).then_inc(merged, 1)
                pool.wait_ge(merged, 3 * n + 2)
                nc.gpsimd.tensor_tensor(total[:, :, bass.ds(n, 1), :].rearrange("p t a v -> p t (a v)"), both[:, :, 0, :],
                                        both[:, :, 1, :], ALU.add).then_inc(merged, 1)

            def edges_of(n, m):
                k = len(POOLED) * n + m
                pool.wait_ge(rectified, k + 1)
                if k >= 2:
                    pool.wait_ge(pooled_free, k - 1)
                nc.gpsimd.tensor_tensor(pooled[:, m % 2, :], signs[:, m % 2, :], a_cols[:, POOLED[m], :], ALU.mult,
                                        saturate=False).then_inc(pooled_made, 1)

            parts(0, 0)
            for n in range(H):
                edges_of(n, 0)
                edges_of(n, 1)
                if n:
                    merge(n - 1)
                edges_of(n, 2)
                if n + 1 < H:
                    parts(n + 1, (n + 1) % 2)
                edges_of(n, 3)
            merge(H - 1)

        @block.scalar
        def _(act):
            split.scalar(act)
            nodes.scalar(act)
            act.wait_ge(w_made, 3)
            act.wait_ge(spilled, 16)
            for j in range(NC):
                act.wait_ge(s_summed, j + 1)
                nc.scalar.activation(s_rows[0:H, j * CH:(j + 1) * CH], c.psum[0:H, 4 + j % 2, :], ACT.Identity,
                                     bias=s_bias[0:H, :], scale=split.unscale[0:H, :]).then_inc(s_kept, 1)
            act.wait_ge(shifts, 1)
            nc.scalar.activation(small["ed"], small["tmp"], ACT.Exp).then_inc(exps, 1)
            nc.scalar.activation(small["eg"], small["tmp"], ACT.Exp, scale=0.2).then_inc(exps, 1)
            nc.scalar.activation(small["es"], small["es"], ACT.Exp).then_inc(exps, 1)
            nc.scalar.activation(small["et"], small["et"], ACT.Exp).then_inc(exps, 1)
            act.wait_ge(prep, 2)
            act.wait_ge(exps, 4)
            nc.scalar.activation(small["u"], small["u"], ACT.Copy).then_inc(evacuated, BANKS)

            def high(n, u):
                act.wait_ge(f_made, 4 * n + 4)
                f, g = fbuf[:, u, :, 0, :], fbuf[:, u, :, 1, :]
                nc.scalar.activation(fg[:, u, :, 0, 0, :], f, ACT.Copy)
                nc.scalar.activation(fg[:, u, :, 1, 0, :], g, ACT.Copy, scale=-1.0)
                nc.scalar.activation(fg[:, u, :, 2, 0, :], g, ACT.Copy).then_inc(hi_made, 1)

            def evacuate(n):
                act.wait_ge(fg_used, n + 1)
                if n:
                    act.wait_ge(merged, 3 * n - 2)
                for b in range(BANKS):
                    k = min(3, NT - 3 * b)
                    nc.scalar.activation(sums[:, 3 * b:3 * b + k, :, :, :].rearrange("p t g a v -> p (t g a v)"),
                                         c.psum[:, b, 0:4 * V * k], ACT.Copy).then_inc(evacuated, 1)

            def marks(n, m):
                k = len(POOLED) * n + m
                if m == 0:
                    act.wait_ge(nd_copied, n + 1)
                    act.wait_ge(s_spread[n % 2], 16 * (n // 2) + 16)
                if k >= 2:
                    act.wait_ge(pooled_made, k - 1)
                nc.scalar.activation(signs[:, m % 2, :], s_rep[:, n % 2, :], ACT.Sign, scale=-1.0,
                                     bias=nd2[:, n % 2, POOLED[m]:POOLED[m] + 1]).then_inc(signed, 1)
                act.wait_ge(signed, k + 1)
                if m == len(POOLED) - 1:
                    act.sem_inc(nd_free, 1)
                nc.scalar.activation(signs[:, m % 2, :], signs[:, m % 2, :], ACT.Relu, scale=-1.0).then_inc(rectified, 1)

            act.wait_ge(h_kept, NT)
            high(0, 0)
            for n in range(H):
                marks(n, 0)
                marks(n, 1)
                if n:
                    evacuate(n - 1)
                marks(n, 2)
                if n + 1 < H:
                    high(n + 1, (n + 1) % 2)
                marks(n, 3)
            evacuate(H - 1)
            act.wait_ge(tail, NT + 6)
            e2 = e_all.rearrange("p t h v -> p (t h v)")
            nc.scalar.activation(e2, e2, ACT.Exp).then_inc(exps, 1)
            for j in range(NC):
                act.wait_ge(deg_made, j + 1)
                nc.scalar.activation(deg_rows[0:34, j * CH:(j + 1) * CH], c.psum[0:34, 6 + j % 2, :], ACT.Copy
                                     ).then_inc(deg_kept, 1)


def neighbour_sums(nc, c, pe, values, moving, banks, chunk, tiles, signal):
    for b, bank in enumerate(banks):
        for j in tiles:
            for part in range(2):
                k = part * FT + b % FT
                mm = nc.tensor.matmul(c.psum[:, bank, :], values[:, j, k * P:(k + 1) * P],
                                      moving[b // FT][:, j, chunk * CH:(chunk + 1) * CH],
                                      start=(j == 0 and part == 0), stop=(j == NT - 1 and part == 1))
        if tiles[-1] == NT - 1:
            mm.then_inc(signal, 1)


def mean_layer(c, S):
    nc, dram = c.nc, c.dram
    a_cols = c.view(AT_AT, [NT, N], F8)
    x = c.view(AT_X, [NT, D], F32)
    F, W = AT_FREE, AT_FREE + 31 * KB
    nodes = NodeValues(c, "n1", F)
    mid = c.view(W, [2, FT, D], F32)
    comb = c.view(W + 4 * KB, [2 * FT, D], F32)
    v32 = c.view(W + 8 * KB, [4 * D], F32)
    vhi, vlo = c.view(W + 12 * KB, [4 * D], F16), c.view(W + 14 * KB, [4 * D], F16)
    vp = [v.rearrange("p (k n) -> p k n", n=D) for v in (vhi, vlo)]
    b_rep = c.view(W + 16 * KB, [4, P], F32)
    b_col = c.view(W + 18 * KB, [4], F32)
    bias = c.view(W + 18 * KB + 64, [D], F32)
    r_deg = c.view(W + 20 * KB, [NT], F32)
    sums = c.view(F + 18 * KB, [2, FT, 2, CH], F16)
    y = c.view(F + 26 * KB, [2, D], F32)
    split = Split(c, "w1", v32, vhi, vlo)
    sem = lambda n: c.sem("m_" + n)
    w_loaded, rep_made, v_made, v_kept, bias_made, bias_kept = (
        sem("w_loaded"), sem("rep_made"), sem("v_made"), sem("v_kept"), sem("bias_made"), sem("bias_kept"))
    deg_ready, summed, high, low = sem("deg_ready"), sem("summed"), sem("high"), sem("low")
    reloaded = sem("reloaded")
    S.weights.place(AT_W)
    out_made, y_made, x_made, chain = sem("out_made"), sem("y_made"), sem("x_made"), sem("chain")

    with nc.Block() as block:
        @block.sync
        def _(sp):
            for m, name in enumerate(("L1_WsT", "L1_WnT")):
                sp.dma_start(mid[:, m], dram[name].rearrange("(t p) f -> p t f", p=P)).then_inc(w_loaded, 16)
            sp.dma_start(comb, dram["L1_Wc"].rearrange("(t p) f -> p t f", p=P)).then_inc(w_loaded, 16)
            for m, name in enumerate(("L1_bs", "L1_bn")):
                sp.dma_start(b_col[:, FT * m:FT * (m + 1)], dram[name]).then_inc(w_loaded, 16)
            sp.dma_start(bias, dram["L1_bc"].partition_broadcast(P)).then_inc(w_loaded, 16)
            sp.dma_start(S.weights.all, S.parts_dram).then_inc(reloaded, 16)
            sp.wait_ge(reloaded, 16)

        @block.tensor
        def _(pe):
            nodes.tensor(pe)
            pe.wait_ge(nodes.kept, NT)

            def sums_of(j):
                banks = [2 * (j % 2), 2 * (j % 2) + 1]
                if j >= 2:
                    pe.wait_ge(low, 2 * (j - 1))
                neighbour_sums(nc, c, pe, nodes.sp, [a_cols], banks, j, list(range(NT)), summed)

            def outputs(j):
                pe.wait_ge(high, 2 * (j + 1))
                pe.wait_ge(low, 2 * (j + 1))
                for q in range(CH // P):
                    t = j * (CH // P) + q
                    if t >= 2:
                        pe.wait_ge(x_made, t - 1)
                    for m in range(2):
                        n = 0
                        for k in range(FT):
                            for a, b in PARTS3:
                                st = (nodes.st[:, 2 * a + k, t * P:(t + 1) * P] if m == 0 else
                                      sums[:, j % 2, k, a, q * P:(q + 1) * P])
                                mm = nc.tensor.matmul(c.psum[:, 4 + t % 2, m * D:(m + 1) * D], st, vp[b][:, FT * m + k, :],
                                                      start=(n == 0), stop=(n == 5))
                                n += 1
                    mm.then_inc(out_made, 1)

            sums_of(0)
            pe.wait_ge(w_loaded, 96)
            for m in range(2):
                for k in range(FT):
                    for o in range(FT):
                        mm = nc.tensor.matmul(c.psum[:, 5 + m, k * D:(k + 1) * D], mid[:, m, o, k * P:(k + 1) * P],
                                              comb[:, FT * m + o, :], start=(o == 0), stop=(o == FT - 1))
            mm.then_inc(v_made, 1)
            pe.wait_ge(rep_made, 4)
            for k in range(4):
                mm = nc.tensor.matmul(c.psum[:, 7, 0:D], b_rep[:, k, :], comb[:, k, :], start=(k == 0), stop=(k == 3))
            mm.then_inc(bias_made, 1)
            pe.wait_ge(v_kept, 1)
            pe.wait_ge(bias_kept, 1)
            split.ready(pe)
            for j in range(NC):
                if j + 1 < NC:
                    sums_of(j + 1)
                outputs(j)

        @block.vector
        def _(dve):
            link = Chain(dve, chain)
            nodes.vector(dve)

            def low_parts(j):
                for b in range(FT):
                    dve.wait_ge(high, 2 * j + b + 1)
                    nc.vector.scalar_tensor_tensor(sums[:, j % 2, b, 1, :], c.psum[:, 2 * (j % 2) + b, :], 1.0 / STATE_SCALE,
                                                   sums[:, j % 2, b, 0, :], ALU.mult, ALU.subtract).then_inc(low, 1)

            dve.wait_ge(w_loaded, 96)
            for k in range(4):
                nc.vector.tensor_copy(b_rep[:, k, :], b_col[:, k:k + 1].broadcast_to([P, P])).then_inc(rep_made, 1)
            dve.wait_ge(v_made, 1)
            nc.vector.tensor_copy(v32, c.psum[:, 5:7, :].rearrange("p b n -> p (b n)")).then_inc(v_kept, 1)
            dve.wait_ge(v_kept, 1)
            split.vector(dve)
            dve.wait_ge(bias_made, 1)
            nc.vector.tensor_tensor(bias, c.psum[:, 7, 0:D], bias, ALU.add).then_inc(bias_kept, 1)
            link(nc.vector.tensor_scalar(r_deg, S.degree[:, :], 1.0, None, ALU.max))
            link(nc.vector.reciprocal(r_deg, r_deg))
            nc.vector.tensor_scalar(r_deg, r_deg, split.plain, None, ALU.mult).then_inc(deg_ready, 1)
            dve.wait_ge(bias_kept, 1)
            dve.wait_ge(deg_ready, 1)
            low_parts(0)
            for j in range(NC):
                if j + 1 < NC:
                    low_parts(j + 1)
                for q in range(CH // P):
                    t = j * (CH // P) + q
                    dve.wait_ge(out_made, t + 1)
                    if t >= 2:
                        dve.wait_ge(x_made, t - 1)
                    nc.vector.scalar_tensor_tensor(y[:, t % 2, :], c.psum[:, 4 + t % 2, 0:D], split.unscale, bias,
                                                   ALU.mult, ALU.add).then_inc(y_made, 1)
                    dve.wait_ge(y_made, 2 * t + 1)
                    nc.vector.scalar_tensor_tensor(y[:, t % 2, :], c.psum[:, 4 + t % 2, D:2 * D], r_deg[:, t:t + 1],
                                                   y[:, t % 2, :], ALU.mult, ALU.add).then_inc(y_made, 1)
                    dve.wait_ge(y_made, 2 * t + 2)
                    nc.vector.scalar_tensor_tensor(x[:, t, :], y[:, t % 2, :], 0.0, x[:, t, :], ALU.max,
                                                   ALU.add).then_inc(x_made, 1)

        @block.gpsimd
        def _(pool):
            split.gpsimd(pool)

        @block.scalar
        def _(act):
            nodes.scalar(act)
            split.scalar(act)
            for j in range(NC):
                for b in range(FT):
                    act.wait_ge(summed, 2 * j + b + 1)
                    if j >= 2:
                        act.wait_ge(out_made, (CH // P) * (j - 1))
                    nc.scalar.activation(sums[:, j % 2, b, 0, :], c.psum[:, 2 * (j % 2) + b, :], ACT.Copy,
                                         scale=1.0 / STATE_SCALE).then_inc(high, 1)


class GatedWeights:
    G3, KT, TOP = 3 * D, 3 * FT, 16384.0

    def __init__(self, c, S):
        self.c, self.nc = c, c.nc
        self.NM = NM = (self.KT + 1) * self.G3
        F = AT_FREE
        self.place(F + 36 * KB)
        self.m32 = c.view(F, [NM], F32)
        self.m32t = self.m32.rearrange("p (k n) -> p k n", n=self.G3)
        self.wg = c.view(AT_W, [self.KT, self.G3], F32)
        self.io = c.view(AT_W + 18 * KB, [2, FT, D], F32)
        self.o32 = c.view(AT_W + 22 * KB, [2 * FT * D], F32)
        self.io_b = c.view(AT_W + 26 * KB, [2 * FT, 34], F32)
        self.io_col = c.view(AT_W + 26 * KB + 544, [2 * FT], F32)
        self.split = Split(c, "w2", self.m32, self.m_hi, self.m_lo, self.TOP)
        self.osplit = Split(c, "w3", self.o32, self.o_hi, self.o_lo)
        sem = lambda n: c.sem("gw_" + n)
        (self.loaded, self.io_zero, self.io_made, self.m_made, self.m_kept, self.uv_made, self.uv_kept, self.uv_zero,
         self.uv_set) = (sem(n) for n in ("loaded", "io_zero", "io_made", "m_made", "m_kept", "uv_made", "uv_kept",
                                          "uv_zero", "uv_set"))

    def place(self, at):
        c = self.c
        self.m_hi, self.m_lo = c.view(at, [self.NM], F16), c.view(at + 10752, [self.NM], F16)
        self.o_hi, self.o_lo = c.view(at + 21504, [2 * FT * D], F16), c.view(at + 23552, [2 * FT * D], F16)
        self.uv = c.view(at + 25600, [self.G3], F16)
        self.all = c.view(at, [PARTS_BYTES // 4], F32)
        self.mp = [v.rearrange("p (k n) -> p k n", n=self.G3) for v in (self.m_hi, self.m_lo)]
        self.op = [v.rearrange("p (k n) -> p k n", n=D) for v in (self.o_hi, self.o_lo)]

    def sync(self, sp):
        dram = self.c.dram
        for m, name in enumerate(("L2_in_W", "L2_out_W")):
            sp.dma_start(self.io[:, m], dram[name].rearrange("(t p) f -> p t f", p=P)).then_inc(self.loaded, 16)
        sp.dma_start(self.wg, dram["L2_WgT"].rearrange("(t p) n -> p t n", p=P)).then_inc(self.loaded, 16)
        for m, name in enumerate(("L2_o1T", "L2_o2T")):
            sp.dma_start(self.o32.rearrange("p (m t f) -> p m t f", m=2, f=D)[:, m],
                         dram[name].rearrange("(t p) f -> p t f", p=P)).then_inc(self.loaded, 16)
        sp.dma_start(self.io_col, dram["L2_iobcol"]).then_inc(self.loaded, 16)

    def tensor(self, pe):
        nc, c, n = self.nc, self.c, 0
        pe.wait_ge(self.loaded, 96)
        for m in range(2):
            for k in range(FT):
                for g in range(3):
                    if n >= 3:
                        pe.wait_ge(self.m_kept, n - 2)
                    for o in range(FT):
                        mm = nc.tensor.matmul(c.psum[:, 4 + n % 3, 0:D], self.io[:, m, o, k * P:(k + 1) * P],
                                              self.wg[:, FT * m + o, g * D:(g + 1) * D], start=(o == 0), stop=(o == FT - 1))
                    mm.then_inc(self.m_made, 1)
                    n += 1
                yield
        pe.wait_ge(self.io_made, 8)
        pe.wait_ge(self.m_kept, 12)
        for g in range(3):
            for k in range(2 * FT):
                mm = nc.tensor.matmul(c.psum[0:34, 4 + g, 0:D], self.io_b[:, k, :], self.wg[:, k, g * D:(g + 1) * D],
                                      start=(k == 0), stop=(k == 2 * FT - 1))
        mm.then_inc(self.uv_made, 1)

    def vector(self, dve):
        nc, c, n = self.nc, self.c, 0
        nc.vector.memset(self.io_b, 0.0).then_inc(self.io_zero, 1)
        nc.vector.memset(self.uv, 0.0).then_inc(self.uv_zero, 1)
        nc.vector.memset(self.m32t[:, self.KT, :], 0.0).then_inc(self.uv_zero, 1)
        dve.wait_ge(self.io_zero, 1)
        dve.wait_ge(self.loaded, 96)
        for m in range(2):
            for k in range(FT):
                for at in (0, 32):
                    nc.vector.tensor_copy(self.io_b[:, FT * m + k, at + m:at + m + 1],
                                          self.io_col[:, FT * m + k:FT * m + k + 1]).then_inc(self.io_made, 1)
        nc.vector.tensor_scalar(self.m32t[:, 2 * FT:self.KT, :], self.wg[:, 2 * FT:self.KT, :], 1.0 / STATE_SCALE, None,
                                ALU.mult).then_inc(self.uv_zero, 1)
        yield
        for m in range(2):
            for k in range(FT):
                for g in range(3):
                    dve.wait_ge(self.m_made, n + 1)
                    nc.vector.tensor_copy(self.m32t[:, FT * m + k, g * D:(g + 1) * D], c.psum[:, 4 + n % 3, 0:D]
                                          ).then_inc(self.m_kept, 1)
                    n += 1
                yield
        dve.wait_ge(self.uv_made, 1)
        dve.wait_ge(self.uv_zero, 3)
        nc.vector.tensor_copy(self.m32t[0:34, self.KT, :].rearrange("p (g n) -> p g n", n=D), c.psum[0:34, 4:7, 0:D]
                              ).then_inc(self.uv_kept, 1)
        dve.wait_ge(self.uv_kept, 1)
        dve.wait_ge(self.m_kept, 12)
        yield from self.split.vector_steps(dve)
        dve.wait_ge(self.split.low, 1)
        nc.vector.tensor_copy(self.uv[0:32, :], self.mp[0][0:32, self.KT, :]).then_inc(self.uv_set, 1)
        nc.vector.tensor_copy(self.uv[32:64, :], self.mp[1][32:64, self.KT, :]).then_inc(self.uv_set, 1)
        yield
        yield from self.osplit.vector_steps(dve)
        dve.wait_ge(self.osplit.low, 1)
        dve.wait_ge(self.uv_set, 2)

    def gpsimd(self, pool):
        self.split.gpsimd(pool)
        self.osplit.gpsimd(pool)

    def scalar(self, act):
        for k in range(9):
            yield
        self.split.scalar(act)
        yield
        yield
        yield
        self.osplit.scalar(act)


def gated_layer(c, S):
    nc, dram = c.nc, c.dram
    G3 = 3 * D
    GT = G3 // P
    KT = 3 * FT
    a_rows, a_cols = c.view(AT_A, [NT, N], F8), c.view(AT_AT, [NT, N], F8)
    x = c.view(AT_X, [NT, D], F32)
    F, W = AT_FREE, AT_W
    weights = S.weights
    mp, op, uv, split, osplit = weights.mp, weights.op, weights.uv, weights.split, weights.osplit
    g_bias = c.view(W + 27136, [GT], F32)
    h_bias = c.view(W + 27168, [GT], F32)
    o1_bias = c.view(W + 27200, [FT], F32)
    deg_rows = c.view(AT_DEG, [N], F16)
    nodes = NodeValues(c, "n2", F + 21 * KB)
    st, sp_ = nodes.st, nodes.sp
    X = c.view(F, [2, 2, FT, 2, CH], F16)
    rs = c.view(F + 16 * KB, [FT, 2, CH], F16)
    s32 = c.view(F + 20 * KB, [FT, CH], F32)
    tr, tz, th, p32 = (c.view(F + (24 + 4 * k) * KB, [FT, CH], F32) for k in range(4))
    t32, tp = ([c.view(F + at * KB + 4 * k * KB, shape, dt) for at in (40, 52)]
               for k, shape, dt in ((0, [FT, CH], F32), (1, [FT, 2, CH], F16)))
    o2_bias = c.view(F + 48 * KB + 256, [D], F32)
    y = c.view(F + 50 * KB, [2, D], F32)

    sem = lambda n: c.sem("r_" + n)
    b_loaded = sem("b_loaded")
    biases, steps_pe = sem("biases"), sem("steps_pe")
    summed, x_high, x_low = sem("summed"), sem("x_high"), sem("x_low")
    gate_done, gate_read = sem("gate_done"), sem("gate_read")
    s_made, p_made, rs_high, rs_low, d_made, e_made, new_made, st_high, st_low = (
        sem(n) for n in ("s_made", "p_made", "rs_high", "rs_low", "d_made", "e_made", "new_made", "st_high", "st_low"))
    turned, sp_kept = sem("turned"), sem("sp_kept")
    o_made, t_made, t_high, t_low, y_summed, y_made, x_made = (
        sem(n) for n in ("o_made", "t_made", "t_high", "t_low", "y_summed", "y_made", "x_made"))
    CB, GB, TB = 2 * FT, 4, 7
    HB = (TB, 0)

    with nc.Block() as block:
        @block.sync
        def _(sp):
            sp.dma_start(g_bias, dram["L2_gbcol"]).then_inc(b_loaded, 16)
            sp.dma_start(o1_bias, dram["L2_o1bcol"]).then_inc(b_loaded, 16)
            sp.dma_start(o2_bias, dram["L2_o2b"].partition_broadcast(P)).then_inc(b_loaded, 16)

        @block.tensor
        def _(pe):
            nodes.tensor(pe)
            pe.wait_ge(nodes.kept, NT)

            def passes(sem, value):
                pe.wait_ge(sem, value)
                pe.sem_inc(steps_pe)

            def sums_of(j, tiles):
                neighbour_sums(nc, c, pe, sp_, [a_cols, a_rows], range(CB), j, tiles, summed)

            def gates(s, j, after=None):
                passes(x_low, CB * (NC * s + j + 1))
                passes(x_high, CB * (NC * s + j + 1))

                def factor(g, kinds, first, last):
                    bank, n = c.psum[:, GB + g % 3, :], 0
                    total = 3 * len(kinds) + (1 if 0 in kinds else 0)
                    if 0 in kinds:
                        nc.tensor.matmul(bank, uv[0:34, g * P:(g + 1) * P], deg_rows[0:34, j * CH:(j + 1) * CH],
                                         start=first, stop=False)
                        n = 1
                    for k in kinds:
                        for a, b in PARTS3:
                            if k < 2 * FT:
                                mov = X[:, j % 2, k // FT, k % FT, a, :]
                            elif g < 4:
                                mov = st[:, 2 * a + k % FT, j * CH:(j + 1) * CH]
                            else:
                                mov = rs[:, k % FT, a, :]
                            n += 1
                            mm = nc.tensor.matmul(bank, mp[b][:, k, g * P:(g + 1) * P], mov, start=False,
                                                  stop=(last and n == total))
                    return mm

                for g in range(GT):
                    passes(gate_read, GT * (NC * s + j) + g + 1)
                    if g < 4:
                        factor(g, list(range(KT)), True, True).then_inc(gate_done, 1)
                    else:
                        factor(g, list(range(2 * FT)), True, False)
                    if after and g in after:
                        after[g]()
                passes(rs_low, FT * (NC * s + j + 1))
                passes(rs_high, FT * (NC * s + j + 1))
                for g in range(4, GT):
                    factor(g, [2 * FT, 2 * FT + 1], False, True).then_inc(gate_done, 1)

            def turn(s, j, halves=(0, 1)):
                passes(st_low, FT * (NC * s + j + 1) + 1)
                passes(st_high, FT * (NC * s + j + 1))
                for half in halves:
                    passes(sp_kept, 2 * (NC * s + j) + half + 1)
                    for q in range(2):
                        t = j * (CH // P) + 2 * half + q
                        for k in range(4):
                            mm = nc.tensor.transpose(c.bank16(TB)[:, (4 * q + k) * P:(4 * q + k + 1) * P],
                                                     st[:, k, t * P:(t + 1) * P], c.ident[:, :])
                    mm.then_inc(turned, 1)

            def next_sums(s, j):
                for b in range(1):
                    passes(x_low, CB * (NC * s + j))
                sums_of(j, list(range(NT)))

            def step(s, more):
                for j in range(NC):
                    if j + 1 < NC:
                        next_sums(s, j + 1)
                    if j < NC - 1:
                        gates(s, j)
                    elif more:
                        turn(s, 0)
                        turn(s, 1)
                        gates(s, j, {3: lambda: turn(s, 2)})
                    else:
                        gates(s, j, {0: lambda: hidden(0, 0), 1: lambda: hidden(0, 1),
                                     2: lambda: hidden(1, 0), 3: lambda: hidden(1, 1)})
                if more:
                    passes(x_low, CB * NC * (s + 1))
                    passes(sp_kept, 2 * (NC * s + 3) + 1)
                    sums_of(0, list(range(0, 12)))
                    turn(s, 3)
                    passes(sp_kept, 2 * (NC * s + 3) + 2)
                    sums_of(0, [12, 13])
                    passes(sp_kept, 2 * NC * (s + 1) + 1)
                    sums_of(0, [14, 15])

            def hidden(j, g):
                pe.wait_ge(st_low, FT * (NC * (STEPS - 1) + j + 1) + 1)
                pe.wait_ge(st_high, FT * (NC * (STEPS - 1) + j + 1))
                if j:
                    pe.wait_ge(t_made, FT * (j - 1) + g + 1)
                n = 0
                for k in range(FT):
                    for a, b in PARTS3:
                        mm = nc.tensor.matmul(c.psum[:, HB[g], :], op[b][:, k, g * P:(g + 1) * P],
                                              st[:, 2 * a + k, j * CH:(j + 1) * CH], start=(n == 0), stop=(n == 5))
                        n += 1
                mm.then_inc(o_made, 1)

            def output(j):
                pe.wait_ge(t_low, FT * (j + 1))
                pe.wait_ge(t_high, FT * (j + 1))
                for q in range(CH // P):
                    t = j * (CH // P) + q
                    if t >= 2:
                        pe.wait_ge(y_made, t - 1)
                    n = 0
                    for k in range(FT):
                        for a, b in PARTS3:
                            mm = nc.tensor.matmul(c.psum[:, 2 + t % 2, 0:D], tp[j % 2][:, k, a, q * P:(q + 1) * P],
                                                  op[b][:, FT + k, :], start=(n == 0), stop=(n == 5))
                            n += 1
                    mm.then_inc(y_summed, 1)

            sums_of(0, list(range(NT)))
            with pe.Fori(0, STEPS - 1) as s:
                step(s, True)
            step(STEPS - 1, False)
            hidden(2, 0)
            hidden(2, 1)
            output(0)
            output(1)
            output(2)
            hidden(3, 0)
            hidden(3, 1)
            output(3)

        @block.vector
        def _(dve):
            dve.wait_ge(b_loaded, 48)
            nc.vector.tensor_scalar(h_bias, g_bias, 0.5, None, ALU.mult).then_inc(biases, 1)
            nodes.vector(dve)

            def low_parts(s, j):
                for b in range(CB):
                    dve.wait_ge(x_high, CB * (NC * s + j) + b + 1)
                    nc.vector.scalar_tensor_tensor(X[:, j % 2, b // FT, b % FT, 1, :], c.psum[:, b, :], 1.0 / STATE_SCALE,
                                                   X[:, j % 2, b // FT, b % FT, 0, :], ALU.mult, ALU.subtract
                                                   ).then_inc(x_low, 1)

            def update(s, j, between=None):
                at = FT * (NC * s + j)
                dve.wait_ge(st_low, at + 1)
                for k in range(FT):
                    nc.vector.tensor_tensor(s32[:, k, :], st[:, k, j * CH:(j + 1) * CH],
                                            st[:, FT + k, j * CH:(j + 1) * CH], ALU.add).then_inc(s_made, 1)
                for k in range(FT):
                    dve.wait_ge(gate_read, GT * (NC * s + j) + k + 4)
                    dve.wait_ge(s_made, at + k + 1)
                    nc.vector.scalar_tensor_tensor(p32[:, k, :], tr[:, k, :], 1.0, s32[:, k, :], ALU.add, ALU.mult
                                                   ).then_inc(p_made, 1)
                for k in range(FT):
                    dve.wait_ge(rs_high, at + k + 1)
                    nc.vector.scalar_tensor_tensor(rs[:, k, 1, :], p32[:, k, :], 0.5, rs[:, k, 0, :], ALU.mult,
                                                   ALU.subtract).then_inc(rs_low, 1)
                if between:
                    between()
                for k in range(FT):
                    dve.wait_ge(gate_read, GT * (NC * s + j) + k + 8)
                    nc.vector.scalar_tensor_tensor(th[:, k, :], th[:, k, :], STATE_SCALE, s32[:, k, :], ALU.mult,
                                                   ALU.subtract).then_inc(d_made, 1)
                    dve.wait_ge(d_made, at + k + 1)
                    nc.vector.scalar_tensor_tensor(tz[:, k, :], tz[:, k, :], 1.0, th[:, k, :], ALU.add, ALU.mult
                                                   ).then_inc(e_made, 1)
                    dve.wait_ge(e_made, at + k + 1)
                    nc.vector.scalar_tensor_tensor(s32[:, k, :], tz[:, k, :], 0.5, s32[:, k, :], ALU.mult, ALU.add
                                                   ).then_inc(new_made, 1)
                for k in range(FT):
                    dve.wait_ge(st_high, at + k + 1)
                    nc.vector.tensor_tensor(st[:, FT + k, j * CH:(j + 1) * CH], s32[:, k, :],
                                            st[:, k, j * CH:(j + 1) * CH], ALU.subtract).then_inc(st_low, 1)

            def step(s, more):
                for j in range(NC):
                    if j + 1 < NC:
                        low_parts(s, j + 1)
                    update(s, j, hidden_early if not more and j == NC - 1 else None)
                if more:
                    low_parts(s + 1, 0)

            def hidden_low(j):
                for g in range(FT):
                    dve.wait_ge(t_high, FT * j + g + 1)
                    nc.vector.scalar_tensor_tensor(tp[j % 2][:, g, 1, :], t32[j % 2][:, g, :], STATE_SCALE,
                                                   tp[j % 2][:, g, 0, :], ALU.mult, ALU.subtract).then_inc(t_low, 1)

            def hidden_early():
                hidden_low(0)
                hidden_low(1)

            def output(j):
                for q in range(CH // P):
                    t = j * (CH // P) + q
                    dve.wait_ge(y_summed, t + 1)
                    if t >= 2:
                        dve.wait_ge(x_made, t - 1)
                    nc.vector.scalar_tensor_tensor(y[:, t % 2, :], c.psum[:, 2 + t % 2, 0:D], osplit.unscale, o2_bias,
                                                   ALU.mult, ALU.add).then_inc(y_made, 1)
                    dve.wait_ge(y_made, t + 1)
                    nc.vector.tensor_tensor(x[:, t, :], y[:, t % 2, :], x[:, t, :], ALU.add).then_inc(x_made, 1)

            dve.sem_inc(st_low, 1)
            low_parts(0, 0)
            with dve.Fori(0, STEPS - 1) as s:
                step(s, True)
            step(STEPS - 1, False)
            output(0)
            hidden_low(2)
            output(1)
            output(2)
            hidden_low(3)
            output(3)

        @block.scalar
        def _(act):
            nodes.scalar(act)
            act.wait_ge(biases, 1)
            act.sem_inc(gate_read, 3)
            act.sem_inc(sp_kept, 1)

            def high_parts(s, j):
                for b in range(CB):
                    act.wait_ge(summed, CB * (NC * s + j) + b + 1)
                    nc.scalar.activation(X[:, j % 2, b // FT, b % FT, 0, :], c.psum[:, b, :], ACT.Copy,
                                         scale=1.0 / STATE_SCALE).then_inc(x_high, 1)

            def update(s, j, between=None, after=None, before_state=None):
                at = FT * (NC * s + j)

                def gate(g, out, bias, scale):
                    act.wait_ge(gate_done, GT * (NC * s + j) + g + 1)
                    nc.scalar.activation(out[:, g % FT, :], c.psum[:, GB + g % 3, :], ACT.Tanh, bias=bias[:, g:g + 1],
                                         scale=scale).then_inc(gate_read, 1)
                    if after and g in after:
                        after[g]()

                for g in range(FT):
                    gate(g, tr, h_bias, split.half)
                for k in range(FT):
                    act.wait_ge(p_made, at + k + 1)
                    nc.scalar.activation(rs[:, k, 0, :], p32[:, k, :], ACT.Copy, scale=0.5).then_inc(rs_high, 1)
                for g in range(FT, 2 * FT):
                    gate(g, tz, h_bias, split.half)
                if between:
                    between()
                for g in range(2 * FT, 3 * FT):
                    gate(g, th, g_bias, split.plain)
                if before_state:
                    before_state()
                for k in range(FT):
                    act.wait_ge(new_made, at + k + 1)
                    nc.scalar.activation(st[:, k, j * CH:(j + 1) * CH], s32[:, k, :], ACT.Copy).then_inc(st_high, 1)

            def keep(s, j):
                for half in range(2):
                    act.wait_ge(turned, 2 * (NC * s + j) + half + 1)
                    t = j * (CH // P) + 2 * half
                    nc.scalar.activation(sp_[:, t:t + 2, :].rearrange("p t n -> p (t n)"), c.bank16(TB),
                                         ACT.Copy).then_inc(sp_kept, 1)

            def step(s, more):
                for j in range(NC):
                    if j + 1 < NC:
                        high_parts(s, j + 1)
                    if j < NC - 1:
                        update(s, j)
                    elif more:
                        keep(s, 0)
                        keep(s, 1)
                        update(s, j, lambda: keep(s, 2))
                    else:
                        update(s, j, hidden_early, {0: lambda: hidden(0, 0), 1: lambda: hidden(0, 1),
                                                    2: lambda: hidden(1, 0), 3: lambda: hidden(1, 1)},
                               lambda: (hidden(2, 0), hidden(2, 1)))
                if more:
                    keep(s, 3)
                    high_parts(s + 1, 0)

            def hidden(j, g):
                act.wait_ge(o_made, FT * j + g + 1)
                if j >= 2:
                    act.wait_ge(t_low, FT * (j - 2) + g + 1)
                nc.scalar.activation(t32[j % 2][:, g, :], c.psum[:, HB[g], :], ACT.Tanh, bias=o1_bias[:, g:g + 1],
                                     scale=osplit.unscale).then_inc(t_made, 1)

            def hidden_high(j):
                if j >= 2:
                    act.wait_ge(y_summed, (CH // P) * (j - 1))
                for g in range(FT):
                    act.wait_ge(t_made, FT * j + g + 1)
                    nc.scalar.activation(tp[j % 2][:, g, 0, :], t32[j % 2][:, g, :], ACT.Copy, scale=STATE_SCALE
                                         ).then_inc(t_high, 1)

            def hidden_early():
                hidden_high(0)
                hidden_high(1)

            high_parts(0, 0)
            with act.Fori(0, STEPS - 1) as s:
                step(s, True)
            step(STEPS - 1, False)
            hidden_high(2)
            hidden(3, 0)
            hidden(3, 1)
            hidden_high(3)


def hard_attention_layer(c, S):
    nc, dram = c.nc, c.dram
    SCALING = HD ** -0.5
    DOWN = 2.0 ** -17
    x = c.view(AT_X, [NT, D], F32)
    a_rows = c.view(AT_A, [NT, N], F8)
    F, W = AT_FREE, AT_W
    ks = c.view(AT_AT, [H, N], F16)
    qs = c.view(F, [H, N], F16)
    values = c.view(AT_SP, [NT, H, 2, HD], F16)
    w32 = c.view(W, [3 * FT * D + 1], F32)
    w_hi, w_lo = c.view(W + 7 * KB, [3 * FT * D + 1], F16), c.view(W + 11 * KB, [3 * FT * D + 1], F16)
    wp = [v[:, 0:3 * FT * D].rearrange("p (m k n) -> p m k n", m=3, k=FT) for v in (w_hi, w_lo)]
    temp = c.view(W + 15 * KB, [2, CH], F32)
    scal = c.view(W + 27 * KB, [16], F32)
    k_bias, back, bias, be, sq = (scal[:, k:k + 1] for k in range(5))
    best = c.view(W + 27 * KB + 64, [4, 2], F32)
    hard = c.view(AT_ST, [4, N], F16)
    hard_t = c.view(W, [2, NT, P], F16)
    scores = c.view(F + 32 * KB, [4, N], F32)
    mask = c.view(W + 8 * KB, [2, N], F32)
    y = c.view(W + 24 * KB, [2, D], F32)
    flat = c.view(F + 32 * KB, [2, 2, 2, N], F16)
    ON_ACT, ON_POOL = (1, 5), (3, 7)

    nodes = NodeValues(c, "n3", F + 32 * KB)
    split = Split(c, "w4", w32, w_hi, w_lo)
    sem = lambda n: c.sem("h_" + n)
    w_loaded, proj, stacked = sem("w_loaded"), sem("proj"), sem("stacked")
    q_high, q_low, k_full, k_high, k_low = sem("q_high"), sem("q_low"), sem("k_full"), sem("k_high"), sem("k_low")
    v_sum, v_high, v_low = sem("v_sum"), sem("v_high"), sem("v_low")
    consts, masked, mask_ready = sem("consts"), sem("masked"), sem("mask_ready")
    scored, maxed, turned, turned_kept, taken = (
        sem(n) for n in ("scored", "maxed", "turned", "turned_kept", "taken"))
    marked_dve, marked_act, marked_pool = sem("marked_dve"), sem("marked_act"), sem("marked_pool")
    y_half, y_made, stored = sem("y_half"), sem("y_made"), [sem("stored0"), sem("stored1")]
    chain, waited = sem("chain"), sem("waited")
    HALF = N // 2

    def marks_until(i, k):
        if k % 8 in ON_ACT:
            return marked_act, 4 * i + k // 4 + 1
        if k % 8 in ON_POOL:
            return marked_pool, 4 * i + k // 4 + 1
        return marked_dve, 8 * i + k // 2 + 1

    with nc.Block() as block:
        @block.sync
        def _(sp):
            for m, name in enumerate(("L3_WQT", "L3_WKT", "L3_WVT")):
                sp.dma_start(w32[:, m * FT * D:(m + 1) * FT * D].rearrange("p (t f) -> p t f", f=D),
                             dram[name].rearrange("(t p) f -> p t f", p=P)).then_inc(w_loaded, 16)
            for g in range(4):
                sp.dma_start(w32[HD * g:HD * (g + 1), 3 * FT * D:3 * FT * D + 1], dram["L3_we"]).then_inc(w_loaded, 16)
            sp.dma_start(be, dram["L3_be"].partition_broadcast(P)).then_inc(w_loaded, 16)
            for half in range(2):
                for m, (dst, parts) in enumerate(((qs, (0, 0, 1, 1)), (ks, (0, 1, 0, 1)))):
                    sp.wait_ge(k_low if m else q_low, NC * (half + 1))
                    sp.wait_ge(k_high if m else q_high, NC * (half + 1))
                    for h in range(4):
                        for g in range(4):
                            sp.dma_start(dst[HD * g:HD * (g + 1), 4 * half + h, :],
                                         flat[HD * h:HD * (h + 1), m, half, parts[g], :]).then_inc(stacked, 16)
            with sp.Fori(0, NT // 2) as i:
                for u in range(2):
                    sp.wait_ge(y_made, 2 * i + u + 1)
                    sp.dma_start(c.out.rearrange("(t p) f -> t p f", p=P)[bass.ds(2 * i + u, 1), :, :]
                                 .rearrange("a p f -> (a p) f"), y[:, u, :]).then_inc(stored[u], 16)
            for u in range(2):
                sp.wait_ge(stored[u], 16 * NT // 2)

        @block.tensor
        def _(pe):
            nodes.tensor(pe)
            split.ready(pe)
            pe.wait_ge(nodes.kept, NT)
            for n in range(4 * NC):
                half, m, j = n // (2 * NC), n // NC % 2, n % NC
                if m:
                    pe.wait_ge(q_low, n - NC * half - 3)
                elif half:
                    pe.wait_ge(k_full, j + 1)
                f = 0
                for k in range(FT):
                    for a, b in PARTS3:
                        mm = nc.tensor.matmul(c.psum[:, n % 4, :], wp[b][:, m, k, half * P:(half + 1) * P],
                                              nodes.st[:, 2 * a + k, j * CH:(j + 1) * CH], start=(f == 0), stop=(f == 5))
                        f += 1
                mm.then_inc(proj, 1)
            for t in range(NT):
                if t >= 2:
                    pe.wait_ge(v_low, t - 1)
                n = 0
                for k in range(FT):
                    for a, b in PARTS3:
                        mm = nc.tensor.matmul(c.psum[:, 4 + t % 2, 0:D], nodes.st[:, 2 * a + k, t * P:(t + 1) * P],
                                              wp[b][:, 2, k, :], start=(n == 0), stop=(n == 5))
                        n += 1
                mm.then_inc(v_sum, 1)
            pe.wait_ge(k_full, 2 * NC)
            pe.wait_ge(stacked, 16 * 64)
            pe.wait_ge(v_low, NT)
            pe.wait_ge(v_high, NT)

            def score(i, k, half):
                n = 16 * i + k
                for half in (half,):
                    if not (isinstance(i, int) and n == 0):
                        pe.wait_ge(maxed, 2 * (n - 1) + half + 1)
                    for q in range(2):
                        col = HALF * half + CH * q
                        mm = nc.tensor.matmul(c.psum[:, 2 * half + q, :],
                                              qs[:, k % H, bass.ds((2 * i + k // H) * P, P)],
                                              ks[:, k % H, col:col + CH], start=True, stop=True)
                    mm.then_inc(scored, 1)

            def take(i, k):
                n = 16 * i + k
                h, u = k % H, (k // H) % 2
                pe.wait_ge(turned_kept, 2 * n + 2)
                if h == 0 and not (isinstance(i, int) and n < 16):
                    pe.wait_ge(y_made, 2 * i + k // H - 1)
                for t in range(NT):
                    mm = nc.tensor.matmul(c.psum[:, 6 + u, 2 * HD * h:2 * HD * (h + 1)], hard_t[:, k % 2, t, :],
                                          values[:, t, h, :, :].rearrange("p a d -> p (a d)"),
                                          start=(t == 0), stop=(t == NT - 1))
                mm.then_inc(taken, 1)

            def turn(i, k):
                n = 16 * i + k
                pe.wait_ge(*marks_until(i, k))
                for half in range(2):
                    if not (isinstance(i, int) and n == 0):
                        pe.wait_ge(turned_kept, 2 * (n - 1) + half + 1)
                    for t in range(8):
                        mm = nc.tensor.transpose(c.bank16(4 + half)[:, t * P:(t + 1) * P],
                                                 hard[:, k % 4, (8 * half + t) * P:(8 * half + t + 1) * P], c.ident[:, :])
                    mm.then_inc(turned, 1)

            def units(i):
                for k in range(16):
                    first = isinstance(i, int)
                    score(i, k, 0)
                    if not (first and k < 4):
                        take(i, k - 4)
                    score(i, k, 1)
                    if not (first and k < 3):
                        turn(i, k - 3)

            units(0)
            with pe.Fori(1, NT // 2) as i:
                units(i)
            last = NT // 2 - 1
            for k in range(13, 16):
                take(last, k - 1)
                turn(last, k)
            take(last, 15)

        @block.vector
        def _(dve):
            link = Chain(dve, chain)
            dve.wait_ge(w_loaded, 16 * 8)
            split.vector(dve)
            link(nc.vector.tensor_scalar(k_bias, w32[:, 3 * FT * D:3 * FT * D + 1], split.scale, STATE_SCALE * DOWN,
                                         ALU.mult, ALU.mult))
            link(nc.vector.tensor_scalar(back, split.plain, 1.0 / (H * STATE_SCALE * DOWN), None, ALU.mult))
            link(nc.vector.tensor_scalar(sq, split.scale, STATE_SCALE * DOWN, None, ALU.mult))
            link(nc.vector.tensor_scalar(bias, be, sq, sq, ALU.mult, ALU.mult))
            dve.sem_inc(consts, 1)
            nodes.vector(dve)
            dve.wait_ge(split.low, 1)

            for n in range(4 * NC):
                half, m, j = n // (2 * NC), n // NC % 2, n % NC
                hi, lo = (flat[:, m, half, part, j * CH:(j + 1) * CH] for part in range(2))
                if m == 0:
                    dve.wait_ge(q_high, NC * half + j + 1)
                    nc.vector.scalar_tensor_tensor(lo, c.psum[:, n % 4, :], DOWN, hi, ALU.mult, ALU.subtract
                                                   ).then_inc(q_low, 1)
                else:
                    dve.wait_ge(k_high, NC * half + j + 1)
                    nc.vector.tensor_tensor(lo, temp[:, n % 2, :], hi, ALU.subtract).then_inc(k_low, 1)
            for t in range(NT):
                dve.wait_ge(v_high, t + 1)
                nc.vector.scalar_tensor_tensor(values[:, t, :, 1, :], c.psum[:, 4 + t % 2, 0:D].rearrange("p (h d) -> p h d", d=HD),
                                               DOWN, values[:, t, :, 0, :], ALU.mult, ALU.subtract).then_inc(v_low, 1)
            dve.wait_ge(stacked, 16 * 64)

            def unit(i, k):
                n = 16 * i + k
                first = isinstance(i, int) and i == 0
                sem_of, until = marks_until(i, k)
                if k % H == 0:
                    dve.wait_ge(mask_ready, 2 * i + k // H + 1)
                if not (first and k < 4):
                    dve.wait_ge(sem_of, until - (2 if sem_of is marked_dve else 1))
                for half in range(2):
                    dve.wait_ge(scored, 2 * n + half + 1)
                    if half:
                        dve.wait_ge(maxed, 2 * n + 1)
                    dve.sem_inc(waited)
                    at = slice(HALF * half, HALF * (half + 1))
                    nc.vector.tensor_tensor_reduce(scores[:, k % 4, at],
                                                   c.psum[:, 2 * half:2 * half + 2, :].rearrange("p b n -> p (b n)"),
                                                   mask[:, (k // H) % 2, at], 1.0,
                                                   best[:, k % 4, 0:1] if half else -BIG / 4, ALU.add, ALU.max,
                                                   best[:, k % 4, half:half + 1]).then_inc(maxed, 1)
                if sem_of is marked_dve:
                    dve.wait_ge(maxed, 2 * n + 2)
                    if not (first and k < 4):
                        dve.wait_ge(turned, 2 * (n - 3))
                    nc.vector.tensor_scalar(hard[:, k % 4, :], scores[:, k % 4, :], best[:, k % 4, 1:2], None,
                                            ALU.is_equal).then_inc(marked_dve, 1)

            def finish(i, u, after_first):
                qt = 2 * i + u
                dve.wait_ge(taken, H * (qt + 1))
                if after_first:
                    dve.wait_ge(stored[u], 16 * i)
                o = c.psum[:, 6 + u, :].rearrange("p (h a d) -> p h a d", a=2, d=HD)
                yv = y[:, u, :].rearrange("p (h d) -> p h d", d=HD)
                xv = x[:, bass.ds(qt, 1), :].rearrange("p a (h d) -> p (a h) d", d=HD)
                nc.vector.scalar_tensor_tensor(yv, o[:, :, 0, :], back, xv, ALU.mult, ALU.add).then_inc(y_half, 1)
                dve.wait_ge(y_half, qt + 1)
                nc.vector.scalar_tensor_tensor(yv, o[:, :, 1, :], back, yv, ALU.mult, ALU.add).then_inc(y_made, 1)

            for k in range(16):
                unit(0, k)
                if k == 13:
                    finish(0, 0, False)
            with dve.Fori(1, NT // 2) as i:
                for k in range(16):
                    unit(i, k)
                    if k == 5:
                        dve.wait_ge(stored[0], 16 * i)
                        finish(i - 1, 1, False)
                    if k == 13:
                        finish(i, 0, True)
            dve.wait_ge(stored[0], 16 * (NT // 2))
            finish(NT // 2 - 1, 1, True)

        @block.gpsimd
        def _(pool):
            split.gpsimd(pool)
            pool.wait_ge(consts, 1)

            def bias_mask(t):
                pool.wait_ge(masked, t + 1)
                nc.gpsimd.tensor_scalar(mask[:, t % 2, :], mask[:, t % 2, :], bias, None, ALU.min).then_inc(mask_ready, 1)

            bias_mask(0)
            bias_mask(1)
            for n in range(NT * H):
                if n % H in ON_POOL:
                    pool.wait_ge(maxed, 2 * n + 2)
                    if n >= 4:
                        pool.wait_ge(turned, 2 * (n - 3))
                    nc.gpsimd.tensor_scalar(hard[:, n % 4, :], scores[:, n % 4, :], best[:, n % 4, 1:2], None,
                                            ALU.is_equal).then_inc(marked_pool, 1)
                if n % H == H - 1 and n // H + 2 < NT:
                    bias_mask(n // H + 2)

        @block.scalar
        def _(act):
            split.scalar(act)
            nodes.scalar(act)
            act.wait_ge(nodes.low, NT)
            act.wait_ge(consts, 1)
            for n in range(4 * NC):
                half, m, j = n // (2 * NC), n // NC % 2, n % NC
                kept = NC * half + j
                hi = flat[:, m, half, 0, j * CH:(j + 1) * CH]
                act.wait_ge(proj, n + 1)
                if m == 0:
                    nc.scalar.activation(hi, c.psum[:, n % 4, :], ACT.Copy, scale=DOWN).then_inc(q_high, 1)
                else:
                    if kept >= 2:
                        act.wait_ge(k_low, kept - 1)
                    nc.scalar.activation(temp[:, n % 2, :], c.psum[:, n % 4, :], ACT.Identity, bias=k_bias,
                                         scale=SCALING * DOWN).then_inc(k_full, 1)
                    act.wait_ge(k_full, kept + 1)
                    nc.scalar.activation(hi, temp[:, n % 2, :], ACT.Copy).then_inc(k_high, 1)
            for t in range(NT):
                act.wait_ge(v_sum, t + 1)
                nc.scalar.activation(values[:, t, :, 0, :], c.psum[:, 4 + t % 2, 0:D].rearrange("p (h d) -> p h d", d=HD),
                                     ACT.Copy, scale=DOWN).then_inc(v_high, 1)
            act.wait_ge(v_sum, NT)
            act.wait_ge(k_low, 2 * NC)

            def mask_rows(t):
                if t >= 2:
                    act.wait_ge(maxed, 2 * H * (t - 1))
                    act.wait_ge(mask_ready, t - 1)
                nc.scalar.activation(mask[:, t % 2, :], a_rows[:, t, :], ACT.Copy, scale=BIG, bias=-BIG / 2
                                     ).then_inc(masked, 1)

            mask_rows(0)
            mask_rows(1)
            def keep(n):
                for half in range(2):
                    act.wait_ge(turned, 2 * n + half + 1)
                    if n >= 2:
                        act.wait_ge(taken, n - 1)
                    own = n % H in ON_ACT
                    nc.scalar.activation(hard_t[:, n % 2, 8 * half:8 * half + 8, :].rearrange("p t q -> p (t q)"),
                                         c.bank16(4 + half), ACT.Copy, scale=-1.0 if own else 1.0,
                                         bias=1.0 if own else 0.0).then_inc(turned_kept, 1)

            for n in range(NT * H):
                if n >= 3:
                    keep(n - 3)
                if n % H in ON_ACT:
                    act.wait_ge(maxed, 2 * n + 2)
                    if n >= 4:
                        act.wait_ge(turned, 2 * (n - 3))
                    nc.scalar.activation(hard[:, n % 4, :], scores[:, n % 4, :], ACT.Sign, bias=best[:, n % 4, 1:2],
                                         scale=-1.0).then_inc(marked_act, 1)
                if n % H == H - 1 and n // H + 2 < NT:
                    mask_rows(n // H + 2)
            for n in range(NT * H - 3, NT * H):
                keep(n)


class Shared:
    pass
''

def graph_layers(nc, dram, out):
    with ExitStack() as ctx:
        c = Chip(nc, ctx, dram, out)
        S = Shared()
        S.degree = ctx.enter_context(nc.sbuf_tensor("degree", [P, NT], F32))
        layers = [load_phase, attention_layer, mean_layer, gated_layer, hard_attention_layer]
        for layer in layers:
            with ExitStack() as own:
                c.ctx, c.owned = own, []
                layer(c, S)
                if layer is not layers[-1]:
                    c.clear_semaphores()


def kernel(**inputs):
    import numpy as _np
    import concourse.bacc as _bacc
    from concourse import mybir as _mybir
    from concourse.bass_utils import run_bass_kernel_spmd as _run

    nc = _bacc.Bacc("TRN2", target_bir_lowering=False, num_devices=1)
    arrays, dram = {}, {}

    def give(name, a):
        a = _np.ascontiguousarray(a)
        arrays[f"in_{name}_dram"] = a
        dram[name] = nc.dram_tensor(f"in_{name}_dram", a.shape, _mybir.dt.from_np(a.dtype),
                                    kind="ExternalInput").ap()

    give("x", inputs["x"])
    give("adj", inputs["adj"])
    give("L0_W", inputs["L0_gnn_W_w"])
    give("L0_WT", _np.asarray(inputs["L0_gnn_W_w"]).T)
    give("L0_b", inputs["L0_gnn_W_b"])
    give("L0_bcol", _np.asarray(inputs["L0_gnn_W_b"]).reshape(FT, P).T)
    give("L0_a", inputs["L0_gnn_a"])
    I = {k: _np.asarray(v) for k, v in inputs.items()}
    cols = lambda a: a.reshape(-1, P).T
    give("L1_WsT", I["L1_gnn_W_self"].T)
    give("L1_WnT", I["L1_gnn_W_nb"].T)
    give("L1_Wc", I["L1_gnn_W_comb"])
    give("L1_bs", cols(I["L1_gnn_b_self"]))
    give("L1_bn", cols(I["L1_gnn_b_nb"]))
    give("L1_bc", I["L1_gnn_b_comb"])
    give("L2_in_W", I["L2_gnn_in_W"])
    give("L2_out_W", I["L2_gnn_out_W"])
    give("L2_WgT", _np.concatenate([I[f"L2_gnn_{g}_W"].T for g in "rzh"], axis=1))
    give("L2_o1T", I["L2_gnn_o1_W"].T)
    give("L2_o2T", I["L2_gnn_o2_W"].T)
    give("L2_gbcol", _np.concatenate([cols(I[f"L2_gnn_{g}_b"]) for g in "rzh"], axis=1))
    give("L2_o1bcol", cols(I["L2_gnn_o1_b"]))
    give("L2_iobcol", _np.concatenate([cols(I["L2_gnn_in_b"]), cols(I["L2_gnn_out_b"])], axis=1))
    give("L3_WQT", I["L3_gnn_WQ"].T)
    give("L3_WKT", I["L3_gnn_WK"].T)
    give("L3_WVT", I["L3_gnn_WV"].T)
    give("L3_we", I["L3_gnn_we"].reshape(HD, 1))
    give("L3_be", I["L3_gnn_be"])
    give("L2_o2b", I["L2_gnn_o2_b"])
    out = nc.dram_tensor("out_0_dram", (2048, 256), _mybir.dt.float32, kind="ExternalOutput").ap()
    graph_layers(nc, dram, out)
    r = _run(nc, [arrays], core_ids=[0])
    return r.results[0]["out_0_dram"]
```

```python
from contextlib import ExitStack

import concourse.bass as bass
from concourse import mybir
from concourse.alu_op_type import AluOpType as ALU

ACT = mybir.ActivationFunctionType
F32, F16, F8, I32, U32 = (mybir.dt.float32, mybir.dt.float16, mybir.dt.float8e4, mybir.dt.int32,
                          mybir.dt.uint32)
AX_X = mybir.AxisListType.X
RMAX = bass.bass_isa.ReduceOp.max

P = 128
N = 2048
D = 256
NT = N // P
FT = D // P
H = 8
HD = D // H
CH = 512
NC = N // CH
STEPS = 5
EPS = 1e-5
STATE_SCALE = 2048.0
WEIGHT_SCALE = 4096.0
BIG = 1e38
KB = 1024


class Chip:

    def __init__(self, nc, ctx, dram, out):
        self.nc, self.ctx, self.dram, self.out = nc, ctx, dram, out
        self.owned = []
        self.arena = ctx.enter_context(nc.sbuf_tensor("arena", [P, 829 * KB // 16], F32))
        self.psum = ctx.enter_context(nc.psum_tensor("psum", [P, 8, CH], F32))
        self.scales, self.splits = ctx.enter_context(nc.sbuf_tensor("scales", [P, 5, 8], F32)), 0
        self.pattern = ctx.enter_context(nc.sbuf_tensor("pattern", [P, 35], F16))
        self.ident = ctx.enter_context(nc.sbuf_tensor("ident", [P, P], F16))

    def sem(self, name):
        self.owned.append(self.ctx.enter_context(self.nc.semaphore(name)))
        return self.owned[-1]

    def clear_semaphores(self):
        with self.nc.Block() as block:
            @block.gpsimd
            def _(pool):
                for s in self.owned[0::4]:
                    pool.sem_clear(s)

            @block.vector
            def _(dve):
                for s in self.owned[1::4]:
                    dve.sem_clear(s)

            @block.scalar
            def _(act):
                for s in self.owned[2::4]:
                    act.sem_clear(s)

            @block.sync
            def _(sp):
                for s in self.owned[3::4]:
                    sp.sem_clear(s)

    def view(self, at, shape, dt):
        size = {F32: 4, F16: 2, F8: 1, I32: 4}[dt]
        n = 1
        for s in shape:
            n *= s
        v = self.arena[:, at // 4:at // 4 + (n * size + 3) // 4]
        if dt != F32:
            v = v.bitcast(dt)
        v = v[:, 0:n]
        names = "abcdeg"[:len(shape)]
        if len(shape) > 1:
            v = v.rearrange(f"p ({' '.join(names)}) -> p {' '.join(names)}",
                            **{k: s for k, s in zip(names, shape)})
        return v

    def bank16(self, b):
        return self.psum[:, b, :].bitcast(F16)


AT_A = 0
AT_AT = 32 * KB
AT_X = 64 * KB
AT_SP = 80 * KB
AT_ST = 96 * KB
AT_W = 112 * KB
AT_FREE = 112 * KB + 28 * KB
AT_DEG = AT_FREE + 252 * KB // 4 + KB // 4
PARTS_BYTES = 27136


def load_phase(c, S):
    nc = c.nc
    STAGES = 3
    stage = c.view(AT_SP, [STAGES, N], I32)
    rows16 = c.view(AT_SP + 24 * KB, [2, N], F16)
    ON_POOL = (1, 3, 5, 7, 10)
    kept_until = lambda t: sum(q <= t for q in ON_POOL)
    a_rows, a_cols = c.view(AT_A, [NT, N], F8), c.view(AT_AT, [NT, N], F8)
    x = c.view(AT_X, [NT, D], F32)
    adj = c.dram["adj"].rearrange("(t p) j -> t p j", p=P)

    adj_loaded = [c.sem(f"adj_loaded{u}") for u in range(STAGES)]
    rows_kept_pool = c.sem("rows_kept_pool")
    x_loaded = c.sem("x_loaded")
    rows_cast = c.sem("rows_cast")
    rows_kept = c.sem("rows_kept")
    turned = c.sem("turned")
    cols_kept = c.sem("cols_kept")
    ident_zero, ident_made = c.sem("ident_zero"), c.sem("ident_made")
    weights = S.weights = GatedWeights(c, S)

    def one(steps):
        next(steps, None)

    with nc.Block() as block:
        @block.sync
        def _(sp):
            for t in range(NT):
                if t == STAGES:
                    weights.sync(sp)
                if t >= STAGES:
                    sp.wait_ge(rows_cast, t - STAGES + 1)
                    if t - STAGES in ON_POOL:
                        sp.wait_ge(rows_kept_pool, kept_until(t - STAGES))
                    else:
                        sp.wait_ge(rows_kept, t - STAGES + 1 - kept_until(t - STAGES))
                sp.dma_start(stage[:, t % STAGES, :], adj[t]).then_inc(adj_loaded[t % STAGES], 16)
            sp.dma_start(x, c.dram["x"].rearrange("(t p) f -> p t f", p=P)).then_inc(x_loaded, 16)
            sp.wait_ge(x_loaded, 16)

        @block.scalar
        def _(act):
            steps = weights.scalar(act)
            for t in range(NT):
                one(steps)
                act.wait_ge(adj_loaded[t % STAGES], 16 * (t // STAGES + 1))
                if t >= 2:
                    act.wait_ge(turned, t - 1)
                nc.scalar.activation(rows16[:, t % 2, :], stage[:, t % STAGES, :], ACT.Copy,
                                     accum_out=S.degree[:, t:t + 1]).then_inc(rows_cast, 1)
                if t not in ON_POOL:
                    nc.scalar.activation(a_rows[:, t, :], stage[:, t % STAGES, :], ACT.Copy,
                                         saturate=False).then_inc(rows_kept, 1)
            for _ in steps:
                pass

        @block.gpsimd
        def _(pool):
            nc.gpsimd.memset(c.ident[:, :], 0.0).then_inc(ident_zero, 1)
            pool.wait_ge(ident_zero, 1)
            nc.gpsimd.affine_select(out=c.ident[:, :], in_=c.ident[:, :], compare_op=ALU.not_equal, fill=1.0,
                                    base=0, pattern=[[-1, P]], channel_multiplier=1).then_inc(ident_made, 1)

            def rows(t):
                pool.wait_ge(adj_loaded[t % STAGES], 16 * (t // STAGES + 1))
                nc.gpsimd.tensor_copy(a_rows[:, t, :], stage[:, t % STAGES, :], saturate=False).then_inc(rows_kept_pool, 1)

            for t in ON_POOL[0:4]:
                rows(t)
            weights.split.gpsimd(pool)
            for t in ON_POOL[4:]:
                rows(t)
            weights.osplit.gpsimd(pool)

        @block.tensor
        def _(pe):
            pe.wait_ge(ident_made, 1)

            def turn(t):
                u = t % 2
                pe.wait_ge(rows_cast, t + 1)
                for k in range(NT):
                    last = nc.tensor.transpose(c.bank16(2 * u + k // 8)[:, P * (k % 8):P * (k % 8 + 1)],
                                               rows16[:, u, P * k:P * (k + 1)], c.ident[:, :])
                last.then_inc(turned, 1)

            steps = weights.tensor(pe)
            for t in range(NT):
                if t >= 2:
                    pe.wait_ge(cols_kept, t - 1)
                turn(t)
                if t >= 1:
                    one(steps)
            for _ in steps:
                pass

        @block.vector
        def _(dve):
            steps = weights.vector(dve)
            for t in range(NT):
                u = t % 2
                if t >= 1:
                    one(steps)
                dve.wait_ge(turned, t + 1)
                src = c.psum[:, 2 * u:2 * u + 2, :].rearrange("p b n -> p (b n)").bitcast(F16)
                nc.vector.tensor_copy(a_cols[:, :, t * P:(t + 1) * P], src.rearrange("p (t i) -> p t i", i=P),
                                      saturate=False).then_inc(cols_kept, 1)
            for _ in steps:
                pass


class Chain:

    def __init__(self, eng, sem):
        self.eng, self.sem, self.n = eng, sem, 0

    def __call__(self, ins):
        ins.then_inc(self.sem, 1)
        self.n += 1
        self.eng.wait_ge(self.sem, self.n)


class NodeValues:

    def __init__(self, c, name, tmp):
        self.c, self.nc = c, c.nc
        nc, sem = c.nc, lambda n: c.sem(f"{name}_{n}")
        self.x = c.view(AT_X, [NT, D], F32)
        self.sp = c.view(AT_SP, [NT, 2 * D], F16)
        self.st = c.view(AT_ST, [2 * FT, N], F16)
        self.centred = c.view(tmp, [NT, D], F32)
        small = tmp + 16 * KB
        self.stats = c.view(small, [NT, 6], F32)
        self.moments = c.view(small + 512, [NT, 2], F32)
        self.var = c.view(small + 768, [NT], F32)
        self.dev = c.view(small + 832, [NT], F32)
        self.inv = c.view(small + 896, [NT], F32)
        self.t1 = c.view(small + 960, [NT], F32)
        self.factor = c.view(small + 1024, [NT], F32)
        self.chain_dve = sem("chain")
        self.var_ready, self.dev_ready, self.factor_ready = sem("var"), sem("dev"), sem("factor")
        self.stats_ready = sem("stats")
        self.moments_ready = sem("moments")
        self.centre_ready, self.high, self.low = sem("centre"), sem("high"), sem("low")
        self.turned, self.kept_act, self.kept_dve = sem("turned"), sem("kept_act"), sem("kept_dve")

    def vector(self, dve, prep=iter(())):
        nc = self.nc
        link = Chain(dve, self.chain_dve)
        half = NT // 2
        for g in range(2):
            tiles = range(half * g, half * (g + 1))
            cols = slice(half * g, half * (g + 1))
            for t in tiles:
                nc.vector.bn_stats(self.stats[:, t, :], self.x[:, t, :]).then_inc(self.stats_ready, 1)
            for t in tiles:
                dve.wait_ge(self.stats_ready, t + 1)
                nc.vector.bn_aggr(self.moments[:, t, :], self.stats[:, t, :]).then_inc(self.moments_ready, 1)
            dve.wait_ge(self.moments_ready, half * (g + 1))
            nc.vector.tensor_scalar(self.var[:, cols], self.moments[:, cols, 1], EPS, None, ALU.add
                                    ).then_inc(self.var_ready, 1)
            for t in tiles:
                nc.vector.tensor_scalar(self.centred[:, t, :], self.x[:, t, :], self.moments[:, t, 0:1], 0.0,
                                        ALU.subtract, ALU.max).then_inc(self.centre_ready, 1)
            inv, t1, factor = self.inv[:, cols], self.t1[:, cols], self.factor[:, cols]
            dve.wait_ge(self.dev_ready, g + 1)
            link(nc.vector.reciprocal(inv, self.dev[:, cols]))
            dve.wait_ge(self.var_ready, g + 1)
            link(nc.vector.tensor_tensor(t1, inv, inv, ALU.mult))
            link(nc.vector.tensor_tensor(t1, t1, self.var[:, cols], ALU.mult))
            link(nc.vector.tensor_scalar(t1, t1, -0.5 * STATE_SCALE, 1.5 * STATE_SCALE, ALU.mult, ALU.add))
            nc.vector.tensor_tensor(factor, t1, inv, ALU.mult).then_inc(self.factor_ready, 1)
            next(prep, None)
        dve.wait_ge(self.factor_ready, 2)
        dve.wait_ge(self.centre_ready, NT)
        for t in range(NT):
            dve.wait_ge(self.high, t + 1)
            nc.vector.scalar_tensor_tensor(self.sp[:, t, D:2 * D], self.centred[:, t, :], self.factor[:, t:t + 1],
                                           self.sp[:, t, 0:D], ALU.mult, ALU.subtract).then_inc(self.low, 1)
            if t >= 4 and t % 2 == 0:
                self.keep(dve, t - 3)
            if t == half:
                next(prep, None)
        self.keep(dve, NT - 3)
        self.keep(dve, NT - 1)
        for _ in prep:
            pass

    def scalar(self, act, prep=None):
        nc = self.nc
        half = NT // 2
        for g in range(2):
            cols = slice(half * g, half * (g + 1))
            act.wait_ge(self.var_ready, g + 1)
            nc.scalar.activation(self.dev[:, cols], self.var[:, cols], ACT.Sqrt).then_inc(self.dev_ready, 1)
            act.wait_ge(self.factor_ready, g + 1)
            act.wait_ge(self.centre_ready, half * (g + 1))
            for t in range(half * g, half * (g + 1)):
                nc.scalar.activation(self.sp[:, t, 0:D], self.centred[:, t, :], ACT.Copy,
                                     scale=self.factor[:, t:t + 1]).then_inc(self.high, 1)
                if g and t % 2 and t > half + 1:
                    self.keep(act, t - half - 3)
                if t == half + 3 and prep:
                    prep(act)
        for t in range(half - 2, NT, 2):
            self.keep(act, t)

    def keep(self, eng, t):
        eng.wait_ge(self.turned, t + 1)
        to = self.st[:, :, t * P:(t + 1) * P]
        turned = self.c.bank16(6 + t % 2)[:, 0:4 * P].rearrange("p (k i) -> p k i", i=P)
        if t % 2:
            self.nc.vector.tensor_copy(to, turned).then_inc(self.kept_dve, 1)
        else:
            self.nc.scalar.activation(to, turned, ACT.Copy).then_inc(self.kept_act, 1)

    def tensor(self, pe):
        for t in range(NT):
            pe.wait_ge(self.low, t + 1)
            pe.wait_ge(self.high, t + 1)
            if t >= 2:
                pe.wait_ge(self.kept_dve if t % 2 else self.kept_act, t // 2)
            for k in range(4):
                last = self.nc.tensor.transpose(self.c.bank16(6 + t % 2)[:, k * P:(k + 1) * P],
                                                self.sp[:, t, k * P:(k + 1) * P], self.c.ident[:, :])
            last.then_inc(self.turned, 1)

    def ready(self, pe):
        pe.wait_ge(self.kept_act, NT // 2)
        pe.wait_ge(self.kept_dve, NT // 2)


class Split:

    def __init__(self, c, name, w, hi, lo, top=WEIGHT_SCALE):
        self.c, self.nc, self.w, self.hi, self.lo = c, c.nc, w, hi, lo
        t = c.scales[:, c.splits, :]
        c.splits += 1
        self.top = top
        (self.own, self.all_, self.pow2, self.inv, self.scale, self.unscale, self.plain,
         self.half) = (t[:, k:k + 1] for k in range(8))
        sem = lambda n: c.sem(f"{name}_{n}")
        self.own_max, self.all_max, self.chain, self.scaled, self.high, self.low = (
            sem("own_max"), sem("all_max"), sem("chain"), sem("scaled"), sem("high"), sem("low"))

    def vector(self, dve):
        for _ in self.vector_steps(dve):
            pass

    def vector_steps(self, dve):
        nc = self.nc
        link = Chain(dve, self.chain)
        nc.vector.tensor_reduce(self.own, self.w, AX_X, ALU.max, apply_absolute_value=True).then_inc(self.own_max, 1)
        yield
        dve.wait_ge(self.all_max, 1)
        link(nc.vector.tensor_scalar(self.all_, self.all_, 1e-30, None, ALU.max))
        link(nc.vector.tensor_scalar(self.pow2.bitcast(U32), self.all_.bitcast(U32), 0x7F800000, None,
                                     ALU.bitwise_and))
        link(nc.vector.reciprocal(self.inv, self.pow2))
        link(nc.vector.tensor_scalar(self.unscale, self.pow2, 1.0 / (self.top * STATE_SCALE), None, ALU.mult))
        link(nc.vector.tensor_scalar(self.plain, self.pow2, 1.0 / self.top, None, ALU.mult))
        link(nc.vector.tensor_scalar(self.half, self.pow2, 0.5 / self.top, None, ALU.mult))
        nc.vector.tensor_scalar(self.scale, self.inv, self.top, None, ALU.mult).then_inc(self.scaled, 1)
        yield
        dve.wait_ge(self.scaled, 1)
        dve.wait_ge(self.high, 1)
        nc.vector.scalar_tensor_tensor(self.lo, self.w, self.scale, self.hi, ALU.mult, ALU.subtract).then_inc(self.low, 1)

    def gpsimd(self, pool):
        pool.wait_ge(self.own_max, 1)
        self.nc.gpsimd.partition_all_reduce(self.all_, self.own, P, RMAX).then_inc(self.all_max, 1)

    def scalar(self, act):
        act.wait_ge(self.scaled, 1)
        self.nc.scalar.activation(self.hi, self.w, ACT.Copy, scale=self.scale).then_inc(self.high, 1)

    def ready(self, eng):
        eng.wait_ge(self.high, 1)
        eng.wait_ge(self.low, 1)


PARTS3 = ((0, 0), (0, 1), (1, 0))


def attention_layer(c, S):
    nc, dram = c.nc, c.dram
    HX = D + 2 * H
    V = HD + 1
    a_cols = c.view(AT_AT, [NT, N], F8)
    x = c.view(AT_X, [NT, D], F32)
    F = AT_FREE
    hx = c.view(F, [NT, HX], F32)
    s_rep = c.view(F + 18 * KB, [2, N], F32)
    s_rows = c.view(F + 34 * KB, [N], F32)
    edges = c.view(F + 34 * KB, [4, N], F8)
    sums = c.view(F + 42 * KB, [NT, 2, 2, V], F32)
    both = c.view(F + 42 * KB + 8448, [NT, 2, V], F32)
    fbuf = c.view(F + 42 * KB + 8448 + 4224, [2, NT, 2, V], F32)
    fg = c.view(AT_SP, [2, NT, 3, 2, V], F16)
    total = c.view(AT_SP + 13 * KB, [NT, H, V], F32)
    W = AT_W
    w_rows = c.view(W, [FT, D], F32)
    b_rep = c.view(W + 2 * KB, [FT, P], F32)
    bias = c.view(W + 3 * KB, [HX], F32)
    a_blk = c.view(W + 3 * KB + 1088, [FT, 2 * H], F32)
    w32 = c.view(W + 5 * KB, [FT * HX], F32)
    whi = c.view(W + 8 * KB, [FT * HX], F16)
    wlo = c.view(W + 8 * KB + 1088, [FT * HX], F16)
    w32t = w32.rearrange("p (k n) -> p k n", n=HX)
    wp = [v.rearrange("p (k n) -> p k n", n=HX) for v in (whi, wlo)]
    b_col = c.view(W + 11 * KB, [FT], F32)
    mean_h = c.view(W + 11 * KB + 64, [H, V], F32)
    ones = c.view(W + 13 * KB, [P], F32)
    q = W + 14 * KB
    small = {}
    for n in ("ed", "eg", "es", "et", "neg_d", "u", "tmp", "rden"):
        small[n] = c.view(q, [NT, H], F32)
        q += 512
    nd2 = c.view(q, [2, NT], F32)
    empty = c.view(q + 128, [NT], F32)
    s_bias = c.view(q + 192, [1], F32)
    peak = c.view(q + 196, [H + 1], F32)
    peaks = c.view(q + 236, [H + 1], F32)
    hs = c.view(q + 276, [6], F32)
    h_pow, h_inv, h_scale, h_back, h_mean = (hs[:, k:k + 1] for k in range(5))
    et2 = c.view(q + 320, [NT, H, 2], F32)
    elu_made = c.sem("g_elu_made")
    h_peaks = c.view(q + 300, [4], F32)
    h_peaked = c.sem("g_h_peaked")
    v_all = c.view(F, [NT, H, HD], F32)
    e_all = c.view(F + 18 * KB, [NT, H, HD], F32)
    scratch = nc.dram_tensor("s_rows_dram", [H, N], F32, kind="Internal").ap()

    nodes = NodeValues(c, "n0", F + 18 * KB)
    split = Split(c, "w0", w32, whi, wlo)
    sem = lambda n: c.sem("g_" + n)
    w_loaded, a_loaded = sem("w_loaded"), sem("a_loaded")
    blk_zero, rep_made, wa_made, w_made, ba_made = sem("blk_zero"), sem("rep_made"), sem("wa_made"), sem("w_made"), sem("ba_made")
    ones_made = sem("ones_made")
    h_summed, h_kept, s_summed, s_kept = sem("h_summed"), sem("h_kept"), sem("s_summed"), sem("s_kept")
    s_stored, s_spread = sem("s_stored"), [sem("s_spread0"), sem("s_spread1")]
    peak_own, peak_all = sem("peak_own"), sem("peak_all")
    prep, exps, shifts = sem("prep"), sem("exps"), sem("shifts")
    mean_summed = sem("mean_summed")
    f_made, hi_made, lo_made = sem("f_made"), sem("hi_made"), sem("lo_made")
    edge_made, edge_free = sem("edge_made"), sem("edge_free")
    fg_used = sem("fg_used")
    evacuated = sem("evacuated")
    merged = sem("merged")
    nd_copied = sem("nd_copied")
    dchain, pchain = sem("dchain"), sem("pchain")
    tail = sem("tail")
    spilled, pattern_made = sem("spilled"), sem("pattern_made")
    S.parts_dram = nc.dram_tensor("parts_dram", [P, PARTS_BYTES // 4], F32, kind="Internal").ap()
    pe_steps, dve_steps = sem("pe_steps"), sem("dve_steps")
    POOLED = (2, 5, 10, 14)
    OWN = NT - len(POOLED)
    BANKS = -(-NT // 3)
    signs = c.view(W, [2, N], F16)
    pooled = c.view(W + 21 * KB, [2, N], F8)
    signed, rectified, pooled_made, pooled_free, nd_free = (
        sem(n) for n in ("signed", "rectified", "pooled_made", "pooled_free", "nd_free"))

    with nc.Block() as block:
        @block.sync
        def _(sp):
            sp.dma_start(w_rows, dram["L0_W"].rearrange("(t p) f -> p t f", p=P)).then_inc(w_loaded, 16)
            sp.dma_start(w32t[:, :, 0:D], dram["L0_WT"].rearrange("(t p) f -> p t f", p=P)).then_inc(w_loaded, 16)
            sp.dma_start(bias[:, 0:D], dram["L0_b"].partition_broadcast(P)).then_inc(w_loaded, 16)
            sp.dma_start(b_col, dram["L0_bcol"]).then_inc(w_loaded, 16)
            sp.wait_ge(blk_zero, 1)
            for h in range(H):
                lo = HD * (h % 4)
                sp.dma_start(a_blk[lo:lo + HD, h // 4, h:h + 1], dram["L0_a"][0:HD, :]).then_inc(a_loaded, 16)
                sp.dma_start(a_blk[lo:lo + HD, h // 4, H + h:H + h + 1], dram["L0_a"][HD:2 * HD, :]).then_inc(a_loaded, 16)
            sp.dma_start(S.parts_dram, S.weights.all).then_inc(spilled, 16)
            sp.wait_ge(s_kept, NC)
            sp.dma_start(scratch, s_rows[0:H, :]).then_inc(s_stored, 16)
            sp.wait_ge(s_stored, 16)
            for h in range(H):
                if h >= 2:
                    sp.wait_ge(edge_made, OWN * (h - 1))
                    sp.wait_ge(rectified, len(POOLED) * (h - 1))
                sp.dma_start(s_rep[:, h % 2, :], scratch[h, :].partition_broadcast(P)).then_inc(s_spread[h % 2], 16)
            sp.wait_ge(s_spread[0], 16 * (H // 2))
            sp.wait_ge(s_spread[1], 16 * (H // 2))

        @block.tensor
        def _(pe):
            pe.wait_ge(w_loaded, 64)
            pe.wait_ge(a_loaded, 16 * 2 * H)
            for k in range(FT):
                for o in range(FT):
                    last = nc.tensor.matmul(c.psum[:, 0, k * 2 * H:(k + 1) * 2 * H], w_rows[:, o, k * P:(k + 1) * P],
                                            a_blk[:, o, :], start=(o == 0), stop=(o == FT - 1))
            last.then_inc(wa_made, 1)
            pe.wait_ge(rep_made, FT)
            for o in range(FT):
                last = nc.tensor.matmul(c.psum[:, 1, 0:2 * H], b_rep[:, o, :], a_blk[:, o, :],
                                        start=(o == 0), stop=(o == FT - 1))
            for o in range(FT):
                last = nc.tensor.matmul(c.psum[0:H, 2, 0:1], a_blk[:, o, 0:H], b_col[:, o:o + 1],
                                        start=(o == 0), stop=(o == FT - 1))
            last.then_inc(ba_made, 1)
            nodes.tensor(pe)
            split.ready(pe)
            nodes.ready(pe)
            pe.wait_ge(w_made, 3)
            for j in range(NC):
                if j >= 2:
                    pe.wait_ge(s_kept, j - 1)
                n = 0
                for k in range(FT):
                    for a, b in PARTS3:
                        last = nc.tensor.matmul(c.psum[0:H, 4 + j % 2, :], wp[b][:, k, D:D + H],
                                                nodes.st[:, 2 * a + k, j * CH:(j + 1) * CH], start=(n == 0), stop=(n == 5))
                        n += 1
                last.then_inc(s_summed, 1)
            for t in range(NT):
                if t >= 4:
                    pe.wait_ge(h_kept, t - 3)
                n = 0
                for k in range(FT):
                    for a, b in PARTS3:
                        last = nc.tensor.matmul(c.psum[:, t % 4, 0:HX], nodes.st[:, 2 * a + k, t * P:(t + 1) * P],
                                                wp[b][:, k, :], start=(n == 0), stop=(n == 5))
                        n += 1
                last.then_inc(h_summed, 1)
            pe.wait_ge(h_kept, NT)
            pe.wait_ge(ones_made, 1)
            for t in range(NT):
                last = nc.tensor.matmul(c.psum[:, 6, 0:D], ones, hx[:, t, 0:D], start=(t == 0), stop=(t == NT - 1))
            last.then_inc(mean_summed, 1)
            pe.wait_ge(evacuated, BANKS)

            with pe.Fori(0, H // 2) as i:
                for u in range(2):
                    n = 2 * i + u
                    pe.wait_ge(hi_made, n + 1)
                    pe.wait_ge(lo_made, n + 3)
                    for j in range(NT):
                        if j in POOLED:
                            m = POOLED.index(j)
                            buffer, used = pooled[:, m % 2, :], pooled_free
                            pe.wait_ge(pooled_made, len(POOLED) * n + m + 1)
                        else:
                            m = j - sum(q < j for q in POOLED)
                            buffer, used = edges[:, m % 4, :], edge_free
                            pe.wait_ge(edge_made, OWN * n + m + 1)
                        pe.sem_inc(pe_steps)
                        for t in range(NT):
                            if j == 0 and t % 3 == 0:
                                pe.wait_ge(evacuated, BANKS * n + t // 3 + 1)
                                pe.sem_inc(pe_steps)
                            o = c.psum[:, t // 3, 4 * V * (t % 3):4 * V * (t % 3 + 1)]
                            mm = nc.tensor.matmul(o, buffer[:, t * P:(t + 1) * P],
                                                  fg[:, u, j, 0:2, :, :].rearrange("p a b v -> p (a b v)"),
                                                  start=(j == 0 and t % 3 == 0), stop=(j == NT - 1), skip_group_check=True)
                            if t == NT - 1:
                                mm.then_inc(used, 1)
                            last = nc.tensor.matmul(o[:, 2 * V:4 * V], a_cols[:, j, t * P:(t + 1) * P],
                                                    fg[:, u, j, 2, :, :].rearrange("p b v -> p (b v)"),
                                                    start=False, stop=(j == NT - 1), skip_group_check=True)
                    last.then_inc(fg_used, 1)

        @block.vector
        def _(dve):
            link = Chain(dve, dchain)
            nc.vector.memset(ones, 1.0).then_inc(ones_made, 1)
            dve.sem_inc(edge_free, 4)
            dve.sem_inc(lo_made, 2)
            dve.sem_inc(nd_free, 1)
            nc.vector.memset(a_blk, 0.0).then_inc(blk_zero, 1)
            nc.vector.memset(c.pattern[:, :], 0.0).then_inc(pattern_made, 1)
            dve.wait_ge(pattern_made, 1)
            nc.vector.memset(c.pattern[:, 1:34:32], 1.0).then_inc(pattern_made, 1)

            def prepare():
                dve.wait_ge(w_loaded, 64)
                for o in range(FT):
                    nc.vector.tensor_copy(b_rep[:, o, :], b_col[:, o:o + 1].broadcast_to([P, P])).then_inc(rep_made, 1)
                dve.wait_ge(wa_made, 1)
                nc.vector.tensor_copy(w32t[:, :, D:HX], c.psum[:, 0, 0:4 * H].rearrange("p (k n) -> p k n", k=FT)
                                      ).then_inc(w_made, 1)
                dve.wait_ge(w_made, 1)
                steps = split.vector_steps(dve)
                next(steps)
                yield
                dve.wait_ge(ba_made, 1)
                nc.vector.tensor_copy(bias[:, D:HX], c.psum[:, 1, 0:2 * H]).then_inc(w_made, 1)
                nc.vector.tensor_copy(s_bias[0:H, :], c.psum[0:H, 2, 0:1]).then_inc(w_made, 1)
                yield from steps

            nodes.vector(dve, prepare())
            dve.wait_ge(w_made, 3)
            nc.vector.tensor_scalar(empty, S.degree[:, :], 0.0, None, ALU.is_equal).then_inc(tail, 1)
            for t in range(NT):
                dve.wait_ge(h_summed, t + 1)
                nc.vector.scalar_tensor_tensor(hx[:, t, :], c.psum[:, t % 4, 0:HX], split.unscale, bias,
                                               ALU.mult, ALU.add).then_inc(h_kept, 1)
                if t % 4 == 3:
                    dve.wait_ge(h_kept, t + 1)
                    nc.vector.tensor_reduce(h_peaks[:, t // 4:t // 4 + 1], hx[:, t - 3:t + 1, 0:D], mybir.AxisListType.XY,
                                            ALU.max, apply_absolute_value=True).then_inc(h_peaked, 1)
            dve.wait_ge(h_peaked, NT // 4)
            s_all, d_all = hx[:, :, D:D + H], hx[:, :, D + H:HX]
            link(nc.vector.tensor_reduce(peak[:, H:H + 1], h_peaks, AX_X, ALU.max))
            nc.vector.tensor_reduce(peak[:, 0:H], d_all.rearrange("p t h -> p h t"), AX_X, ALU.max).then_inc(peak_own, 1)
            link(nc.vector.tensor_scalar(small["neg_d"], d_all, -1.0, None, ALU.mult))
            dve.wait_ge(peak_all, 1)
            top = peaks[:, 0:H].unsqueeze(1).broadcast_to([P, NT, H])
            link(nc.vector.tensor_tensor(small["u"], s_all, top, ALU.add))
            link(nc.vector.tensor_scalar(small["es"], small["u"], 0.8, 0.0, ALU.mult, ALU.min))
            link(nc.vector.tensor_scalar(small["et"], small["u"], -0.8, 0.0, ALU.mult, ALU.min))
            nc.vector.tensor_tensor(small["tmp"], d_all, top, ALU.subtract).then_inc(shifts, 1)
            link(nc.vector.tensor_scalar(peaks[:, H:H + 1], peaks[:, H:H + 1], 1e-30, None, ALU.max))
            link(nc.vector.tensor_scalar(h_pow.bitcast(U32), peaks[:, H:H + 1].bitcast(U32), 0x7F800000, None, ALU.bitwise_and))
            link(nc.vector.reciprocal(h_inv, h_pow))
            link(nc.vector.tensor_scalar(h_scale, h_inv, WEIGHT_SCALE, None, ALU.mult))
            link(nc.vector.tensor_scalar(h_back, h_pow, 1.0, None, ALU.mult))
            link(nc.vector.tensor_scalar(h_mean, h_scale, 1.0 / N, None, ALU.mult))
            dve.wait_ge(exps, 4)

            def make_f(n, u):
                for g, e in enumerate(("ed", "eg")):
                    col = small[e][:, :, bass.ds(n, 1)]
                    nc.vector.scalar_tensor_tensor(fbuf[:, u, :, g, 0:HD], hx[:, :, bass.ds(n * HD, HD)], h_scale,
                                                   col.broadcast_to([P, NT, HD]), ALU.mult, ALU.mult).then_inc(f_made, 1)
                    nc.vector.tensor_scalar(fbuf[:, u, :, g, HD:V], col, WEIGHT_SCALE, None, ALU.mult).then_inc(f_made, 1)
                nc.vector.tensor_copy(nd2[:, u, :], small["neg_d"][:, :, bass.ds(n, 1)].rearrange("p t a -> p (t a)")
                                      ).then_inc(nd_copied, 1)

            def head(i, u, more):
                n = 2 * i + u
                dve.wait_ge(nd_copied, n + 1)
                dve.wait_ge(s_spread[u], 16 * i + 16)
                for m, j in enumerate(j for j in range(NT) if j not in POOLED):
                    if more and m == 6:
                        dve.wait_ge(lo_made, n + 2)
                        dve.wait_ge(nd_free, n + 1)
                        make_f(n + 1, 1 - u)
                    dve.wait_ge(edge_free, OWN * n + m + 1)
                    dve.sem_inc(dve_steps)
                    nc.vector.scalar_tensor_tensor(edges[:, m % 4, :], s_rep[:, u, :], nd2[:, u, j:j + 1],
                                                   a_cols[:, j, :], ALU.is_gt, ALU.mult, saturate=False).then_inc(edge_made, 1)

            make_f(0, 0)
            with dve.Fori(0, H // 2 - 1) as i:
                head(i, 0, True)
                head(i, 1, True)
            head(H // 2 - 1, 0, True)
            head(H // 2 - 1, 1, False)
            dve.wait_ge(mean_summed, 1)
            nc.vector.tensor_scalar(mean_h[:, :, 0:HD], c.psum[:, 6, 0:D].rearrange("p (h v) -> p h v", v=HD),
                                    h_mean, None, ALU.mult).then_inc(prep, 1)
            nc.vector.memset(mean_h[:, :, HD:V], WEIGHT_SCALE).then_inc(prep, 1)
            dve.wait_ge(prep, 2)

            def divide(g):
                ts, done = slice(4 * g, 4 * g + 4), 1 + 6 * g
                dve.wait_ge(merged, 3 * (H - 1) + 3 * (g + 1))
                for t in range(4 * g, 4 * g + 4):
                    flat = total[:, t].rearrange("p h v -> p (h v)")
                    nc.vector.scalar_tensor_tensor(flat, mean_h.rearrange("p h v -> p (h v)"), empty[:, t:t + 1],
                                                   flat, ALU.mult, ALU.add).then_inc(tail, 1)
                dve.wait_ge(tail, done + 4)
                rden = small["rden"][:, ts, :]
                link(nc.vector.reciprocal(rden, total[:, ts, :, HD]))
                link(nc.vector.tensor_scalar(rden, rden, h_back, None, ALU.mult))
                nc.vector.tensor_tensor(v_all[:, ts], total[:, ts, :, 0:HD],
                                        rden.unsqueeze(3).broadcast_to([P, 4, H, HD]), ALU.mult).then_inc(tail, 1)
                dve.wait_ge(tail, done + 5)
                nc.vector.tensor_scalar(e_all[:, ts], v_all[:, ts], 0.0, None, ALU.min).then_inc(tail, 1)

            def elu(g):
                ts = slice(4 * g, 4 * g + 4)
                dve.wait_ge(exps, 4 + 2 * (g + 1))
                nc.vector.scalar_tensor_tensor(v_all[:, ts], v_all[:, ts], 0.0, e_all[:, ts], ALU.max, ALU.add
                                               ).then_inc(elu_made, 1)

            for g in range(NT // 4):
                divide(g)
                if g:
                    elu(g - 1)
            elu(NT // 4 - 1)

        @block.gpsimd
        def _(pool):
            link = Chain(pool, pchain)
            split.gpsimd(pool)
            pool.wait_ge(peak_own, 1)
            nc.gpsimd.partition_all_reduce(peaks, peak, P, RMAX).then_inc(peak_all, 1)
            pool.wait_ge(exps, 4)
            link(nc.gpsimd.tensor_copy(et2[:, :, :, 0], small["es"]))
            link(nc.gpsimd.tensor_copy(et2[:, :, :, 1], small["et"]))
            def parts(n, u):
                pool.wait_ge(f_made, 4 * n + 4)
                pool.wait_ge(hi_made, n + 1)
                f, g = fbuf[:, u, :, 0, :], fbuf[:, u, :, 1, :]
                nc.gpsimd.tensor_tensor(fg[:, u, :, 0, 1, :], f, fg[:, u, :, 0, 0, :], ALU.subtract)
                nc.gpsimd.tensor_tensor(fg[:, u, :, 1, 1, :], fg[:, u, :, 2, 0, :], g, ALU.subtract)
                nc.gpsimd.tensor_tensor(fg[:, u, :, 2, 1, :], g, fg[:, u, :, 2, 0, :], ALU.subtract).then_inc(lo_made, 1)

            def merge(n, first=0, tiles=NT, done=0):
                at, count = slice(first, first + tiles), 3 * (n + done)
                if count:
                    pool.wait_ge(merged, count)
                pool.wait_ge(evacuated, BANKS * (n + 1) + -(-(first + tiles) // 3))
                nc.gpsimd.tensor_tensor(both[:, at], sums[:, at, :, 0, :], sums[:, at, :, 1, :], ALU.add).then_inc(merged, 1)
                pool.wait_ge(merged, count + 1)
                nc.gpsimd.tensor_tensor(both[:, at], both[:, at], et2[:, at, n, :].unsqueeze(3)
                                        .broadcast_to([P, tiles, 2, V]), ALU.mult).then_inc(merged, 1)
                pool.wait_ge(merged, count + 2)
                nc.gpsimd.tensor_tensor(total[:, at, n, :], both[:, at, 0, :], both[:, at, 1, :], ALU.add).then_inc(merged, 1)

            def edges_of(n, m):
                k = len(POOLED) * n + m
                pool.wait_ge(rectified, k + 1)
                if k >= 2:
                    pool.wait_ge(pooled_free, k - 1)
                nc.gpsimd.tensor_tensor(pooled[:, m % 2, :], signs[:, m % 2, :], a_cols[:, POOLED[m], :], ALU.mult,
                                        saturate=False).then_inc(pooled_made, 1)

            parts(0, 0)
            for n in range(H):
                edges_of(n, 0)
                edges_of(n, 1)
                if n:
                    merge(n - 1)
                edges_of(n, 2)
                if n + 1 < H:
                    parts(n + 1, (n + 1) % 2)
                edges_of(n, 3)
            for g in range(NT // 4):
                merge(H - 1, 4 * g, 4, g)
            for g in range(NT // 4):
                pool.wait_ge(elu_made, g + 1)
                xg = x[:, 4 * g:4 * g + 4].rearrange("p t f -> p (t f)")
                nc.gpsimd.tensor_tensor(xg, v_all[:, 4 * g:4 * g + 4].rearrange("p t h v -> p (t h v)"), xg, ALU.add)

        @block.scalar
        def _(act):
            nodes.scalar(act, split.scalar)
            act.wait_ge(w_made, 3)
            act.wait_ge(spilled, 16)
            for j in range(NC):
                act.wait_ge(s_summed, j + 1)
                nc.scalar.activation(s_rows[0:H, j * CH:(j + 1) * CH], c.psum[0:H, 4 + j % 2, :], ACT.Identity,
                                     bias=s_bias[0:H, :], scale=split.unscale[0:H, :]).then_inc(s_kept, 1)
            act.wait_ge(shifts, 1)
            nc.scalar.activation(small["ed"], small["tmp"], ACT.Exp).then_inc(exps, 1)
            nc.scalar.activation(small["eg"], small["tmp"], ACT.Exp, scale=0.2).then_inc(exps, 1)
            nc.scalar.activation(small["es"], small["es"], ACT.Exp).then_inc(exps, 1)
            nc.scalar.activation(small["et"], small["et"], ACT.Exp).then_inc(exps, 1)
            act.wait_ge(exps, 4)
            act.sem_inc(evacuated, BANKS)

            def high(n, u):
                act.wait_ge(f_made, 4 * n + 4)
                f, g = fbuf[:, u, :, 0, :], fbuf[:, u, :, 1, :]
                nc.scalar.activation(fg[:, u, :, 0, 0, :], f, ACT.Copy)
                nc.scalar.activation(fg[:, u, :, 1, 0, :], g, ACT.Copy, scale=-1.0)
                nc.scalar.activation(fg[:, u, :, 2, 0, :], g, ACT.Copy).then_inc(hi_made, 1)

            def evacuate(n):
                act.wait_ge(fg_used, n + 1)
                if n:
                    act.wait_ge(merged, 3 * n - 2)
                for b in range(BANKS):
                    k = min(3, NT - 3 * b)
                    nc.scalar.activation(sums[:, 3 * b:3 * b + k, :, :, :].rearrange("p t g a v -> p (t g a v)"),
                                         c.psum[:, b, 0:4 * V * k], ACT.Copy).then_inc(evacuated, 1)

            def marks(n, m):
                k = len(POOLED) * n + m
                if m == 0:
                    act.wait_ge(nd_copied, n + 1)
                    act.wait_ge(s_spread[n % 2], 16 * (n // 2) + 16)
                if k >= 2:
                    act.wait_ge(pooled_made, k - 1)
                nc.scalar.activation(signs[:, m % 2, :], s_rep[:, n % 2, :], ACT.Sign, scale=-1.0,
                                     bias=nd2[:, n % 2, POOLED[m]:POOLED[m] + 1]).then_inc(signed, 1)
                act.wait_ge(signed, k + 1)
                if m == len(POOLED) - 1:
                    act.sem_inc(nd_free, 1)
                nc.scalar.activation(signs[:, m % 2, :], signs[:, m % 2, :], ACT.Relu, scale=-1.0).then_inc(rectified, 1)

            act.wait_ge(h_kept, NT)
            high(0, 0)
            for n in range(H):
                marks(n, 0)
                marks(n, 1)
                if n:
                    evacuate(n - 1)
                marks(n, 2)
                if n + 1 < H:
                    high(n + 1, (n + 1) % 2)
                marks(n, 3)
            evacuate(H - 1)
            for g in range(NT // 4):
                act.wait_ge(tail, 1 + 6 * (g + 1))
                e = e_all[:, 4 * g:4 * g + 4].rearrange("p t h v -> p (t h v)")
                nc.scalar.activation(e, e, ACT.Exp).then_inc(exps, 1)
                act.wait_ge(exps, 4 + 2 * g + 1)
                nc.scalar.activation(e, e, ACT.Copy, bias=-1.0).then_inc(exps, 1)


class DegreeRows:

    def __init__(self, c, name, chunks, bank):
        self.c, self.nc, self.chunks, self.bank = c, c.nc, chunks, bank
        self.rows = c.view(AT_DEG, [N], F16)
        self.adjacency = c.view(AT_AT, [NT, N], F8), c.view(AT_A, [NT, N], F8)
        self.made, self.kept = c.sem(f"{name}_deg_made"), c.sem(f"{name}_deg_kept")

    def tensor(self, pe):
        for n, j in enumerate(self.chunks):
            for m, adj in enumerate(self.adjacency):
                for t in range(NT):
                    mm = self.nc.tensor.matmul(self.c.psum[0:34, self.bank + n, :], self.c.pattern[:, 1 - m:35 - m],
                                               adj[:, t, j * CH:(j + 1) * CH], start=(m == 0 and t == 0),
                                               stop=(m == 1 and t == NT - 1))
            mm.then_inc(self.made, 1)

    def scalar(self, act):
        for n, j in enumerate(self.chunks):
            act.wait_ge(self.made, n + 1)
            self.nc.scalar.activation(self.rows[0:34, j * CH:(j + 1) * CH], self.c.psum[0:34, self.bank + n, :], ACT.Copy
                                      ).then_inc(self.kept, 1)


def neighbour_sums(nc, c, pe, values, moving, banks, chunk, tiles, signal):
    for b, bank in enumerate(banks):
        for j in tiles:
            for part in range(2):
                k = part * FT + b % FT
                mm = nc.tensor.matmul(c.psum[:, bank, :], values[:, j, k * P:(k + 1) * P],
                                      moving[b // FT][:, j, chunk * CH:(chunk + 1) * CH],
                                      start=(j == 0 and part == 0), stop=(j == NT - 1 and part == 1))
        if tiles[-1] == NT - 1:
            mm.then_inc(signal, 1)


def mean_layer(c, S):
    nc, dram = c.nc, c.dram
    a_cols = c.view(AT_AT, [NT, N], F8)
    x = c.view(AT_X, [NT, D], F32)
    F, W = AT_FREE, AT_FREE + 31 * KB
    nodes = NodeValues(c, "n1", F)
    mid = c.view(W, [2, FT, D], F32)
    comb = c.view(W + 4 * KB, [2 * FT, D], F32)
    v32 = c.view(W + 8 * KB, [4 * D], F32)
    vhi, vlo = c.view(W + 12 * KB, [4 * D], F16), c.view(W + 14 * KB, [4 * D], F16)
    vp = [v.rearrange("p (k n) -> p k n", n=D) for v in (vhi, vlo)]
    b_rep = c.view(W + 16 * KB, [4, P], F32)
    b_col = c.view(W + 18 * KB, [4], F32)
    bias = c.view(W + 18 * KB + 64, [D], F32)
    r_deg = c.view(W + 20 * KB, [NT], F32)
    sums = c.view(F + 18 * KB, [2, FT, 2, CH], F16)
    y = c.view(F + 26 * KB, [2, D], F32)
    split = Split(c, "w1", v32, vhi, vlo)
    degrees = DegreeRows(c, "m", (0, 1), 2)
    sem = lambda n: c.sem("m_" + n)
    w_loaded, rep_made, v_made, v_kept, bias_made, bias_kept = (
        sem("w_loaded"), sem("rep_made"), sem("v_made"), sem("v_kept"), sem("bias_made"), sem("bias_kept"))
    deg_ready, summed, high, low = sem("deg_ready"), sem("summed"), sem("high"), sem("low")
    reloaded = sem("reloaded")
    S.weights.place(AT_W)
    out_made, y_made, x_made, chain = sem("out_made"), sem("y_made"), sem("x_made"), sem("chain")

    with nc.Block() as block:
        @block.sync
        def _(sp):
            for m, name in enumerate(("L1_WsT", "L1_WnT")):
                sp.dma_start(mid[:, m], dram[name].rearrange("(t p) f -> p t f", p=P)).then_inc(w_loaded, 16)
            sp.dma_start(comb, dram["L1_Wc"].rearrange("(t p) f -> p t f", p=P)).then_inc(w_loaded, 16)
            for m, name in enumerate(("L1_bs", "L1_bn")):
                sp.dma_start(b_col[:, FT * m:FT * (m + 1)], dram[name]).then_inc(w_loaded, 16)
            sp.dma_start(bias, dram["L1_bc"].partition_broadcast(P)).then_inc(w_loaded, 16)
            sp.dma_start(S.weights.all, S.parts_dram).then_inc(reloaded, 16)
            sp.wait_ge(reloaded, 16)

        @block.tensor
        def _(pe):
            degrees.tensor(pe)
            nodes.tensor(pe)
            nodes.ready(pe)

            def sums_of(j):
                banks = [2 * (j % 2), 2 * (j % 2) + 1]
                if j >= 2:
                    pe.wait_ge(low, 2 * (j - 1))
                neighbour_sums(nc, c, pe, nodes.sp, [a_cols], banks, j, list(range(NT)), summed)

            def outputs(j):
                pe.wait_ge(high, 2 * (j + 1))
                pe.wait_ge(low, 2 * (j + 1))
                for q in range(CH // P):
                    t = j * (CH // P) + q
                    if t >= 2:
                        pe.wait_ge(x_made, t - 1)
                    for m in range(2):
                        n = 0
                        for k in range(FT):
                            for a, b in PARTS3:
                                st = (nodes.st[:, 2 * a + k, t * P:(t + 1) * P] if m == 0 else
                                      sums[:, j % 2, k, a, q * P:(q + 1) * P])
                                mm = nc.tensor.matmul(c.psum[:, 4 + t % 2, m * D:(m + 1) * D], st, vp[b][:, FT * m + k, :],
                                                      start=(n == 0), stop=(n == 5))
                                n += 1
                    mm.then_inc(out_made, 1)

            sums_of(0)
            pe.wait_ge(w_loaded, 96)
            for m in range(2):
                for k in range(FT):
                    for o in range(FT):
                        mm = nc.tensor.matmul(c.psum[:, 5 + m, k * D:(k + 1) * D], mid[:, m, o, k * P:(k + 1) * P],
                                              comb[:, FT * m + o, :], start=(o == 0), stop=(o == FT - 1))
            mm.then_inc(v_made, 1)
            pe.wait_ge(rep_made, 4)
            for k in range(4):
                mm = nc.tensor.matmul(c.psum[:, 7, 0:D], b_rep[:, k, :], comb[:, k, :], start=(k == 0), stop=(k == 3))
            mm.then_inc(bias_made, 1)
            pe.wait_ge(degrees.kept, 2)
            sums_of(1)
            pe.wait_ge(v_kept, 1)
            pe.wait_ge(bias_kept, 1)
            split.ready(pe)
            for j in range(NC):
                if j and j + 1 < NC:
                    sums_of(j + 1)
                outputs(j)

        @block.vector
        def _(dve):
            link = Chain(dve, chain)
            nodes.vector(dve)

            def low_parts(j):
                for b in range(FT):
                    dve.wait_ge(high, 2 * j + b + 1)
                    nc.vector.scalar_tensor_tensor(sums[:, j % 2, b, 1, :], c.psum[:, 2 * (j % 2) + b, :], 1.0 / STATE_SCALE,
                                                   sums[:, j % 2, b, 0, :], ALU.mult, ALU.subtract).then_inc(low, 1)

            dve.wait_ge(w_loaded, 96)
            for k in range(4):
                nc.vector.tensor_copy(b_rep[:, k, :], b_col[:, k:k + 1].broadcast_to([P, P])).then_inc(rep_made, 1)
            dve.wait_ge(v_made, 1)
            nc.vector.tensor_copy(v32, c.psum[:, 5:7, :].rearrange("p b n -> p (b n)")).then_inc(v_kept, 1)
            dve.wait_ge(v_kept, 1)
            split.vector(dve)
            dve.wait_ge(bias_made, 1)
            nc.vector.tensor_tensor(bias, c.psum[:, 7, 0:D], bias, ALU.add).then_inc(bias_kept, 1)
            link(nc.vector.tensor_scalar(r_deg, S.degree[:, :], 1.0, None, ALU.max))
            link(nc.vector.reciprocal(r_deg, r_deg))
            nc.vector.tensor_scalar(r_deg, r_deg, split.plain, None, ALU.mult).then_inc(deg_ready, 1)
            dve.wait_ge(bias_kept, 1)
            dve.wait_ge(deg_ready, 1)
            low_parts(0)
            for j in range(NC):
                if j + 1 < NC:
                    low_parts(j + 1)
                for q in range(CH // P):
                    t = j * (CH // P) + q
                    dve.wait_ge(out_made, t + 1)
                    if t >= 2:
                        dve.wait_ge(x_made, t - 1)
                    nc.vector.scalar_tensor_tensor(y[:, t % 2, :], c.psum[:, 4 + t % 2, 0:D], split.unscale, bias,
                                                   ALU.mult, ALU.add).then_inc(y_made, 1)
                    dve.wait_ge(y_made, 2 * t + 1)
                    nc.vector.scalar_tensor_tensor(y[:, t % 2, :], c.psum[:, 4 + t % 2, D:2 * D], r_deg[:, t:t + 1],
                                                   y[:, t % 2, :], ALU.mult, ALU.add).then_inc(y_made, 1)
                    dve.wait_ge(y_made, 2 * t + 2)
                    nc.vector.scalar_tensor_tensor(x[:, t, :], y[:, t % 2, :], 0.0, x[:, t, :], ALU.max,
                                                   ALU.add).then_inc(x_made, 1)

        @block.gpsimd
        def _(pool):
            split.gpsimd(pool)

        @block.scalar
        def _(act):
            nodes.scalar(act)
            degrees.scalar(act)
            split.scalar(act)
            for j in range(NC):
                for b in range(FT):
                    act.wait_ge(summed, 2 * j + b + 1)
                    if j >= 2:
                        act.wait_ge(out_made, (CH // P) * (j - 1))
                    nc.scalar.activation(sums[:, j % 2, b, 0, :], c.psum[:, 2 * (j % 2) + b, :], ACT.Copy,
                                         scale=1.0 / STATE_SCALE).then_inc(high, 1)


class GatedWeights:
    G3, KT, TOP = 3 * D, 3 * FT, 16384.0

    def __init__(self, c, S):
        self.c, self.nc = c, c.nc
        self.NM = NM = (self.KT + 1) * self.G3
        F = AT_FREE
        self.place(F + 36 * KB)
        self.m32 = c.view(F, [NM], F32)
        self.m32t = self.m32.rearrange("p (k n) -> p k n", n=self.G3)
        self.wg = c.view(AT_W, [self.KT, self.G3], F32)
        self.io = c.view(AT_W + 18 * KB, [2, FT, D], F32)
        self.o32 = c.view(AT_W + 22 * KB, [2 * FT * D], F32)
        self.io_b = c.view(AT_W + 26 * KB, [2 * FT, 34], F32)
        self.io_col = c.view(AT_W + 26 * KB + 544, [2 * FT], F32)
        self.split = Split(c, "w2", self.m32, self.m_hi, self.m_lo, self.TOP)
        self.osplit = Split(c, "w3", self.o32, self.o_hi, self.o_lo)
        sem = lambda n: c.sem("gw_" + n)
        (self.loaded, self.io_zero, self.io_made, self.m_made, self.m_kept, self.uv_made, self.uv_kept, self.uv_zero,
         self.uv_set) = (sem(n) for n in ("loaded", "io_zero", "io_made", "m_made", "m_kept", "uv_made", "uv_kept",
                                          "uv_zero", "uv_set"))

    def place(self, at):
        c = self.c
        self.m_hi, self.m_lo = c.view(at, [self.NM], F16), c.view(at + 10752, [self.NM], F16)
        self.o_hi, self.o_lo = c.view(at + 21504, [2 * FT * D], F16), c.view(at + 23552, [2 * FT * D], F16)
        self.uv = c.view(at + 25600, [self.G3], F16)
        self.all = c.view(at, [PARTS_BYTES // 4], F32)
        self.mp = [v.rearrange("p (k n) -> p k n", n=self.G3) for v in (self.m_hi, self.m_lo)]
        self.op = [v.rearrange("p (k n) -> p k n", n=D) for v in (self.o_hi, self.o_lo)]

    def sync(self, sp):
        dram = self.c.dram
        for m, name in enumerate(("L2_in_W", "L2_out_W")):
            sp.dma_start(self.io[:, m], dram[name].rearrange("(t p) f -> p t f", p=P)).then_inc(self.loaded, 16)
        sp.dma_start(self.wg, dram["L2_WgT"].rearrange("(t p) n -> p t n", p=P)).then_inc(self.loaded, 16)
        for m, name in enumerate(("L2_o1T", "L2_o2T")):
            sp.dma_start(self.o32.rearrange("p (m t f) -> p m t f", m=2, f=D)[:, m],
                         dram[name].rearrange("(t p) f -> p t f", p=P)).then_inc(self.loaded, 16)
        sp.dma_start(self.io_col, dram["L2_iobcol"]).then_inc(self.loaded, 16)

    def tensor(self, pe):
        nc, c, n = self.nc, self.c, 0
        pe.wait_ge(self.loaded, 96)
        for m in range(2):
            for k in range(FT):
                for g in range(3):
                    if n >= 3:
                        pe.wait_ge(self.m_kept, n - 2)
                    for o in range(FT):
                        mm = nc.tensor.matmul(c.psum[:, 4 + n % 3, 0:D], self.io[:, m, o, k * P:(k + 1) * P],
                                              self.wg[:, FT * m + o, g * D:(g + 1) * D], start=(o == 0), stop=(o == FT - 1))
                    mm.then_inc(self.m_made, 1)
                    n += 1
                yield
        pe.wait_ge(self.io_made, 8)
        pe.wait_ge(self.m_kept, 12)
        for g in range(3):
            for k in range(2 * FT):
                mm = nc.tensor.matmul(c.psum[0:34, 4 + g, 0:D], self.io_b[:, k, :], self.wg[:, k, g * D:(g + 1) * D],
                                      start=(k == 0), stop=(k == 2 * FT - 1))
        mm.then_inc(self.uv_made, 1)

    def vector(self, dve):
        nc, c, n = self.nc, self.c, 0
        nc.vector.memset(self.io_b, 0.0).then_inc(self.io_zero, 1)
        nc.vector.memset(self.uv, 0.0).then_inc(self.uv_zero, 1)
        nc.vector.memset(self.m32t[:, self.KT, :], 0.0).then_inc(self.uv_zero, 1)
        dve.wait_ge(self.io_zero, 1)
        dve.wait_ge(self.loaded, 96)
        for m in range(2):
            for k in range(FT):
                for at in (0, 32):
                    nc.vector.tensor_copy(self.io_b[:, FT * m + k, at + m:at + m + 1],
                                          self.io_col[:, FT * m + k:FT * m + k + 1]).then_inc(self.io_made, 1)
        nc.vector.tensor_scalar(self.m32t[:, 2 * FT:self.KT, :], self.wg[:, 2 * FT:self.KT, :], 1.0 / STATE_SCALE, None,
                                ALU.mult).then_inc(self.uv_zero, 1)
        yield
        for m in range(2):
            for k in range(FT):
                for g in range(3):
                    dve.wait_ge(self.m_made, n + 1)
                    nc.vector.tensor_copy(self.m32t[:, FT * m + k, g * D:(g + 1) * D], c.psum[:, 4 + n % 3, 0:D]
                                          ).then_inc(self.m_kept, 1)
                    n += 1
                yield
        dve.wait_ge(self.uv_made, 1)
        dve.wait_ge(self.uv_zero, 3)
        nc.vector.tensor_copy(self.m32t[0:34, self.KT, :].rearrange("p (g n) -> p g n", n=D), c.psum[0:34, 4:7, 0:D]
                              ).then_inc(self.uv_kept, 1)
        dve.wait_ge(self.uv_kept, 1)
        dve.wait_ge(self.m_kept, 12)
        yield from self.split.vector_steps(dve)
        dve.wait_ge(self.split.low, 1)
        nc.vector.tensor_copy(self.uv[0:32, :], self.mp[0][0:32, self.KT, :]).then_inc(self.uv_set, 1)
        nc.vector.tensor_copy(self.uv[32:64, :], self.mp[1][32:64, self.KT, :]).then_inc(self.uv_set, 1)
        yield
        yield from self.osplit.vector_steps(dve)
        dve.wait_ge(self.osplit.low, 1)
        dve.wait_ge(self.uv_set, 2)

    def scalar(self, act):
        for k in range(9):
            yield
        self.split.scalar(act)
        yield
        yield
        yield
        self.osplit.scalar(act)


def gated_layer(c, S):
    nc, dram = c.nc, c.dram
    G3 = 3 * D
    GT = G3 // P
    KT = 3 * FT
    a_rows, a_cols = c.view(AT_A, [NT, N], F8), c.view(AT_AT, [NT, N], F8)
    x = c.view(AT_X, [NT, D], F32)
    F, W = AT_FREE, AT_W
    weights = S.weights
    mp, op, uv, split, osplit = weights.mp, weights.op, weights.uv, weights.split, weights.osplit
    g_bias = c.view(W + 27136, [GT], F32)
    h_bias = c.view(W + 27168, [GT], F32)
    o1_bias = c.view(W + 27200, [FT], F32)
    deg_rows = c.view(AT_DEG, [N], F16)
    nodes = NodeValues(c, "n2", F + 21 * KB)
    st, sp_ = nodes.st, nodes.sp
    X = c.view(F, [2, 2, FT, 2, CH], F16)
    rs = c.view(F + 16 * KB, [FT, 2, CH], F16)
    s32 = c.view(F + 20 * KB, [FT, CH], F32)
    tr, tz, th, p32 = (c.view(F + (24 + 4 * k) * KB, [FT, CH], F32) for k in range(4))
    t32, tp = ([c.view(F + at * KB + 4 * k * KB, shape, dt) for at in (40, 52)]
               for k, shape, dt in ((0, [FT, CH], F32), (1, [FT, 2, CH], F16)))
    o2_bias = c.view(F + 48 * KB + 256, [D], F32)
    y = c.view(F + 50 * KB, [2, D], F32)

    degrees = DegreeRows(c, "r", (2, 3), 4)
    sem = lambda n: c.sem("r_" + n)
    b_loaded = sem("b_loaded")
    biases, steps_pe = sem("biases"), sem("steps_pe")
    summed, x_high, x_low = sem("summed"), sem("x_high"), sem("x_low")
    gate_done, gate_read = sem("gate_done"), sem("gate_read")
    s_made, p_made, rs_high, rs_low, d_made, e_made, new_made, st_high, st_low = (
        sem(n) for n in ("s_made", "p_made", "rs_high", "rs_low", "d_made", "e_made", "new_made", "st_high", "st_low"))
    turned, sp_kept = sem("turned"), sem("sp_kept")
    o_made, t_made, t_high, t_low, y_summed, y_made, x_made = (
        sem(n) for n in ("o_made", "t_made", "t_high", "t_low", "y_summed", "y_made", "x_made"))
    CB, GB, TB = 2 * FT, 4, 7
    TURNS = ({}, {}, {1: (0, 0), 2: (0, 1), 3: (1, 0)}, {0: (1, 1), 2: (2, 0), 3: (2, 1)})
    HB = (TB, 0)

    with nc.Block() as block:
        @block.sync
        def _(sp):
            sp.dma_start(g_bias, dram["L2_gbcol"]).then_inc(b_loaded, 16)
            sp.dma_start(o1_bias, dram["L2_o1bcol"]).then_inc(b_loaded, 16)
            sp.dma_start(o2_bias, dram["L2_o2b"].partition_broadcast(P)).then_inc(b_loaded, 16)

        @block.tensor
        def _(pe):
            degrees.tensor(pe)
            nodes.tensor(pe)
            nodes.ready(pe)
            pe.wait_ge(degrees.kept, 2)

            def passes(sem, value):
                pe.wait_ge(sem, value)
                pe.sem_inc(steps_pe)

            def sums_of(j, tiles):
                neighbour_sums(nc, c, pe, sp_, [a_cols, a_rows], range(CB), j, tiles, summed)

            def gates(s, j, after=None):
                passes(x_low, CB * (NC * s + j + 1))
                passes(x_high, CB * (NC * s + j + 1))

                def factor(g, kinds, first, last):
                    bank, n = c.psum[:, GB + g % 3, :], 0
                    total = 3 * len(kinds) + (1 if 0 in kinds else 0)
                    if 0 in kinds:
                        nc.tensor.matmul(bank, uv[0:34, g * P:(g + 1) * P], deg_rows[0:34, j * CH:(j + 1) * CH],
                                         start=first, stop=False)
                        n = 1
                    for k in kinds:
                        for a, b in PARTS3:
                            if k < 2 * FT:
                                mov = X[:, j % 2, k // FT, k % FT, a, :]
                            elif g < 4:
                                mov = st[:, 2 * a + k % FT, j * CH:(j + 1) * CH]
                            else:
                                mov = rs[:, k % FT, a, :]
                            n += 1
                            mm = nc.tensor.matmul(bank, mp[b][:, k, g * P:(g + 1) * P], mov, start=False,
                                                  stop=(last and n == total))
                    return mm

                for g in range(GT):
                    passes(gate_read, GT * (NC * s + j) + g + 1)
                    if g < 4:
                        factor(g, list(range(KT)), True, True).then_inc(gate_done, 1)
                    else:
                        factor(g, list(range(2 * FT)), True, False)
                    if after and g in after:
                        after[g]()
                passes(rs_low, FT * (NC * s + j + 1))
                passes(rs_high, FT * (NC * s + j + 1))
                for g in range(4, GT):
                    factor(g, [2 * FT, 2 * FT + 1], False, True).then_inc(gate_done, 1)

            def turn(s, j, half):
                passes(st_low, FT * (NC * s + j + 1) + 1)
                passes(st_high, FT * (NC * s + j + 1))
                passes(sp_kept, 2 * (NC * s + j) + half + 1)
                for q in range(2):
                    t = j * (CH // P) + 2 * half + q
                    for k in range(4):
                        mm = nc.tensor.transpose(c.bank16(TB)[:, (4 * q + k) * P:(4 * q + k + 1) * P],
                                                 st[:, k, t * P:(t + 1) * P], c.ident[:, :])
                mm.then_inc(turned, 1)

            def next_sums(s, j):
                passes(x_low, CB * (NC * s + j))
                sums_of(j, list(range(NT)))

            def step(s, more):
                for j in range(NC):
                    if j + 1 < NC:
                        next_sums(s, j + 1)
                    if more or j < NC - 1:
                        gates(s, j, {g: (lambda h=h: turn(s, *h)) for g, h in TURNS[j].items()} if more else None)
                    else:
                        gates(s, j, {0: lambda: hidden(0, 0), 1: lambda: hidden(0, 1),
                                     2: lambda: hidden(1, 0), 3: lambda: hidden(1, 1)})
                if more:
                    passes(x_low, CB * NC * (s + 1))
                    passes(sp_kept, 2 * (NC * s + 3) + 1)
                    sums_of(0, list(range(0, 10)))
                    turn(s, 3, 0)
                    sums_of(0, [10, 11])
                    turn(s, 3, 1)
                    sums_of(0, [12, 13])
                    passes(sp_kept, 2 * NC * (s + 1) + 1)
                    sums_of(0, [14, 15])

            def hidden(j, g):
                pe.wait_ge(st_low, FT * (NC * (STEPS - 1) + j + 1) + 1)
                pe.wait_ge(st_high, FT * (NC * (STEPS - 1) + j + 1))
                if j:
                    pe.wait_ge(t_made, FT * (j - 1) + g + 1)
                n = 0
                for k in range(FT):
                    for a, b in PARTS3:
                        mm = nc.tensor.matmul(c.psum[:, HB[g], :], op[b][:, k, g * P:(g + 1) * P],
                                              st[:, 2 * a + k, j * CH:(j + 1) * CH], start=(n == 0), stop=(n == 5))
                        n += 1
                mm.then_inc(o_made, 1)

            def output(j):
                pe.wait_ge(t_low, FT * (j + 1))
                pe.wait_ge(t_high, FT * (j + 1))
                for q in range(CH // P):
                    t = j * (CH // P) + q
                    if t >= 2:
                        pe.wait_ge(y_made, t - 1)
                    n = 0
                    for k in range(FT):
                        for a, b in PARTS3:
                            mm = nc.tensor.matmul(c.psum[:, 2 + t % 2, 0:D], tp[j % 2][:, k, a, q * P:(q + 1) * P],
                                                  op[b][:, FT + k, :], start=(n == 0), stop=(n == 5))
                            n += 1
                    mm.then_inc(y_summed, 1)

            sums_of(0, list(range(NT)))
            with pe.Fori(0, STEPS - 1) as s:
                step(s, True)
            step(STEPS - 1, False)
            hidden(2, 0)
            hidden(2, 1)
            output(0)
            output(1)
            output(2)
            hidden(3, 0)
            hidden(3, 1)
            output(3)

        @block.vector
        def _(dve):
            nodes.vector(dve)
            dve.wait_ge(b_loaded, 48)
            nc.vector.tensor_scalar(h_bias, g_bias, 0.5, None, ALU.mult).then_inc(biases, 1)

            def low_parts(s, j):
                for b in range(CB):
                    dve.wait_ge(x_high, CB * (NC * s + j) + b + 1)
                    nc.vector.scalar_tensor_tensor(X[:, j % 2, b // FT, b % FT, 1, :], c.psum[:, b, :], 1.0 / STATE_SCALE,
                                                   X[:, j % 2, b // FT, b % FT, 0, :], ALU.mult, ALU.subtract
                                                   ).then_inc(x_low, 1)

            def update(s, j, between=None):
                at = FT * (NC * s + j)
                dve.wait_ge(st_low, at + 1)
                for k in range(FT):
                    nc.vector.tensor_tensor(s32[:, k, :], st[:, k, j * CH:(j + 1) * CH],
                                            st[:, FT + k, j * CH:(j + 1) * CH], ALU.add).then_inc(s_made, 1)
                for k in range(FT):
                    dve.wait_ge(gate_read, GT * (NC * s + j) + k + 4)
                    dve.wait_ge(s_made, at + k + 1)
                    nc.vector.scalar_tensor_tensor(p32[:, k, :], tr[:, k, :], 1.0, s32[:, k, :], ALU.add, ALU.mult
                                                   ).then_inc(p_made, 1)
                for k in range(FT):
                    dve.wait_ge(rs_high, at + k + 1)
                    nc.vector.scalar_tensor_tensor(rs[:, k, 1, :], p32[:, k, :], 0.5, rs[:, k, 0, :], ALU.mult,
                                                   ALU.subtract).then_inc(rs_low, 1)
                if between:
                    between()
                for k in range(FT):
                    dve.wait_ge(gate_read, GT * (NC * s + j) + k + 8)
                    nc.vector.scalar_tensor_tensor(th[:, k, :], th[:, k, :], STATE_SCALE, s32[:, k, :], ALU.mult,
                                                   ALU.subtract).then_inc(d_made, 1)
                    dve.wait_ge(d_made, at + k + 1)
                    nc.vector.scalar_tensor_tensor(tz[:, k, :], tz[:, k, :], 1.0, th[:, k, :], ALU.add, ALU.mult
                                                   ).then_inc(e_made, 1)
                    dve.wait_ge(e_made, at + k + 1)
                    nc.vector.scalar_tensor_tensor(s32[:, k, :], tz[:, k, :], 0.5, s32[:, k, :], ALU.mult, ALU.add
                                                   ).then_inc(new_made, 1)
                for k in range(FT):
                    dve.wait_ge(st_high, at + k + 1)
                    nc.vector.tensor_tensor(st[:, FT + k, j * CH:(j + 1) * CH], s32[:, k, :],
                                            st[:, k, j * CH:(j + 1) * CH], ALU.subtract).then_inc(st_low, 1)

            def step(s, more):
                for j in range(NC):
                    if j + 1 < NC:
                        low_parts(s, j + 1)
                    update(s, j, hidden_early if not more and j == NC - 1 else None)
                if more:
                    low_parts(s + 1, 0)

            def hidden_low(j):
                for g in range(FT):
                    dve.wait_ge(t_high, FT * j + g + 1)
                    nc.vector.scalar_tensor_tensor(tp[j % 2][:, g, 1, :], t32[j % 2][:, g, :], STATE_SCALE,
                                                   tp[j % 2][:, g, 0, :], ALU.mult, ALU.subtract).then_inc(t_low, 1)

            def hidden_early():
                hidden_low(0)
                hidden_low(1)

            def output(j):
                for q in range(CH // P):
                    t = j * (CH // P) + q
                    dve.wait_ge(y_summed, t + 1)
                    if t >= 2:
                        dve.wait_ge(x_made, t - 1)
                    nc.vector.scalar_tensor_tensor(y[:, t % 2, :], c.psum[:, 2 + t % 2, 0:D], osplit.unscale, o2_bias,
                                                   ALU.mult, ALU.add).then_inc(y_made, 1)
                    dve.wait_ge(y_made, t + 1)
                    nc.vector.tensor_tensor(x[:, t, :], y[:, t % 2, :], x[:, t, :], ALU.add).then_inc(x_made, 1)

            dve.sem_inc(st_low, 1)
            low_parts(0, 0)
            with dve.Fori(0, STEPS - 1) as s:
                step(s, True)
            step(STEPS - 1, False)
            output(0)
            hidden_low(2)
            output(1)
            output(2)
            hidden_low(3)
            output(3)

        @block.scalar
        def _(act):
            nodes.scalar(act)
            degrees.scalar(act)
            act.wait_ge(biases, 1)
            act.sem_inc(gate_read, 3)
            act.sem_inc(sp_kept, 1)

            def high_parts(s, j):
                for b in range(CB):
                    act.wait_ge(summed, CB * (NC * s + j) + b + 1)
                    nc.scalar.activation(X[:, j % 2, b // FT, b % FT, 0, :], c.psum[:, b, :], ACT.Copy,
                                         scale=1.0 / STATE_SCALE).then_inc(x_high, 1)

            def update(s, j, between=None, after=None, before_state=None):
                at = FT * (NC * s + j)

                def gate(g, out, bias, scale):
                    act.wait_ge(gate_done, GT * (NC * s + j) + g + 1)
                    nc.scalar.activation(out[:, g % FT, :], c.psum[:, GB + g % 3, :], ACT.Tanh, bias=bias[:, g:g + 1],
                                         scale=scale).then_inc(gate_read, 1)
                    if after and g in after:
                        after[g]()

                for g in range(FT):
                    gate(g, tr, h_bias, split.half)
                for k in range(FT):
                    act.wait_ge(p_made, at + k + 1)
                    nc.scalar.activation(rs[:, k, 0, :], p32[:, k, :], ACT.Copy, scale=0.5).then_inc(rs_high, 1)
                for g in range(FT, 2 * FT):
                    gate(g, tz, h_bias, split.half)
                if between:
                    between()
                for g in range(2 * FT, 3 * FT):
                    gate(g, th, g_bias, split.plain)
                if before_state:
                    before_state()
                for k in range(FT):
                    act.wait_ge(new_made, at + k + 1)
                    nc.scalar.activation(st[:, k, j * CH:(j + 1) * CH], s32[:, k, :], ACT.Copy).then_inc(st_high, 1)

            def keep(s, j, half):
                act.wait_ge(turned, 2 * (NC * s + j) + half + 1)
                t = j * (CH // P) + 2 * half
                nc.scalar.activation(sp_[:, t:t + 2, :].rearrange("p t n -> p (t n)"), c.bank16(TB),
                                     ACT.Copy).then_inc(sp_kept, 1)

            def step(s, more):
                for j in range(NC):
                    if j + 1 < NC:
                        high_parts(s, j + 1)
                    if more or j < NC - 1:
                        update(s, j, after={g: (lambda h=h: keep(s, *h)) for g, h in TURNS[j].items()} if more else None)
                    else:
                        update(s, j, hidden_early, {0: lambda: hidden(0, 0), 1: lambda: hidden(0, 1),
                                                    2: lambda: hidden(1, 0), 3: lambda: hidden(1, 1)},
                               lambda: (hidden(2, 0), hidden(2, 1)))
                if more:
                    keep(s, 3, 0)
                    keep(s, 3, 1)
                    high_parts(s + 1, 0)

            def hidden(j, g):
                act.wait_ge(o_made, FT * j + g + 1)
                if j >= 2:
                    act.wait_ge(t_low, FT * (j - 2) + g + 1)
                nc.scalar.activation(t32[j % 2][:, g, :], c.psum[:, HB[g], :], ACT.Tanh, bias=o1_bias[:, g:g + 1],
                                     scale=osplit.unscale).then_inc(t_made, 1)

            def hidden_high(j):
                if j >= 2:
                    act.wait_ge(y_summed, (CH // P) * (j - 1))
                for g in range(FT):
                    act.wait_ge(t_made, FT * j + g + 1)
                    nc.scalar.activation(tp[j % 2][:, g, 0, :], t32[j % 2][:, g, :], ACT.Copy, scale=STATE_SCALE
                                         ).then_inc(t_high, 1)

            def hidden_early():
                hidden_high(0)
                hidden_high(1)

            high_parts(0, 0)
            with act.Fori(0, STEPS - 1) as s:
                step(s, True)
            step(STEPS - 1, False)
            hidden_high(2)
            hidden(3, 0)
            hidden(3, 1)
            hidden_high(3)


def hard_attention_layer(c, S):
    nc, dram = c.nc, c.dram
    SCALING = HD ** -0.5
    DOWN = 2.0 ** -17
    x = c.view(AT_X, [NT, D], F32)
    a_rows = c.view(AT_A, [NT, N], F8)
    F, W = AT_FREE, AT_W
    ks = c.view(AT_AT, [H, N], F16)
    qs = c.view(F, [H, N], F16)
    values = c.view(AT_SP, [NT, H, 2, HD], F16)
    w32 = c.view(W, [3 * FT * D + 1], F32)
    w_hi, w_lo = c.view(W + 7 * KB, [3 * FT * D + 1], F16), c.view(W + 11 * KB, [3 * FT * D + 1], F16)
    wp = [v[:, 0:3 * FT * D].rearrange("p (m k n) -> p m k n", m=3, k=FT) for v in (w_hi, w_lo)]
    temp = c.view(W + 15 * KB, [2, CH], F32)
    scal = c.view(W + 27 * KB, [16], F32)
    k_bias, back, bias, be, sq = (scal[:, k:k + 1] for k in range(5))
    best = c.view(W + 27 * KB + 64, [4, 2], F32)
    hard = c.view(AT_ST, [4, N], F16)
    hard_t = c.view(W, [2, NT, P], F16)
    scores = c.view(F + 32 * KB, [4, N], F32)
    mask = c.view(W + 8 * KB, [2, N], F32)
    y = c.view(W + 24 * KB, [2, D], F32)
    flat = c.view(F + 32 * KB, [2, 2, 2, N], F16)
    ON_ACT, ON_POOL = (1, 3, 5), (0, 4, 6)

    nodes = NodeValues(c, "n3", F + 32 * KB)
    split = Split(c, "w4", w32, w_hi, w_lo)
    sem = lambda n: c.sem("h_" + n)
    w_loaded, proj, stacked = sem("w_loaded"), sem("proj"), sem("stacked")
    q_high, q_low, k_full, k_high, k_low = sem("q_high"), sem("q_low"), sem("k_full"), sem("k_high"), sem("k_low")
    v_sum, v_high, v_low = sem("v_sum"), sem("v_high"), sem("v_low")
    consts, masked, mask_ready = sem("consts"), sem("masked"), sem("mask_ready")
    scored, maxed, turned, turned_kept, taken = (
        sem(n) for n in ("scored", "maxed", "turned", "turned_kept", "taken"))
    marked_dve, marked_act, marked_pool = sem("marked_dve"), sem("marked_act"), sem("marked_pool")
    y_half, y_made, stored = sem("y_half"), sem("y_made"), [sem("stored0"), sem("stored1")]
    chain, waited = sem("chain"), sem("waited")
    HALF = N // 2
    STACK = (0, 0, 1, 1), (0, 1, 0, 1)
    copied = sem("copied")

    def marks_until(i, k):
        by_engine = ((marked_act, ON_ACT), (marked_pool, ON_POOL),
                     (marked_dve, [h for h in range(H) if h not in ON_ACT + ON_POOL]))
        for sem, heads in by_engine:
            if k % H in heads:
                return sem, len(heads) * (2 * i + k // H) + list(heads).index(k % H) + 1

    with nc.Block() as block:
        @block.sync
        def _(sp):
            for m, name in enumerate(("L3_WQT", "L3_WKT", "L3_WVT")):
                sp.dma_start(w32[:, m * FT * D:(m + 1) * FT * D].rearrange("p (t f) -> p t f", f=D),
                             dram[name].rearrange("(t p) f -> p t f", p=P)).then_inc(w_loaded, 16)
            for g in range(4):
                sp.dma_start(w32[HD * g:HD * (g + 1), 3 * FT * D:3 * FT * D + 1], dram["L3_we"]).then_inc(w_loaded, 16)
            sp.dma_start(be, dram["L3_be"].partition_broadcast(P)).then_inc(w_loaded, 16)
            for half in range(2):
                for m, (dst, parts) in enumerate(zip((qs, ks), STACK)):
                    sp.wait_ge(k_low if m else q_low, NC * (half + 1))
                    sp.wait_ge(k_high if m else q_high, NC * (half + 1))
                    for h in range(4):
                        for g in (g for g in range(4) if g != h):
                            sp.dma_start(dst[HD * g:HD * (g + 1), 4 * half + h, :],
                                         flat[HD * h:HD * (h + 1), m, half, parts[g], :]).then_inc(stacked, 16)
            sp.sem_inc(stored[1], 16)
            with sp.Fori(0, NT // 2) as i:
                for u in range(2):
                    sp.wait_ge(y_made, 2 * i + u + 1)
                    sp.dma_start(c.out.rearrange("(t p) f -> t p f", p=P)[bass.ds(2 * i + u, 1), :, :]
                                 .rearrange("a p f -> (a p) f"), y[:, u, :]).then_inc(stored[u], 16)
            for u in range(2):
                sp.wait_ge(stored[u], 16 * (NT // 2 + u))

        @block.tensor
        def _(pe):
            nodes.tensor(pe)
            split.ready(pe)
            nodes.ready(pe)
            for n in range(4 * NC):
                half, m, j = n // (2 * NC), n // NC % 2, n % NC
                if m:
                    pe.wait_ge(q_low, n - NC * half - 3)
                elif half:
                    pe.wait_ge(k_full, j + 1)
                f = 0
                for k in range(FT):
                    for a, b in PARTS3:
                        mm = nc.tensor.matmul(c.psum[:, n % 4, :], wp[b][:, m, k, half * P:(half + 1) * P],
                                              nodes.st[:, 2 * a + k, j * CH:(j + 1) * CH], start=(f == 0), stop=(f == 5))
                        f += 1
                mm.then_inc(proj, 1)
            for t in range(NT):
                if t >= 2:
                    pe.wait_ge(v_low, t - 1)
                n = 0
                for k in range(FT):
                    for a, b in PARTS3:
                        mm = nc.tensor.matmul(c.psum[:, 4 + t % 2, 0:D], nodes.st[:, 2 * a + k, t * P:(t + 1) * P],
                                              wp[b][:, 2, k, :], start=(n == 0), stop=(n == 5))
                        n += 1
                mm.then_inc(v_sum, 1)
            pe.wait_ge(k_full, 2 * NC)
            pe.wait_ge(stacked, 16 * 48)
            pe.wait_ge(copied, 16)
            pe.wait_ge(v_low, NT)
            pe.wait_ge(v_high, NT)

            def score(i, k, half):
                n = 16 * i + k
                if not (isinstance(i, int) and n == 0):
                    pe.wait_ge(maxed, 2 * (n - 1) + half + 1)
                for q in range(2):
                    col = HALF * half + CH * q
                    mm = nc.tensor.matmul(c.psum[:, 2 * half + q, :],
                                          qs[:, k % H, bass.ds((2 * i + k // H) * P, P)],
                                          ks[:, k % H, col:col + CH], start=True, stop=True)
                mm.then_inc(scored, 1)

            def take(i, k):
                n = 16 * i + k
                h, u = k % H, (k // H) % 2
                pe.wait_ge(turned_kept, 2 * n + 2)
                if h == 0 and not (isinstance(i, int) and n < 16):
                    pe.wait_ge(y_made, 2 * i + k // H - 1)
                for t in range(NT):
                    mm = nc.tensor.matmul(c.psum[:, 6 + u, 2 * HD * h:2 * HD * (h + 1)], hard_t[:, k % 2, t, :],
                                          values[:, t, h, :, :].rearrange("p a d -> p (a d)"),
                                          start=(t == 0), stop=(t == NT - 1))
                mm.then_inc(taken, 1)

            def turn(i, k, half):
                n = 16 * i + k
                pe.wait_ge(*marks_until(i, k))
                if not (isinstance(i, int) and n == 0):
                    pe.wait_ge(turned_kept, 2 * (n - 1) + half + 1)
                for t in range(8):
                    mm = nc.tensor.transpose(c.bank16(4 + half)[:, t * P:(t + 1) * P],
                                             hard[:, k % 4, (8 * half + t) * P:(8 * half + t + 1) * P], c.ident[:, :])
                mm.then_inc(turned, 1)

            def units(i):
                first = isinstance(i, int)
                for k in range(16):
                    score(i, k, 0)
                    score(i, k, 1)
                    if not (first and k < 3):
                        turn(i, k - 3, 0)
                    if not (first and k < 3):
                        turn(i, k - 3, 1)
                    if not (first and k < 4):
                        take(i, k - 4)

            units(0)
            with pe.Fori(1, NT // 2) as i:
                units(i)
            last = NT // 2 - 1
            for k in range(13, 16):
                take(last, k - 1)
                turn(last, k, 0)
                turn(last, k, 1)
            take(last, 15)

        @block.vector
        def _(dve):
            link = Chain(dve, chain)

            def prepare():
                dve.wait_ge(w_loaded, 16 * 8)
                yield from split.vector_steps(dve)

            nodes.vector(dve, prepare())
            link(nc.vector.tensor_scalar(k_bias, w32[:, 3 * FT * D:3 * FT * D + 1], split.scale, STATE_SCALE * DOWN,
                                         ALU.mult, ALU.mult))
            link(nc.vector.tensor_scalar(back, split.plain, 1.0 / (H * STATE_SCALE * DOWN), None, ALU.mult))
            link(nc.vector.tensor_scalar(sq, split.scale, STATE_SCALE * DOWN, None, ALU.mult))
            link(nc.vector.tensor_scalar(bias, be, sq, sq, ALU.mult, ALU.mult))
            dve.sem_inc(consts, 1)
            dve.wait_ge(split.low, 1)

            for n in range(4 * NC):
                half, m, j = n // (2 * NC), n // NC % 2, n % NC
                hi, lo = (flat[:, m, half, part, j * CH:(j + 1) * CH] for part in range(2))
                if m == 0:
                    dve.wait_ge(q_high, NC * half + j + 1)
                    nc.vector.scalar_tensor_tensor(lo, c.psum[:, n % 4, :], DOWN, hi, ALU.mult, ALU.subtract
                                                   ).then_inc(q_low, 1)
                else:
                    dve.wait_ge(k_high, NC * half + j + 1)
                    nc.vector.tensor_tensor(lo, temp[:, n % 2, :], hi, ALU.subtract).then_inc(k_low, 1)
            for t in range(NT):
                dve.wait_ge(v_high, t + 1)
                nc.vector.scalar_tensor_tensor(values[:, t, :, 1, :], c.psum[:, 4 + t % 2, 0:D].rearrange("p (h d) -> p h d", d=HD),
                                               DOWN, values[:, t, :, 0, :], ALU.mult, ALU.subtract).then_inc(v_low, 1)
                half, m, h = t // 8, t // 4 % 2, t % 4
                if t == 0:
                    dve.wait_ge(q_low, 2 * NC)
                    dve.wait_ge(k_low, 2 * NC)
                nc.vector.tensor_copy((ks if m else qs)[HD * h:HD * (h + 1), 4 * half + h, :],
                                      flat[HD * h:HD * (h + 1), m, half, STACK[m][h], :]).then_inc(copied, 1)
            for t in range(2):
                dve.wait_ge(masked, t + 1)
                nc.vector.tensor_scalar(mask[:, t, :], mask[:, t, :], bias, None, ALU.min).then_inc(mask_ready, 1)
            dve.wait_ge(copied, 16)
            dve.wait_ge(stacked, 16 * 48)

            def unit(i, k):
                n = 16 * i + k
                first = isinstance(i, int) and i == 0
                if k % H == 0:
                    dve.wait_ge(mask_ready, 2 * i + k // H + 1)
                if not (first and k < 4):
                    dve.wait_ge(*marks_until(i, k - 4))
                for half in range(2):
                    dve.wait_ge(scored, 2 * n + half + 1)
                    if half:
                        dve.wait_ge(maxed, 2 * n + 1)
                    dve.sem_inc(waited)
                    at = slice(HALF * half, HALF * (half + 1))
                    nc.vector.tensor_tensor_reduce(scores[:, k % 4, at],
                                                   c.psum[:, 2 * half:2 * half + 2, :].rearrange("p b n -> p (b n)"),
                                                   mask[:, (k // H) % 2, at], 1.0,
                                                   best[:, k % 4, 0:1] if half else -BIG / 4, ALU.add, ALU.max,
                                                   best[:, k % 4, half:half + 1]).then_inc(maxed, 1)
                if k % H not in ON_ACT + ON_POOL:
                    dve.wait_ge(maxed, 2 * n + 2)
                    if not (first and k < 4):
                        dve.wait_ge(turned, 2 * (n - 3))
                    nc.vector.tensor_scalar(hard[:, k % 4, :], scores[:, k % 4, :], best[:, k % 4, 1:2], None,
                                            ALU.is_equal).then_inc(marked_dve, 1)

            def finish(i, u, stores=None):
                qt = 2 * i + u
                dve.wait_ge(taken, H * (qt + 1))
                if stores is not None:
                    dve.wait_ge(stored[u], stores)
                o = c.psum[:, 6 + u, :].rearrange("p (h a d) -> p h a d", a=2, d=HD)
                yv = y[:, u, :].rearrange("p (h d) -> p h d", d=HD)
                xv = x[:, bass.ds(qt, 1), :].rearrange("p a (h d) -> p (a h) d", d=HD)
                nc.vector.scalar_tensor_tensor(yv, o[:, :, 0, :], back, xv, ALU.mult, ALU.add).then_inc(y_half, 1)
                dve.wait_ge(y_half, qt + 1)
                nc.vector.scalar_tensor_tensor(yv, o[:, :, 1, :], back, yv, ALU.mult, ALU.add).then_inc(y_made, 1)

            for k in range(16):
                unit(0, k)
                if k == 13:
                    finish(0, 0)
            with dve.Fori(1, NT // 2) as i:
                for k in range(16):
                    unit(i, k)
                    if k == 5:
                        finish(i - 1, 1, 16 * i)
                    if k == 13:
                        finish(i, 0, 16 * i)
            finish(NT // 2 - 1, 1, 16 * (NT // 2))

        @block.gpsimd
        def _(pool):
            split.gpsimd(pool)
            pool.wait_ge(consts, 1)

            def bias_mask(t):
                pool.wait_ge(masked, t + 1)
                nc.gpsimd.tensor_scalar(mask[:, t % 2, :], mask[:, t % 2, :], bias, None, ALU.min).then_inc(mask_ready, 1)

            for n in range(NT * H):
                if n % H in ON_POOL:
                    pool.wait_ge(maxed, 2 * n + 2)
                    if n >= 4:
                        pool.wait_ge(turned, 2 * (n - 3))
                    nc.gpsimd.tensor_scalar(hard[:, n % 4, :], scores[:, n % 4, :], best[:, n % 4, 1:2], None,
                                            ALU.is_equal).then_inc(marked_pool, 1)
                if n % H == 0 and 0 < n // H < NT - 1:
                    bias_mask(n // H + 1)

        @block.scalar
        def _(act):
            nodes.scalar(act, split.scalar)
            act.wait_ge(nodes.low, NT)
            act.wait_ge(consts, 1)
            for n in range(4 * NC):
                half, m, j = n // (2 * NC), n // NC % 2, n % NC
                kept = NC * half + j
                hi = flat[:, m, half, 0, j * CH:(j + 1) * CH]
                act.wait_ge(proj, n + 1)
                if m == 0:
                    nc.scalar.activation(hi, c.psum[:, n % 4, :], ACT.Copy, scale=DOWN).then_inc(q_high, 1)
                else:
                    if kept >= 2:
                        act.wait_ge(k_low, kept - 1)
                    nc.scalar.activation(temp[:, n % 2, :], c.psum[:, n % 4, :], ACT.Identity, bias=k_bias,
                                         scale=SCALING * DOWN).then_inc(k_full, 1)
                    act.wait_ge(k_full, kept + 1)
                    nc.scalar.activation(hi, temp[:, n % 2, :], ACT.Copy).then_inc(k_high, 1)
            for t in range(NT):
                act.wait_ge(v_sum, t + 1)
                nc.scalar.activation(values[:, t, :, 0, :], c.psum[:, 4 + t % 2, 0:D].rearrange("p (h d) -> p h d", d=HD),
                                     ACT.Copy, scale=DOWN).then_inc(v_high, 1)
            act.wait_ge(v_sum, NT)
            act.wait_ge(k_low, 2 * NC)

            def mask_rows(t, half):
                if t >= 2:
                    act.wait_ge(maxed, 2 * H * (t - 1))
                    act.wait_ge(mask_ready, t - 1)
                at = slice(HALF * half, HALF * (half + 1))
                made = nc.scalar.activation(mask[:, t % 2, at], a_rows[:, t, at], ACT.Copy, scale=BIG, bias=-BIG / 2)
                if half:
                    made.then_inc(masked, 1)

            def keep(n, half):
                act.wait_ge(turned, 2 * n + half + 1)
                if n >= 2:
                    act.wait_ge(taken, n - 1)
                own = n % H in ON_ACT
                nc.scalar.activation(hard_t[:, n % 2, 8 * half:8 * half + 8, :].rearrange("p t q -> p (t q)"),
                                     c.bank16(4 + half), ACT.Copy, scale=-1.0 if own else 1.0,
                                     bias=1.0 if own else 0.0).then_inc(turned_kept, 1)

            for t in range(2):
                mask_rows(t, 0)
                mask_rows(t, 1)
            for n in range(NT * H):
                for half in range(2):
                    if n >= 3:
                        keep(n - 3, half)
                    m = n - 1
                    if m >= 0 and m % H in ON_ACT:
                        act.wait_ge(maxed, 2 * m + 2)
                        if m >= 4:
                            act.wait_ge(turned, 2 * (m - 3))
                        at = slice(HALF * half, HALF * (half + 1))
                        made = nc.scalar.activation(hard[:, m % 4, at], scores[:, m % 4, at], ACT.Sign,
                                                    bias=best[:, m % 4, 1:2], scale=-1.0)
                        if half:
                            made.then_inc(marked_act, 1)
                    if n % H == 0 and 0 < n // H < NT - 1:
                        mask_rows(n // H + 1, half)
            for n in range(NT * H - 3, NT * H):
                keep(n, 0)
                keep(n, 1)


class Shared:
    pass

''

def graph_layers(nc, dram, out):
    with ExitStack() as ctx:
        c = Chip(nc, ctx, dram, out)
        S = Shared()
        S.degree = ctx.enter_context(nc.sbuf_tensor("degree", [P, NT], F32))
        layers = [load_phase, attention_layer, mean_layer, gated_layer, hard_attention_layer]
        for layer in layers:
            with ExitStack() as own:
                c.ctx, c.owned = own, []
                layer(c, S)
                if layer is not layers[-1]:
                    c.clear_semaphores()


def kernel(**inputs):
    import numpy as _np
    import concourse.bacc as _bacc
    from concourse import mybir as _mybir
    from concourse.bass_utils import run_bass_kernel_spmd as _run

    nc = _bacc.Bacc("TRN2", target_bir_lowering=False, num_devices=1)
    arrays, dram = {}, {}

    def give(name, a):
        a = _np.ascontiguousarray(a)
        arrays[f"in_{name}_dram"] = a
        dram[name] = nc.dram_tensor(f"in_{name}_dram", a.shape, _mybir.dt.from_np(a.dtype),
                                    kind="ExternalInput").ap()

    give("x", inputs["x"])
    give("adj", inputs["adj"])
    give("L0_W", inputs["L0_gnn_W_w"])
    give("L0_WT", _np.asarray(inputs["L0_gnn_W_w"]).T)
    give("L0_b", inputs["L0_gnn_W_b"])
    give("L0_bcol", _np.asarray(inputs["L0_gnn_W_b"]).reshape(FT, P).T)
    give("L0_a", inputs["L0_gnn_a"])
    I = {k: _np.asarray(v) for k, v in inputs.items()}
    cols = lambda a: a.reshape(-1, P).T
    give("L1_WsT", I["L1_gnn_W_self"].T)
    give("L1_WnT", I["L1_gnn_W_nb"].T)
    give("L1_Wc", I["L1_gnn_W_comb"])
    give("L1_bs", cols(I["L1_gnn_b_self"]))
    give("L1_bn", cols(I["L1_gnn_b_nb"]))
    give("L1_bc", I["L1_gnn_b_comb"])
    give("L2_in_W", I["L2_gnn_in_W"])
    give("L2_out_W", I["L2_gnn_out_W"])
    give("L2_WgT", _np.concatenate([I[f"L2_gnn_{g}_W"].T for g in "rzh"], axis=1))
    give("L2_o1T", I["L2_gnn_o1_W"].T)
    give("L2_o2T", I["L2_gnn_o2_W"].T)
    give("L2_gbcol", _np.concatenate([cols(I[f"L2_gnn_{g}_b"]) for g in "rzh"], axis=1))
    give("L2_o1bcol", cols(I["L2_gnn_o1_b"]))
    give("L2_iobcol", _np.concatenate([cols(I["L2_gnn_in_b"]), cols(I["L2_gnn_out_b"])], axis=1))
    give("L3_WQT", I["L3_gnn_WQ"].T)
    give("L3_WKT", I["L3_gnn_WK"].T)
    give("L3_WVT", I["L3_gnn_WV"].T)
    give("L3_we", I["L3_gnn_we"].reshape(HD, 1))
    give("L3_be", I["L3_gnn_be"])
    give("L2_o2b", I["L2_gnn_o2_b"])
    out = nc.dram_tensor("out_0_dram", (2048, 256), _mybir.dt.float32, kind="ExternalOutput").ap()
    graph_layers(nc, dram, out)
    r = _run(nc, [arrays], core_ids=[0])
    return r.results[0]["out_0_dram"]
```
